# Optimizing a Trainium2 kernel written in Bass

```python
import numpy as np
import jax
import jax.numpy as jnp

def _softmax(x, axis=-1):
    return jax.nn.softmax(x, axis=axis)

def _gelu(x):
    return jax.nn.gelu(x, approximate=True)

def _silu(x):
    return jax.nn.silu(x)

def _sigmoid(x):
    return jax.nn.sigmoid(x)

def _layernorm(x, axis=-1, eps=1e-05):
    m = jnp.mean(x, axis=axis, keepdims=True)
    v = jnp.var(x, axis=axis, keepdims=True)
    return (x - m) / jnp.sqrt(v + eps)

def _scatter_add(tgt, idx, src, axis=0):
    return tgt.at[idx].add(src)

def _segment_sum(src, seg, n):
    return jax.ops.segment_sum(src, seg, n)
kernel_name = 'mk_xattn_ffn_d2_seqx_r4_c004b9'

def setup_inputs(seed: int=0):
    np.random.seed(seed)
    _w = jnp.asarray

    def _rec_inputs():
        import jax
        import jax.numpy as jnp
        _rk = jax.random.key(seed)
        x = -0.0005146 + 1 * jax.random.normal(jax.random.fold_in(_rk, 1), (16, 256, 256), jnp.float32)
        _lenS = 256 - jax.random.randint(jax.random.fold_in(_rk, 7), (16,), 0, max(1, 256 // 4) + 1, jnp.int32)
        _lenS2 = 77 - jax.random.randint(jax.random.fold_in(_rk, 8), (16,), 0, max(1, 77 // 4) + 1, jnp.int32)
        _ctx_1024P = jax.random.normal(jax.random.fold_in(_rk, 11), (16, 16, 256), jnp.float32)
        _ctx_1024c = jax.random.dirichlet(jax.random.fold_in(_rk, 511), 0.3 * jnp.ones((16,), jnp.float32), (16, 77))
        _ctx_1024t = jnp.einsum('bsk,bkd->bsd', _ctx_1024c, _ctx_1024P)
        _ctx_1024t = _ctx_1024t * jax.lax.rsqrt(jnp.mean(jnp.square(_ctx_1024t)) + 1e-12) * 0.953939
        ctx_1024 = -0.000392918 + 0.999932 * (_ctx_1024t + 0.3 * jax.random.normal(jax.random.fold_in(_rk, 611), (16, 77, 256), jnp.float32))
        return (x, ctx_1024)
    x, ctx_1024 = _rec_inputs()

    def _L0_xattn_setup():
        import jax, jax.numpy as jnp
        import numpy as np
        DIM = 256
        DIM_HEAD = 64
        HEADS = 16
        INNER = DIM_HEAD * HEADS
        EPS = 1e-05

        def layer_norm(x, g, b):
            m = jnp.mean(x, axis=-1, keepdims=True)
            v = jnp.mean(jnp.square(x - m), axis=-1, keepdims=True)
            return (x - m) * jax.lax.rsqrt(v + EPS) * g + b
        key = jax.random.key(seed)
        ks = jax.random.split(key, 8)
        B, N_IMG, N_LAT = (4, 1024, 128)
        std = 1.0 / np.sqrt(DIM)
        return {'image_embeds': jax.random.normal(ks[0], (B, N_IMG, DIM), dtype=jnp.float32), 'latents': jax.random.normal(ks[1], (B, N_LAT, DIM), dtype=jnp.float32), 'ln1_g': jnp.ones((DIM,), jnp.float32), 'ln1_b': jnp.zeros((DIM,), jnp.float32), 'ln2_g': jnp.ones((DIM,), jnp.float32), 'ln2_b': jnp.zeros((DIM,), jnp.float32), 'Wq': jax.random.normal(ks[2], (DIM, INNER), dtype=jnp.float32) * std, 'Wkv': jax.random.normal(ks[3], (DIM, 2 * INNER), dtype=jnp.float32) * std, 'Wo': jax.random.normal(ks[4], (INNER, DIM), dtype=jnp.float32) * std}
    _L0_xattn_all = _L0_xattn_setup()
    _L0_xattn_in = {k: v for k, v in _L0_xattn_all.items() if k in ('ln1_g', 'ln1_b', 'ln2_g', 'ln2_b', 'Wq', 'Wkv', 'Wo')}
    del _L0_xattn_all

    def _L0_ffn_setup():
        import jax, jax.numpy as jnp
        import numpy as np
        B, S, D, F, E, TOP_K = (4, 512, 256, 1024, 8, 2)
        LN_EPS = 1e-05
        key = jax.random.key(seed)
        ks = jax.random.split(key, 4)
        sc = lambda fan_in: 1.0 / np.sqrt(fan_in)
        return {'x': jax.random.normal(ks[0], (B, S, D), jnp.float32), 'W1': jax.random.normal(ks[1], (E, D, F), jnp.float32) * sc(D), 'b1': jnp.zeros((E, F), jnp.float32), 'W2': jax.random.normal(ks[2], (E, F, D), jnp.float32) * sc(F), 'b2': jnp.zeros((E, D), jnp.float32), 'Wr': jax.random.normal(ks[3], (D, E), jnp.float32) * sc(D), 'br': jnp.zeros((E,), jnp.float32), 'gamma': jnp.ones((D,), jnp.float32), 'beta': jnp.zeros((D,), jnp.float32)}
    _L0_ffn_all = _L0_ffn_setup()
    _L0_ffn_in = {k: v for k, v in _L0_ffn_all.items() if k in ('W1', 'b1', 'W2', 'b2', 'Wr', 'br', 'gamma', 'beta')}
    del _L0_ffn_all

    def _L1_xattn_setup():
        import jax, jax.numpy as jnp
        import numpy as np
        D_MODEL = 256
        NUM_HEADS = 16
        D_K = D_MODEL // NUM_HEADS

        def _split_heads(x):
            B, S, _ = x.shape
            return x.reshape(B, S, NUM_HEADS, D_K).transpose(0, 2, 1, 3)
        key = jax.random.key(seed)
        ks = jax.random.split(key, 11)
        B, S, D = (2, 512, D_MODEL)
        scale = 1.0 / np.sqrt(D)
        inp = {'q': jax.random.normal(ks[0], (B, S, D), jnp.float32), 'k': jax.random.normal(ks[1], (B, S, D), jnp.float32), 'v': jax.random.normal(ks[2], (B, S, D), jnp.float32), 'wq': jax.random.normal(ks[3], (D, D), jnp.float32) * scale, 'bq': jnp.zeros((D,), jnp.float32), 'wk': jax.random.normal(ks[4], (D, D), jnp.float32) * scale, 'bk': jnp.zeros((D,), jnp.float32), 'wv': jax.random.normal(ks[5], (D, D), jnp.float32) * scale, 'bv': jnp.zeros((D,), jnp.float32), 'wo': jax.random.normal(ks[6], (D, D), jnp.float32) * scale, 'bo': jnp.zeros((D,), jnp.float32)}
        return inp
    _L1_xattn_all = _L1_xattn_setup()
    _L1_xattn_in = {k: v for k, v in _L1_xattn_all.items() if k in ('wq', 'bq', 'wk', 'bk', 'wv', 'bv', 'wo', 'bo')}
    del _L1_xattn_all

    def _L1_ffn_setup():
        import jax, jax.numpy as jnp
        import numpy as np
        B, S, D_MODEL, D_HIDDEN = (4, 512, 256, 1024)

        def act_quant(x):
            scale = 127.0 / jnp.clip(jnp.max(jnp.abs(x), axis=-1, keepdims=True), 1e-05)
            return jnp.clip(jnp.round(x * scale), -128, 127) / scale

        def weight_quant(w):
            scale = 1.0 / jnp.clip(jnp.mean(jnp.abs(w)), 1e-05)
            return jnp.clip(jnp.round(w * scale), -1, 1) / scale

        def bit_linear(x, w):
            xq = x + jax.lax.stop_gradient(act_quant(x) - x)
            wq = w + jax.lax.stop_gradient(weight_quant(w) - w)
            return jnp.einsum('bsd,hd->bsh', xq, wq)

        def depthwise_conv1d(x_bcl, w, b):
            y = jax.lax.conv_general_dilated(x_bcl, w, window_strides=(1,), padding=[(1, 1)], dimension_numbers=('NCH', 'OIH', 'NCH'), feature_group_count=x_bcl.shape[1])
            return y + b[None, :, None]
        key = jax.random.key(seed)
        ks = jax.random.split(key, 5)
        lim1 = 1.0 / np.sqrt(D_MODEL)
        lim2 = 1.0 / np.sqrt(D_HIDDEN)
        limc = 1.0 / np.sqrt(3.0)
        return {'x': jax.random.normal(ks[0], (B, S, D_MODEL), dtype=jnp.float32), 'w1': jax.random.uniform(ks[1], (D_HIDDEN, D_MODEL), jnp.float32, -lim1, lim1), 'conv_w': jax.random.uniform(ks[2], (D_HIDDEN, 1, 3), jnp.float32, -limc, limc), 'conv_b': jax.random.uniform(ks[3], (D_HIDDEN,), jnp.float32, -limc, limc), 'w2': jax.random.uniform(ks[4], (D_MODEL, D_HIDDEN), jnp.float32, -lim2, lim2)}
    _L1_ffn_all = _L1_ffn_setup()
    _L1_ffn_in = {k: v for k, v in _L1_ffn_all.items() if k in ('w1', 'conv_w', 'conv_b', 'w2')}
    del _L1_ffn_all
    return {'x': x, 'ctx_1024': ctx_1024, 'L0_xattn_ln1_g': _L0_xattn_in['ln1_g'], 'L0_xattn_ln1_b': _L0_xattn_in['ln1_b'], 'L0_xattn_ln2_g': _L0_xattn_in['ln2_g'], 'L0_xattn_ln2_b': _L0_xattn_in['ln2_b'], 'L0_xattn_Wq': _L0_xattn_in['Wq'], 'L0_xattn_Wkv': _L0_xattn_in['Wkv'], 'L0_xattn_Wo': _L0_xattn_in['Wo'], 'L0_ffn_W1': _L0_ffn_in['W1'], 'L0_ffn_b1': _L0_ffn_in['b1'], 'L0_ffn_W2': _L0_ffn_in['W2'], 'L0_ffn_b2': _L0_ffn_in['b2'], 'L0_ffn_Wr': _L0_ffn_in['Wr'], 'L0_ffn_br': _L0_ffn_in['br'], 'L0_ffn_gamma': _L0_ffn_in['gamma'], 'L0_ffn_beta': _L0_ffn_in['beta'], 'L1_xattn_wq': _L1_xattn_in['wq'], 'L1_xattn_bq': _L1_xattn_in['bq'], 'L1_xattn_wk': _L1_xattn_in['wk'], 'L1_xattn_bk': _L1_xattn_in['bk'], 'L1_xattn_wv': _L1_xattn_in['wv'], 'L1_xattn_bv': _L1_xattn_in['bv'], 'L1_xattn_wo': _L1_xattn_in['wo'], 'L1_xattn_bo': _L1_xattn_in['bo'], 'L1_ffn_w1': _L1_ffn_in['w1'], 'L1_ffn_conv_w': _L1_ffn_in['conv_w'], 'L1_ffn_conv_b': _L1_ffn_in['conv_b'], 'L1_ffn_w2': _L1_ffn_in['w2']}

def reference(x, ctx_1024, L0_xattn_ln1_g, L0_xattn_ln1_b, L0_xattn_ln2_g, L0_xattn_ln2_b, L0_xattn_Wq, L0_xattn_Wkv, L0_xattn_Wo, L0_ffn_W1, L0_ffn_b1, L0_ffn_W2, L0_ffn_b2, L0_ffn_Wr, L0_ffn_br, L0_ffn_gamma, L0_ffn_beta, L1_xattn_wq, L1_xattn_bq, L1_xattn_wk, L1_xattn_bk, L1_xattn_wv, L1_xattn_bv, L1_xattn_wo, L1_xattn_bo, L1_ffn_w1, L1_ffn_conv_w, L1_ffn_conv_b, L1_ffn_w2):
    import jax
    import jax.numpy as jnp

    def _L0_xattn_ref(image_embeds, latents, ln1_g, ln1_b, ln2_g, ln2_b, Wq, Wkv, Wo):
        import jax, jax.numpy as jnp
        import numpy as np
        DIM = 256
        DIM_HEAD = 64
        HEADS = 16
        INNER = DIM_HEAD * HEADS
        EPS = 1e-05

        def layer_norm(x, g, b):
            m = jnp.mean(x, axis=-1, keepdims=True)
            v = jnp.mean(jnp.square(x - m), axis=-1, keepdims=True)
            return (x - m) * jax.lax.rsqrt(v + EPS) * g + b
        B, S_lat, _ = latents.shape
        x = layer_norm(image_embeds, ln1_g, ln1_b)
        l = layer_norm(latents, ln2_g, ln2_b)
        q = l @ Wq
        kv_in = jnp.concatenate([x, l], axis=1)
        kv = kv_in @ Wkv
        k, v = jnp.split(kv, 2, axis=-1)

        def to_heads(t):
            return t.reshape(t.shape[0], t.shape[1], HEADS, DIM_HEAD).transpose(0, 2, 1, 3)
        q, k, v = (to_heads(q), to_heads(k), to_heads(v))
        scale = 1.0 / np.sqrt(np.sqrt(DIM_HEAD))
        w = jnp.einsum('bhqd,bhkd->bhqk', q * scale, k * scale)
        w = jax.nn.softmax(w.astype(jnp.float32), axis=-1).astype(q.dtype)
        out = jnp.einsum('bhqk,bhkd->bhqd', w, v)
        out = out.transpose(0, 2, 1, 3).reshape(B, S_lat, INNER)
        return out @ Wo

    def _L0_ffn_ref(x, W1, b1, W2, b2, Wr, br, gamma, beta):
        import jax, jax.numpy as jnp
        import numpy as np
        B, S, D, F, E, TOP_K = (4, 512, 256, 1024, 8, 2)
        LN_EPS = 1e-05
        b, s, d = x.shape
        e = Wr.shape[1]
        rw = jax.nn.softmax(x.mean(axis=1) @ Wr + br, axis=-1)
        x_flat = x.reshape(-1, d)
        rw_tok = jnp.repeat(rw, s, axis=0)
        tk_w, tk_i = jax.lax.top_k(rw_tok, TOP_K)
        tk_w = jax.nn.softmax(tk_w, axis=-1)
        h = jax.nn.gelu(jnp.einsum('nd,edf->enf', x_flat, W1) + b1[:, None, :], approximate=False)
        expert_out = jnp.einsum('enf,efd->end', h, W2) + b2[:, None, :]
        onehot = jax.nn.one_hot(tk_i, e, dtype=x.dtype)
        cw = jnp.einsum('nk,nke->ne', tk_w, onehot)
        out = jnp.einsum('ne,end->nd', cw, expert_out).reshape(b, s, d)
        y = out + x
        mu = y.mean(axis=-1, keepdims=True)
        var = y.var(axis=-1, keepdims=True)
        return (y - mu) / jnp.sqrt(var + LN_EPS) * gamma + beta

    def _L1_xattn_ref(q, k, v, wq, bq, wk, bk, wv, bv, wo, bo):
        import jax, jax.numpy as jnp
        import numpy as np
        D_MODEL = 256
        NUM_HEADS = 16
        D_K = D_MODEL // NUM_HEADS

        def _split_heads(x):
            B, S, _ = x.shape
            return x.reshape(B, S, NUM_HEADS, D_K).transpose(0, 2, 1, 3)
        qh = _split_heads(q @ wq.T + bq)
        kh = _split_heads(k @ wk.T + bk)
        vh = _split_heads(v @ wv.T + bv)
        scores = jnp.einsum('bhqd,bhkd->bhqk', qh, kh) / np.sqrt(D_K)
        attn = jax.nn.softmax(scores, axis=-1)
        ctx = jnp.einsum('bhqk,bhkd->bhqd', attn, vh)
        B, H, S, dk = ctx.shape
        ctx = ctx.transpose(0, 2, 1, 3).reshape(B, S, H * dk)
        return ctx @ wo.T + bo

    def _L1_ffn_ref(x, w1, conv_w, conv_b, w2):
        import jax, jax.numpy as jnp
        import numpy as np
        B, S, D_MODEL, D_HIDDEN = (4, 512, 256, 1024)

        def act_quant(x):
            scale = 127.0 / jnp.clip(jnp.max(jnp.abs(x), axis=-1, keepdims=True), 1e-05)
            return jnp.clip(jnp.round(x * scale), -128, 127) / scale

        def weight_quant(w):
            scale = 1.0 / jnp.clip(jnp.mean(jnp.abs(w)), 1e-05)
            return jnp.clip(jnp.round(w * scale), -1, 1) / scale

        def bit_linear(x, w):
            xq = x + jax.lax.stop_gradient(act_quant(x) - x)
            wq = w + jax.lax.stop_gradient(weight_quant(w) - w)
            return jnp.einsum('bsd,hd->bsh', xq, wq)

        def depthwise_conv1d(x_bcl, w, b):
            y = jax.lax.conv_general_dilated(x_bcl, w, window_strides=(1,), padding=[(1, 1)], dimension_numbers=('NCH', 'OIH', 'NCH'), feature_group_count=x_bcl.shape[1])
            return y + b[None, :, None]
        h = bit_linear(x, w1)
        h = depthwise_conv1d(h.transpose(0, 2, 1), conv_w, conv_b)
        h = h.transpose(0, 2, 1)
        h = jax.nn.silu(h)
        return bit_linear(h, w2)
    x = x + _L0_xattn_ref(ctx_1024, _layernorm(x, axis=-1), L0_xattn_ln1_g, L0_xattn_ln1_b, L0_xattn_ln2_g, L0_xattn_ln2_b, L0_xattn_Wq, L0_xattn_Wkv, L0_xattn_Wo)
    x = x + _L0_ffn_ref(_layernorm(x, axis=-1), L0_ffn_W1, L0_ffn_b1, L0_ffn_W2, L0_ffn_b2, L0_ffn_Wr, L0_ffn_br, L0_ffn_gamma, L0_ffn_beta)
    x = x + _L1_xattn_ref(_layernorm(x, axis=-1), ctx_1024, ctx_1024, L1_xattn_wq, L1_xattn_bq, L1_xattn_wk, L1_xattn_bk, L1_xattn_wv, L1_xattn_bv, L1_xattn_wo, L1_xattn_bo)
    x = x + _L1_ffn_ref(_layernorm(x, axis=-1), L1_ffn_w1, L1_ffn_conv_w, L1_ffn_conv_b, L1_ffn_w2)
    return x

_drawn_inputs = setup_inputs


def setup_inputs(seed=0):
    import zlib

    import numpy as np

    out = dict(_drawn_inputs(seed))
    spreads = {'L0_xattn_ln1_g': (1.0, 0.2),
     'L0_xattn_ln1_b': (0.0, 0.1),
     'L0_xattn_ln2_g': (1.0, 0.2),
     'L0_xattn_ln2_b': (0.0, 0.1),
     'L0_ffn_b1': (0.0, 0.377),
     'L0_ffn_b2': (0.0, 0.267),
     'L0_ffn_br': (0.0, 0.1),
     'L0_ffn_gamma': (1.0, 0.2),
     'L0_ffn_beta': (0.0, 0.1),
     'L1_xattn_bq': (0.0, 0.724),
     'L1_xattn_bk': (0.0, 2.0),
     'L1_xattn_bv': (0.0, 0.1),
     'L1_xattn_bo': (0.0, 0.1)}
    factors = {}
    for name, (base, spread) in spreads.items():
        noise = np.random.default_rng([zlib.crc32(name.encode()), seed]).standard_normal(out[name].shape)
        drawn = base * np.exp(spread * noise) if base else spread * noise
        out[name] = jnp.asarray(drawn.astype(out[name].dtype))
    for name, factor in factors.items():
        out[name] = (out[name] * factor).astype(out[name].dtype)
    return out
```

```python
from contextlib import ExitStack

import concourse.bass as bass
from concourse import mybir

F32 = mybir.dt.float32
BF16 = mybir.dt.bfloat16
U32 = mybir.dt.uint32
ALU = mybir.AluOpType
ACT = mybir.ActivationFunctionType
AX = mybir.AxisListType

P = 128
B, S, D = 16, 256, 256
C = 77
DC = D // P
TT = S // P
H0, DH0 = 16, 64
INNER = H0 * DH0
PAIRS = H0 // 2
STEPS = PAIRS * TT
KEYS = S + C
KT = 3
KP = KEYS // KT
E, F, TOPK = 8, 1024, 2
FT = F // P
H1, DH1 = 16, 16
HG, HI = 4, 4
EPS = 1e-5
MAGIC = 1.5 * 2.0 ** 23

VEC_LINKS = 59


class Signal:

    def __init__(self, sem, per):
        self.sem, self.per = sem, per

    def at(self, b, n):
        return b * self.per + n


def build(nc, x, ctx_in, ln1_g, ln1_b, ln2_g, ln2_b, Wq, Wkv, Wo, W1, b1, W2, b2, Wr, br, gamma, beta,
          wq, bq, wk, bk, wv, bv, wo, bo, fw1, conv_w, conv_b, fw2, out):
    assert KT * KP == KEYS and KP <= P
    with ExitStack() as stack:
        def sb(name, shape, dt=F32):
            return stack.enter_context(nc.sbuf_tensor(name, shape, dt))

        def sem(name):
            return stack.enter_context(nc.semaphore(name))

        def signal(name, per):
            return Signal(sem(name), per)

        wq0 = sb("wq0", [P, DC, INNER])
        wkv0 = sb("wkv0", [P, DC, 2 * INNER])
        wo0 = sb("wo0", [P, PAIRS, D])
        wr = sb("wr", [P, DC, E])
        brow = sb("brow", [1, E])
        g1 = sb("g1", [P, DC]); bb1 = sb("bb1", [P, DC])
        g2 = sb("g2", [P, DC]); bb2 = sb("bb2", [P, DC])
        gammaB = sb("gammaB", [P, D]); betaB = sb("betaB", [P, D])
        boB = sb("boB", [P, D]); bvB = sb("bvB", [P, D])
        bqp = sb("bqp", [P, HG]); bkp = sb("bkp", [P, HG])
        wqT = sb("wqT", [P, DC, HG, HI, 32])
        wkT = sb("wkT", [P, DC, HG, HI, 32])
        wvT = sb("wvT", [P, DC, D])
        woT = sb("woT", [P, DC, D])
        f1T = sb("f1T", [P, DC, F], BF16)
        f2T = sb("f2T", [P, FT, D], BF16)
        cw = sb("cw", [P, FT, 3]); cb = sb("cb", [P, FT])
        mw = sb("mw", [P, 2]); ws = sb("ws", [P, 2]); absum = sb("absum", [P, 2])
        ident = sb("ident", [P, P]); identb = sb("identb", [P, P], BF16)
        ones = sb("ones", [P, P])
        mhalf = sb("mhalf", [P, 3])
        xin = sb("xin", [P, TT, D]); cin = sb("cin", [C, D])
        xn = sb("xn", [P, TT, D]); cn = sb("cn", [C, D])
        st = sb("st", [P, 3, 6]); mv = sb("mv", [P, 3, 2]); var = sb("var", [P, 3]); rstd = sb("rstd", [P, 3])
        kvT = sb("kvT", [P, DC, KEYS]); cT = sb("cT", [P, DC, C])
        qT = sb("qT", [P, 2, S]); kT = sb("kT", [P, 2, KEYS])
        V = sb("V", [KP, KT, H0, DH0 + 1])
        nmax = sb("nmax", [P, 2, 2])
        Pr = sb("Pr", [P, 2, 2, KEYS])
        PT = sb("PT", [KP, 2, 2, KT, P])
        rinv = sb("rinv", [P, 2])
        aT_aN = sb("aT_aN", [P, 2 * TT * INNER])
        aN = aT_aN[:, 0:TT * INNER].rearrange("p (t n) -> p t n", t=TT)
        aT = aT_aN[:, TT * INNER:].rearrange("p (a q) -> p a q", a=PAIRS)
        x1 = sb("x1", [P, TT, D]); x1b = sb("x1b", [P, TT, D])
        yT = sb("yT", [P, DC, S]); ysum = sb("ysum", [P, DC])
        lg = sb("lg", [1, E]); nlg = sb("nlg", [1, 1]); ex = sb("ex", [1, E]); exs = sb("exs", [1, 1])
        rex = sb("rex", [1, 1]); rw = sb("rw", [1, E]); top = sb("top", [1, 8]); idx = sb("idx", [1, 8], U32)
        gap = sb("gap", [1, 1]); egap = sb("egap", [1, 1]); wden = sb("wden", [1, 1]); wtop = sb("wtop", [1, 2])
        wrow = sb("wrow", [1, 2, P]); wB = sb("wB", [P, 2])
        W1s = sb("W1s", [P, TOPK, DC, F]); W2s = sb("W2s", [P, TOPK, FT, D])
        b1r = sb("b1r", [FT, TOPK, P]); b2r = sb("b2r", [1, TOPK, D]); b1T = sb("b1T", [P, TOPK, FT])
        hT = sb("hT", [P, TOPK, FT, S])
        y2 = sb("y2", [P, TT, D])
        x2 = sb("x2", [P, TT, D]); x2b = sb("x2b", [P, TT, D])
        q1T = sb("q1T", [P, HG, S]); k1T = sb("k1T", [P, HG, C]); v1 = sb("v1", [C, H1, DH1 + 1])
        nmax1 = sb("nmax1", [P, TT, HI, HG]); P1 = aT_aN[:, 0:TT * H1 * C].rearrange("p (t i g c) -> p t i g c", t=TT, i=HI, g=HG); 
        PT1 = hT[0:C, 1, :, :].rearrange("p a q -> p (a q)").rearrange("p (i g q) -> p i g q", i=HI, g=HG)
        rinv1 = sb("rinv1", [P, H1]); a1 = sb("a1", [P, TT, D]); a1T = sb("a1T", [P, DC, S])
        x3 = sb("x3", [P, TT, D])
        am = sb("am", [P, TT]); sc = sb("sc", [P, TT]); inv = sb("inv", [P, TT])
        qf = y2; qx = sb("qx", [P, TT, D], BF16); qxT = sb("qxT", [P, DC, S], BF16)
        dg = sb("dg", [P, TT, P]); sB = sb("sB", [P, S])
        hb = sb("hb", [P, FT, S + 2])
        cv = hT[:, 0, :, :]; mj = sb("mj", [P, S])
        q2 = sb("q2", [P, FT, S], BF16)
        dg2, sB2 = dg, sB; am2 = sb("am2", [P, TT]); inv2 = sb("inv2", [P, TT])
        sc2 = sb("sc2", [P, TT])
        x4 = sb("x4", [P, TT, D])
        st1 = W1s[:, 0, :, :].rearrange("p a n -> p (a n)")
        st2 = W1s[:, 1, :, :].rearrange("p a n -> p (a n)")
        stq = hT[:, 0, :, :].rearrange("p a n -> p (a n)")
        stb1 = q2[:, :, :].rearrange("p a n -> p (a n)")
        stb2 = aN[:, :, :].rearrange("p a n -> p (a n)").bitcast(BF16)[:, 0:2048]

        ps = stack.enter_context(nc.psum_tensor("ps", [P, 8, 512], F32))
        psb = ps[:, :, :].rearrange("p a n -> p (a n)").bitcast(BF16).rearrange("p (a n) -> p a n", a=8)

        ld = {n: sem(f"ld_{n}") for n in ("vec", "w0", "l1", "ffn", "bias")}
        ident_made = sem("ident_made"); consts_made = sem("consts_made")
        setup_pe = sem("setup_pe"); setup_dve = sem("setup_dve")
        x_in = signal("x_in", 16); c_in = signal("c_in", 16); out_done = signal("out_done", 16)
        var_ready = signal("var_ready", 5); rstd_ready = signal("rstd_ready", 5); xn_ready = signal("xn_ready", 4)
        xT_done = signal("xT_done", 4); cT_done = signal("cT_done", 1)
        xT_ready = signal("xT_ready", 4); cT_ready = signal("cT_ready", 1)
        v_done = signal("v_done", 2 * KT); v_act = signal("v_act", KT); v_dve = signal("v_dve", KT)
        q_done = signal("q_done", PAIRS); q_ready = signal("q_ready", PAIRS)
        k_done = signal("k_done", PAIRS); k_ready = signal("k_ready", PAIRS)
        score_done = signal("score_done", STEPS); max_ready = signal("max_ready", STEPS)
        exp_ready = signal("exp_ready", STEPS); pt_done = signal("pt_done", STEPS)
        pt_act = signal("pt_act", STEPS); pt_dve = signal("pt_dve", STEPS)
        pv_done = signal("pv_done", STEPS); norm_ready = signal("norm_ready", STEPS)
        aT_done = signal("aT_done", 4); aT_act = signal("aT_act", 2); aT_dve = signal("aT_dve", 2)
        wo_done = signal("wo_done", TT); x1_ready = signal("x1_ready", 1); x1b_ready = signal("x1b_ready", 1)
        logit_done = signal("logit_done", 1); logit_ready = signal("logit_ready", 1)
        rexp_ready = signal("rexp_ready", 1); idx_ready = signal("idx_ready", 1)
        gap_ready = signal("gap_ready", 1); egap_ready = signal("egap_ready", 1)
        wtop_ready = signal("wtop_ready", 1); wrow_ready = signal("wrow_ready", 1)
        wB_done = signal("wB_done", 1); b2_done = signal("b2_done", 1)
        w1_in = [signal(f"w1_in{e}", 16) for e in range(TOPK)]
        w2_in = [signal(f"w2_in{e}", 16) for e in range(TOPK)]
        b_in = signal("b_in", 16 * 2 * TOPK)
        b1T_done = signal("b1T_done", 1); b1T_ready = signal("b1T_ready", 1)
        h_done = signal("h_done", TOPK * FT); gelu_ready = signal("gelu_ready", TOPK * FT)
        moe_done = signal("moe_done", TT)
        x2_ready = signal("x2_ready", 1); x2b_ready = signal("x2b_ready", 1)
        q1_done = signal("q1_done", 2); q1_ready = signal("q1_ready", 4)
        k1_done = signal("k1_done", 1); k1_ready = signal("k1_ready", 1)
        v1_done = signal("v1_done", 1); v1_ready = signal("v1_ready", 1)
        s1_done = signal("s1_done", TT); s1_shift = signal("s1_shift", TT); e1_ready = signal("e1_ready", TT)
        t1_done = signal("t1_done", TT * HI); t1_act = signal("t1_act", TT * 2); t1_dve = signal("t1_dve", TT * 2)
        pv1_done = signal("pv1_done", TT); a1_ready = signal("a1_ready", TT)
        a1T_done = signal("a1T_done", 1); a1T_ready = signal("a1T_ready", 1); wo1_done = signal("wo1_done", 1)
        dg_ready = signal("dg_ready", 1); sB_done = signal("sB_done", 1); sB_ready = signal("sB_ready", 1)
        f1_done = signal("f1_done", 4); hb_ready = signal("hb_ready", 4); tap_ready = signal("tap_ready", 4)
        conv_ready = signal("conv_ready", 4); silu_ready = signal("silu_ready", 4)
        mj_ready = signal("mj_ready", 1); mjT_done = signal("mjT_done", 1)
        dg2_ready = signal("dg2_ready", 1); sB2_done = signal("sB2_done", 1); sB2_ready = signal("sB2_ready", 1)
        q2_ready = signal("q2_ready", 4); f2_done = signal("f2_done", TT); x4_ready = signal("x4_ready", 1)
        vec_link = signal("vec_link", VEC_LINKS)

        block = stack.enter_context(nc.Block())

        def row(v):
            return v.rearrange("(a n) -> a n", a=1)

        @block.sync
        def _(sp):
            def load_x(b):
                sp.dma_start(xin[:, :, :], x[b].rearrange("(t p) d -> p t d", p=P)).then_inc(x_in.sem, 16)
                sp.dma_start(cin[:, :], ctx_in[b]).then_inc(c_in.sem, 16)

            load_x(0)
            with nc.allow_non_contiguous_dma(reason="small vectors laid out one feature per partition"):
                for dst, src in ((g1, ln1_g), (bb1, ln1_b), (g2, ln2_g), (bb2, ln2_b)):
                    sp.dma_start(dst[:, :], src.rearrange("(c p) -> p c", p=P)).then_inc(ld["vec"], 16)
                sp.dma_start(wq0[:, :, :], Wq.rearrange("(c p) n -> p c n", p=P)).then_inc(ld["w0"], 16)
                sp.dma_start(wkv0[:, :, :], Wkv.rearrange("(c p) n -> p c n", p=P)).then_inc(ld["w0"], 16)
                sp.dma_start(wo0[:, :, :], Wo.rearrange("(j p) n -> p j n", p=P)).then_inc(ld["w0"], 16)
                sp.dma_start(wr[:, :, :], Wr.rearrange("(c p) n -> p c n", p=P)).then_inc(ld["w0"], 16)
                sp.dma_start(st1, fw1.rearrange("(a p) n -> p a n", p=P)).then_inc(ld["ffn"], 16)
                sp.dma_start(st2, fw2.rearrange("(a p) n -> p a n", p=P)).then_inc(ld["ffn"], 16)
                for k, w in enumerate((wq, wk, wv, wo)):
                    sp.dma_start(stq[:, k * 512:(k + 1) * 512], w.rearrange("(a p) n -> p a n", p=P))\
                      .then_inc(ld["l1"], 16)
                sp.dma_start(brow[:, :], row(br)).then_inc(ld["bias"], 16)
                sp.dma_start(cw[:, :, :], conv_w.rearrange("(j p) a k -> p j (a k)", p=P)).then_inc(ld["bias"], 16)
                sp.dma_start(cb[:, :], conv_b.rearrange("(j p) -> p j", p=P)).then_inc(ld["bias"], 16)
                for dst, src in ((gammaB, gamma), (betaB, beta), (boB, bo), (bvB, bv)):
                    sp.dma_start(dst[:, :], row(src).to_broadcast([P, D])).then_inc(ld["bias"], 16)
                sp.wait_ge(consts_made, 4)
                for dst, src in ((bqp, bq), (bkp, bk)):
                    v = src.rearrange("(g i c) -> i c g", g=HG, i=HI)
                    for i in range(HI):
                        sp.dma_start(dst[32 * i:32 * i + DH1, :], v[i]).then_inc(ld["bias"], 16)
            sp.wait_ge(setup_dve, SETUP_DVE_END)
            with sp.Fori(0, B) as b:
                sp.wait_ge(x1_ready.sem, x1_ready.at(b, 1))
                sp.wait_ge(cT_done.sem, cT_done.at(b, 1))
                nxt = (b + 1) % B
                load_x(nxt)
                sp.wait_ge(idx_ready.sem, idx_ready.at(b, 1))
                sp.nop(nofuse=True)
                for k in range(TOPK):
                    e = sp.value_load(idx[0:1, k:k + 1], min_val=0, max_val=E - 1)
                    sp.dma_start(W1s[:, k, :, :], W1[e].rearrange("(c p) n -> p c n", p=P)).then_inc(w1_in[k].sem, 16)
                    sp.dma_start(b1r[:, k, :], b1[e].rearrange("(j p) -> j p", p=P)).then_inc(b_in.sem, 16)
                    sp.dma_start(b2r[:, k, :], row(b2[e])).then_inc(b_in.sem, 16)
                    sp.dma_start(W2s[:, k, :, :], W2[e].rearrange("(j p) n -> p j n", p=P)).then_inc(w2_in[k].sem, 16)
                sp.wait_ge(x4_ready.sem, x4_ready.at(b, 1))
                sp.dma_start(out[b].rearrange("(t p) d -> p t d", p=P), x4[:, :, :]).then_inc(out_done.sem, 16)
                sp.wait_ge(out_done.sem, out_done.at(b, 16))
                sp.nop(nofuse=True)
            sp.wait_ge(out_done.sem, 16 * B)
            sp.wait_ge(x_in.sem, 16 * (B + 1))
            sp.wait_ge(c_in.sem, 16 * (B + 1))

        @block.gpsimd
        def _(pool):
            pool.memset(ident[:, :], 0.0).then_inc(ident_made, 1)
            pool.memset(identb[:, :], 0.0).then_inc(ident_made, 1)
            pool.memset(bqp[:, :], 0.0).then_inc(consts_made, 1)
            pool.memset(bkp[:, :], 0.0).then_inc(consts_made, 1)
            pool.memset(ones[:, :], 1.0).then_inc(consts_made, 1)
            pool.memset(mhalf[:, :], -0.5).then_inc(consts_made, 1)
            pool.wait_ge(ident_made, 2)
            for m in (ident, identb):
                pool.affine_select(out=m[:, :], in_=m[:, :], compare_op=ALU.not_equal, fill=1.0,
                                   base=0, pattern=[[-1, P]], channel_multiplier=1).then_inc(ident_made, 1)
            pool.memset(V[:, :, :, DH0:DH0 + 1], 1.0).then_inc(consts_made, 1)
            pool.memset(v1[:, :, DH1:DH1 + 1], 1.0).then_inc(consts_made, 1)
            pool.memset(hb[:, :, 0:1], 0.0).then_inc(consts_made, 1)
            pool.memset(hb[:, :, S + 1:S + 2], 0.0).then_inc(consts_made, 1)
            pool.memset(mv[:, :, :], 1.0).then_inc(consts_made, 1)
            pool.memset(wqT[:, :, :, :, :], 0.0).then_inc(consts_made, 1)
            pool.memset(wkT[:, :, :, :, :], 0.0).then_inc(consts_made, 1)
            pool.wait_ge(consts_made, 11)
            pool.wait_ge(ld["bias"], 16 * (7 + 2 * HI))

            def rsqrt(b, n):
                pool.wait_ge(var_ready.sem, var_ready.at(b, n))
                pool.tensor_tensor(rstd[:, :], var[:, :], mhalf[:, :], ALU.pow).then_inc(rstd_ready.sem, 1)

            with pool.Fori(0, B) as b:
                rsqrt(b, 1)
                pool.wait_ge(x1_ready.sem, x1_ready.at(b, 1))
                for t in range(TT):
                    ins = pool.tensor_tensor(x1b[:, t, :], x1[:, t, :], betaB[:, :], ALU.add)
                ins.then_inc(x1b_ready.sem, 1)
                rsqrt(b, 2)
                rsqrt(b, 3)
                pool.wait_ge(x2_ready.sem, x2_ready.at(b, 1))
                for t in range(TT):
                    ins = pool.tensor_tensor(x2b[:, t, :], x2[:, t, :], boB[:, :], ALU.add)
                ins.then_inc(x2b_ready.sem, 1)
                rsqrt(b, 4)
                rsqrt(b, 5)

        @block.tensor
        def _(pe):
            mm, tr = pe.matmul, pe.transpose
            pe.wait_ge(ident_made, 4)
            pe.wait_ge(consts_made, 11)
            pe.wait_ge(ld["l1"], 64)
            for k in range(4):
                for a in range(2):
                    for c in range(DC):
                        ins = tr(ps[:, k, (2 * a + c) * P:(2 * a + c + 1) * P],
                                 stq[:, k * 512 + a * 256 + c * P:k * 512 + a * 256 + (c + 1) * P], ident[:, :])
                ins.then_inc(setup_pe, 1)
            pe.wait_ge(setup_dve, 2)
            mm(ps[:, 7, 0:2], ones[:, :], absum[:, :], start=True, stop=True).then_inc(setup_pe, 1)
            pe.wait_ge(setup_dve, SETUP_DVE_Q)
            for c in range(DC):
                for j in range(FT):
                    ins = tr(psb[:, 4 + c, j * P:(j + 1) * P], stb1[:, j * D + c * P:j * D + (c + 1) * P], identb[:, :])
            for j in range(FT):
                for c in range(DC):
                    ins = tr(psb[:, 6 + j // 4, (j % 4) * 256 + c * P:(j % 4) * 256 + (c + 1) * P],
                             stb2[:, c * F + j * P:c * F + (j + 1) * P], identb[:, :])
            ins.then_inc(setup_pe, 1)
            pe.wait_ge(ld["w0"], 64)
            pe.wait_ge(setup_dve, SETUP_DVE_END)

            def transpose_x(b, n, src, dst, idn):
                pe.wait_ge(xn_ready.sem, xn_ready.at(b, n))
                for c in range(DC):
                    for t in range(TT):
                        ins = tr(dst[:, 6, c * S + t * P:c * S + (t + 1) * P], src[:, t, c * P:(c + 1) * P], idn[:, :])
                ins.then_inc(xT_done.sem, 1)

            def project_q(b, p):
                for c in range(DC):
                    ins = mm(ps[:, 7, 0:S], wq0[:, c, p * P:(p + 1) * P], kvT[:, c, 0:S], start=c == 0, stop=c == DC - 1)
                ins.then_inc(q_done.sem, 1)

            def project_k(b, p):
                pe.wait_ge(q_ready.sem, q_ready.at(b, p + 1))
                for c in range(DC):
                    ins = mm(ps[:, 7, 0:KEYS], wkv0[:, c, p * P:(p + 1) * P], kvT[:, c, :], start=c == 0, stop=c == DC - 1)
                ins.then_inc(k_done.sem, 1)

            def scores(b, s):
                p, t = divmod(s, TT)
                pe.wait_ge(k_ready.sem, k_ready.at(b, p + 1))
                if s >= 2:
                    pe.wait_ge(exp_ready.sem, exp_ready.at(b, s - 1))
                for h in range(2):
                    r = slice(64 * h, 64 * h + 64)
                    ins = mm(ps[:, 2 * (s % 2) + h, 0:KEYS], qT[r, p % 2, t * P:(t + 1) * P], kT[r, p % 2, :],
                             start=True, stop=True)
                ins.then_inc(score_done.sem, 1)

            def transpose_p(b, s):
                pe.wait_ge(exp_ready.sem, exp_ready.at(b, s + 1))
                for h in range(2):
                    for k in range(KT):
                        ins = tr(ps[0:KP, 4 + h, k * P:(k + 1) * P], Pr[:, s % 2, h, k * KP:(k + 1) * KP], ident[:, :])
                ins.then_inc(pt_done.sem, 1)

            def attend(b, s):
                p = s // TT
                pe.wait_ge(pt_act.sem, pt_act.at(b, s + 1))
                pe.wait_ge(pt_dve.sem, pt_dve.at(b, s + 1))
                if s >= 1:
                    pe.wait_ge(norm_ready.sem, norm_ready.at(b, s))
                for h in range(2):
                    for k in range(KT):
                        ins = mm(ps[:, 6, h * (DH0 + 1):(h + 1) * (DH0 + 1)], PT[:, s % 2, h, k, :], V[:, k, 2 * p + h, :],
                                 start=k == 0, stop=k == KT - 1)
                ins.then_inc(pv_done.sem, 1)

            with pe.Fori(0, B) as b:
                transpose_x(b, 1, xn, ps, ident)
                for n, src in enumerate((cn, cin)):
                    for c in range(DC):
                        ins = tr(ps[:, 7, (2 * n + c) * C:(2 * n + c + 1) * C], src[:, c * P:(c + 1) * P], ident[0:C, 0:C])
                ins.then_inc(cT_done.sem, 1)
                pe.wait_ge(xT_ready.sem, xT_ready.at(b, 1))
                pe.wait_ge(cT_ready.sem, cT_ready.at(b, 1))
                project_q(b, 0)
                for k in range(KT):
                    for n in range(2):
                        for c in range(DC):
                            ins = mm(ps[0:KP, 2 * k + n, :], kvT[:, c, k * KP:(k + 1) * KP],
                                     wkv0[:, c, INNER + n * 512:INNER + (n + 1) * 512], start=c == 0, stop=c == DC - 1)
                        ins.then_inc(v_done.sem, 1)
                project_k(b, 0)
                pe.wait_ge(v_act.sem, v_act.at(b, KT))
                pe.wait_ge(v_dve.sem, v_dve.at(b, KT))
                scores(b, 0)
                for s in range(STEPS):
                    ahead = s % TT == 0 and s // TT + 1 < PAIRS
                    if ahead:
                        project_q(b, s // TT + 1)
                    if s + 1 < STEPS:
                        scores(b, s + 1)
                    if s >= 1:
                        attend(b, s - 1)
                    transpose_p(b, s)
                    if ahead:
                        project_k(b, s // TT + 1)
                attend(b, STEPS - 1)
                pe.wait_ge(norm_ready.sem, norm_ready.at(b, STEPS))
                for g in range(4):
                    for p in (2 * g, 2 * g + 1):
                        for t in range(TT):
                            ins = tr(ps[:, g, (p % 2) * S + t * P:(p % 2) * S + (t + 1) * P],
                                     aN[:, t, p * P:(p + 1) * P], ident[:, :])
                    ins.then_inc(aT_done.sem, 1)
                pe.wait_ge(aT_act.sem, aT_act.at(b, 2))
                pe.wait_ge(aT_dve.sem, aT_dve.at(b, 2))
                for t in range(TT):
                    for p in range(PAIRS):
                        ins = mm(ps[:, 4 + t, 0:D], aT[:, p, t * P:(t + 1) * P], wo0[:, p, :], start=p == 0, stop=p == PAIRS - 1)
                    ins.then_inc(wo_done.sem, 1)
                transpose_x(b, 2, xn, ps, ident)
                pe.wait_ge(xT_ready.sem, xT_ready.at(b, 2))
                for c in range(DC):
                    ins = mm(ps[0:1, 7, 0:E], ysum[:, c:c + 1], wr[:, c, :], start=c == 0, stop=c == DC - 1)
                ins.then_inc(logit_done.sem, 1)
                pe.wait_ge(wtop_ready.sem, wtop_ready.at(b, 1))
                pe.nop(nofuse=True)
                mm(ps[:, 7, 0:2], ones[0:1, :], wtop[:, :], start=True, stop=True).then_inc(wB_done.sem, 1)
                pe.wait_ge(b_in.sem, b_in.at(b, 16 * 2 * TOPK))
                pe.nop(nofuse=True)
                for k in range(TOPK):
                    ins = tr(ps[:, 6, k * FT:(k + 1) * FT], b1r[:, k, :], ident[0:FT, 0:FT])
                ins.then_inc(b1T_done.sem, 1)
                for k in range(TOPK):
                    pe.wait_ge(w1_in[k].sem, w1_in[k].at(b, 16))
                    for j in range(FT):
                        if k > 0 and j % 2 == 0:
                            pe.wait_ge(gelu_ready.sem, gelu_ready.at(b, j + 2))
                        for c in range(DC):
                            ins = mm(ps[:, j // 2, (j % 2) * S:(j % 2 + 1) * S], W1s[:, k, c, j * P:(j + 1) * P], yT[:, c, :],
                                     start=c == 0, stop=c == DC - 1)
                        ins.then_inc(h_done.sem, 1)
                pe.wait_ge(wrow_ready.sem, wrow_ready.at(b, 1))
                pe.nop(nofuse=True)
                for k in range(TOPK):
                    ins = mm(ps[:, 6, S:S + D], wrow[:, k, :], b2r[:, k, :], start=k == 0, stop=k == TOPK - 1)
                ins.then_inc(b2_done.sem, 1)
                for k in range(TOPK):
                    pe.wait_ge(w2_in[k].sem, w2_in[k].at(b, 16))
                    pe.wait_ge(gelu_ready.sem, gelu_ready.at(b, (k + 1) * FT))
                    for t in range(TT):
                        for j in range(FT):
                            ins = mm(ps[:, 4 + t, k * D:(k + 1) * D], hT[:, k, j, t * P:(t + 1) * P], W2s[:, k, j, :],
                                     start=j == 0, stop=j == FT - 1)
                        if k == TOPK - 1:
                            ins.then_inc(moe_done.sem, 1)
                for g in range(HG):
                    for c in range(DC):
                        ins = mm(ps[:, 2, g * C:(g + 1) * C], wkT[:, c, g, :, :].rearrange("p i c -> p (i c)"), cT[:, c, :],
                                 start=c == 0, stop=c == DC - 1)
                ins.then_inc(k1_done.sem, 1)
                for c in range(DC):
                    ins = mm(ps[0:C, 3, 0:D], cT[:, c, :], wvT[:, c, :], start=c == 0, stop=c == DC - 1)
                ins.then_inc(v1_done.sem, 1)
                transpose_x(b, 3, xn, ps, ident)
                pe.wait_ge(xT_ready.sem, xT_ready.at(b, 3))
                for g in range(HG):
                    for c in range(DC):
                        ins = mm(ps[:, g // 2, (g % 2) * S:(g % 2 + 1) * S], wqT[:, c, g, :, :].rearrange("p i c -> p (i c)"),
                                 yT[:, c, :], start=c == 0, stop=c == DC - 1)
                    if g % 2:
                        ins.then_inc(q1_done.sem, 1)
                pe.wait_ge(q1_ready.sem, q1_ready.at(b, 4))
                pe.wait_ge(k1_ready.sem, k1_ready.at(b, 1))
                pe.wait_ge(v1_ready.sem, v1_ready.at(b, 1))
                for t in range(TT):
                    for g in range(HG):
                        for i in range(HI):
                            r = slice(32 * i, 32 * i + 32)
                            ins = mm(ps[:, 4 * t + i, g * C:(g + 1) * C], q1T[r, g, t * P:(t + 1) * P], k1T[r, g, :],
                                     start=True, stop=True)
                    ins.then_inc(s1_done.sem, 1)
                for t in range(TT):
                    pe.wait_ge(e1_ready.sem, e1_ready.at(b, t + 1))
                    for i in range(HI):
                        for g in range(HG):
                            ins = tr(ps[0:C, 4 * t + i, g * P:(g + 1) * P], P1[:, t, i, g, :], ident[:, :])
                        ins.then_inc(t1_done.sem, 1)
                    pe.wait_ge(t1_act.sem, t1_act.at(b, 2 * t + 2))
                    pe.wait_ge(t1_dve.sem, t1_dve.at(b, 2 * t + 2))
                    for i in range(HI):
                        for g in range(HG):
                            h = HI * g + i
                            ins = mm(ps[:, 4 * t, h * (DH1 + 1):(h + 1) * (DH1 + 1)], PT1[:, i, g, :], v1[:, h, :],
                                     start=True, stop=True)
                    ins.then_inc(pv1_done.sem, 1)
                pe.wait_ge(a1_ready.sem, a1_ready.at(b, TT))
                for c in range(DC):
                    for t in range(TT):
                        ins = tr(ps[:, 1, c * S + t * P:c * S + (t + 1) * P], a1[:, t, c * P:(c + 1) * P], ident[:, :])
                ins.then_inc(a1T_done.sem, 1)
                pe.wait_ge(a1T_ready.sem, a1T_ready.at(b, 1))
                for t in range(TT):
                    for c in range(DC):
                        ins = mm(ps[:, 2, t * D:(t + 1) * D], a1T[:, c, t * P:(t + 1) * P], woT[:, c, :],
                                 start=c == 0, stop=c == DC - 1)
                ins.then_inc(wo1_done.sem, 1)
                transpose_x(b, 4, qx, psb, identb)
                pe.wait_ge(dg_ready.sem, dg_ready.at(b, 1))
                for t in range(TT):
                    ins = mm(ps[:, 7, t * P:(t + 1) * P], ones[:, :], dg[:, t, :], start=True, stop=True)
                ins.then_inc(sB_done.sem, 1)
                pe.wait_ge(xT_ready.sem, xT_ready.at(b, 4))
                for j in range(FT):
                    for c in range(DC):
                        ins = mm(ps[:, j // 2, (j % 2) * S:(j % 2 + 1) * S], f1T[:, c, j * P:(j + 1) * P], qxT[:, c, :],
                                 start=c == 0, stop=c == DC - 1)
                    if j % 2:
                        ins.then_inc(f1_done.sem, 1)
                pe.wait_ge(mj_ready.sem, mj_ready.at(b, 1))
                for t in range(TT):
                    ins = tr(ps[:, 6, t * P:(t + 1) * P], mj[:, t * P:(t + 1) * P], ident[:, :])
                ins.then_inc(mjT_done.sem, 1)
                pe.wait_ge(dg2_ready.sem, dg2_ready.at(b, 1))
                for t in range(TT):
                    ins = mm(ps[:, 7, t * P:(t + 1) * P], ones[:, :], dg2[:, t, :], start=True, stop=True)
                ins.then_inc(sB2_done.sem, 1)
                pe.wait_ge(q2_ready.sem, q2_ready.at(b, 4))
                for t in range(TT):
                    for j in range(FT):
                        ins = mm(ps[:, 4 + t, 0:D], q2[:, j, t * P:(t + 1) * P], f2T[:, j, :], start=j == 0, stop=j == FT - 1)
                    ins.then_inc(f2_done.sem, 1)

        @block.scalar
        def _(act):
            fn = act.activation
            act.wait_ge(setup_dve, SETUP_DVE_END)
            act.wait_ge(ld["vec"], 64)

            def q_out(b, p):
                act.wait_ge(q_done.sem, q_done.at(b, p + 1))
                fn(qT[:, p % 2, :], ps[:, 7, 0:S], ACT.Copy, scale=DH0 ** -0.5).then_inc(q_ready.sem, 1)

            def exps(b, s):
                act.wait_ge(max_ready.sem, max_ready.at(b, s + 1))
                for h in range(2):
                    ins = fn(Pr[:, s % 2, h, :], ps[:, 2 * (s % 2) + h, 0:KEYS], ACT.Exp, bias=nmax[:, s % 2, h:h + 1])
                ins.then_inc(exp_ready.sem, 1)

            with act.Fori(0, B) as b:
                act.wait_ge(xT_done.sem, xT_done.at(b, 1))
                for c in range(DC):
                    ins = fn(kvT[:, c, 0:S], ps[:, 6, c * S:(c + 1) * S], ACT.Identity, scale=g2[:, c:c + 1], bias=bb2[:, c:c + 1])
                ins.then_inc(xT_ready.sem, 1)
                q_out(b, 0)
                for k in range(KT):
                    act.wait_ge(v_done.sem, v_done.at(b, 2 * k + 1))
                    fn(V[:, k, 0:8, 0:DH0], ps[0:KP, 2 * k, :].rearrange("p (h d) -> p h d", d=DH0), ACT.Copy)\
                        .then_inc(v_act.sem, 1)
                exps(b, 0)
                for s in range(STEPS):
                    if s % TT == 0 and s // TT + 1 < PAIRS:
                        q_out(b, s // TT + 1)
                    if s + 1 < STEPS:
                        exps(b, s + 1)
                    act.wait_ge(pt_done.sem, pt_done.at(b, s + 1))
                    fn(PT[:, s % 2, 0, :, :].rearrange("p k q -> p (k q)"), ps[0:KP, 4, 0:KT * P], ACT.Copy)\
                        .then_inc(pt_act.sem, 1)
                for g in (0, 2):
                    act.wait_ge(aT_done.sem, aT_done.at(b, g + 1))
                    fn(aT[:, 2 * g:2 * g + 2, :].rearrange("p a q -> p (a q)"), ps[:, g, :], ACT.Copy).then_inc(aT_act.sem, 1)
                act.wait_ge(xT_done.sem, xT_done.at(b, 2))
                for c in range(DC):
                    ins = fn(yT[:, c, :], ps[:, 6, c * S:(c + 1) * S], ACT.Copy, accum_out=ysum[:, c:c + 1])
                ins.then_inc(xT_ready.sem, 1)
                act.wait_ge(logit_ready.sem, logit_ready.at(b, 1))
                fn(ex[:, :], lg[:, :], ACT.Exp, bias=nlg[:, :], accum_out=exs[:, :]).then_inc(rexp_ready.sem, 1)
                act.wait_ge(gap_ready.sem, gap_ready.at(b, 1))
                fn(egap[:, :], gap[:, :], ACT.Exp).then_inc(egap_ready.sem, 1)
                act.wait_ge(b1T_done.sem, b1T_done.at(b, 1))
                fn(b1T[:, :, :].rearrange("p k j -> p (k j)"), ps[:, 6, 0:TOPK * FT], ACT.Copy).then_inc(b1T_ready.sem, 1)
                act.wait_ge(b1T_ready.sem, b1T_ready.at(b, 1))
                for k in range(TOPK):
                    for j in range(FT):
                        act.wait_ge(h_done.sem, h_done.at(b, k * FT + (j // 2) * 2 + 2))
                        fn(hT[:, k, j, :], ps[:, j // 2, (j % 2) * S:(j % 2 + 1) * S], ACT.Gelu,
                           bias=b1T[:, k, j:j + 1]).then_inc(gelu_ready.sem, 1)
                act.wait_ge(xT_done.sem, xT_done.at(b, 3))
                fn(yT[:, :, :].rearrange("p c q -> p (c q)"), ps[:, 6, :], ACT.Copy).then_inc(xT_ready.sem, 1)
                for g in range(HG):
                    act.wait_ge(q1_done.sem, q1_done.at(b, g // 2 + 1))
                    fn(q1T[:, g, :], ps[:, g // 2, (g % 2) * S:(g % 2 + 1) * S], ACT.Identity, scale=DH1 ** -0.5,
                       bias=bqp[:, g:g + 1]).then_inc(q1_ready.sem, 1)
                for t in range(TT):
                    act.wait_ge(s1_shift.sem, s1_shift.at(b, t + 1))
                    v = P1[:, t, :, :, :].rearrange("p i g c -> p (i g c)")
                    fn(v, v, ACT.Exp).then_inc(e1_ready.sem, 1)
                for t in range(TT):
                    for i in (0, 2):
                        act.wait_ge(t1_done.sem, t1_done.at(b, 4 * t + i + 1))
                        if t:
                            act.wait_ge(pv1_done.sem, pv1_done.at(b, t))
                        fn(PT1[:, i, :, :].rearrange("p g q -> p (g q)"), ps[0:C, 4 * t + i, :], ACT.Copy).then_inc(t1_act.sem, 1)
                act.wait_ge(a1T_done.sem, a1T_done.at(b, 1))
                fn(a1T[:, :, :].rearrange("p c q -> p (c q)"), ps[:, 1, :], ACT.Copy).then_inc(a1T_ready.sem, 1)
                act.wait_ge(xT_done.sem, xT_done.at(b, 4))
                fn(qxT[:, :, :].rearrange("p c q -> p (c q)"), psb[:, 6, 0:512], ACT.Copy).then_inc(xT_ready.sem, 1)
                act.wait_ge(sB_done.sem, sB_done.at(b, 1))
                fn(sB[:, :], ps[:, 7, 0:S], ACT.Copy).then_inc(sB_ready.sem, 1)
                for g in range(4):
                    act.wait_ge(hb_ready.sem, hb_ready.at(b, g + 1))
                    for j in (2 * g, 2 * g + 1):
                        ins = fn(cv[:, j, :], hb[:, j, 1:S + 1], ACT.Identity, scale=cw[:, j, 1:2], bias=cb[:, j:j + 1])
                    ins.then_inc(tap_ready.sem, 1)
                for g in range(4):
                    act.wait_ge(conv_ready.sem, conv_ready.at(b, g + 1))
                    v = cv[:, 2 * g:2 * g + 2, :].rearrange("p a q -> p (a q)")
                    fn(v, v, ACT.Silu).then_inc(silu_ready.sem, 1)
                act.wait_ge(sB2_done.sem, sB2_done.at(b, 1))
                fn(sB2[:, :], ps[:, 7, 0:S], ACT.Copy).then_inc(sB2_ready.sem, 1)

        @block.vector
        def _(dve):
            tt, ts, stt, cp, red = (dve.tensor_tensor, dve.tensor_scalar, dve.scalar_tensor_tensor,
                                    dve.tensor_copy, dve.tensor_reduce)
            n_setup = [0]

            def did(ins):
                n_setup[0] += 1
                ins.then_inc(setup_dve, 1)
                dve.wait_ge(setup_dve, n_setup[0])

            dve.wait_ge(ld["ffn"], 32)
            for k, w in enumerate((st1, st2)):
                did(red(absum[:, k:k + 1], w, AX.X, ALU.add, apply_absolute_value=True))
            dve.wait_ge(setup_pe, 5)
            did(ts(mw[:, :], ps[:, 7, 0:2], 1.0 / (F * D), 1e-5, ALU.mult, ALU.max))
            did(dve.reciprocal(ws[:, :], mw[:, :]))
            for k, (w, dst) in enumerate(((st1, stb1), (st2, stb2))):
                did(ts(w, w, ws[:, k:k + 1], MAGIC, ALU.mult, ALU.add))
                did(ts(w, w, MAGIC, 1.0, ALU.subtract, ALU.min))
                did(ts(dst, w, -1.0, None, ALU.max))
            assert n_setup[0] == SETUP_DVE_Q
            dve.wait_ge(setup_pe, 4)
            dve.wait_ge(consts_made, 11)
            for k, dst in enumerate((wqT, wkT)):
                for a in range(2):
                    for c in range(DC):
                        did(cp(dst[:, c, 2 * a:2 * a + 2, :, 0:DH1],
                               ps[:, k, (2 * a + c) * P:(2 * a + c + 1) * P].rearrange("p (g i c) -> p g i c", g=2, i=HI)))
            for k, dst in ((2, wvT), (3, woT)):
                for c in range(DC):
                    did(cp(dst[:, c, :].rearrange("p (a n) -> p a n", a=2),
                           ps[:, k, :].rearrange("p (a c n) -> p a c n", a=2, c=DC)[:, :, c, :]))
            dve.wait_ge(ld["bias"], 16 * (7 + 2 * HI))
            did(ts(bqp[:, :], bqp[:, :], DH1 ** -0.5, None, ALU.mult))
            dve.wait_ge(setup_pe, 6)
            for c in range(DC):
                did(cp(f1T[:, c, :], psb[:, 4 + c, :]))
            for n in range(2):
                did(cp(f2T[:, 4 * n:4 * n + 4, :].rearrange("p a n -> p (a n)"), psb[:, 6 + n, :]))
            assert n_setup[0] == SETUP_DVE_END, n_setup[0]

            links = [0]

            def link(b, ins):
                links[0] += 1
                ins.then_inc(vec_link.sem, 1)
                dve.wait_ge(vec_link.sem, vec_link.at(b, links[0]))

            def stats(b, n, srcs, scale, add):
                for t, src in enumerate(srcs):
                    ins = dve.bn_stats(st[0:src.shape[0], t, :], src)
                link(b, ins)
                dve.nop(nofuse=True)
                for t, src in enumerate(srcs):
                    ins = dve.bn_aggr(mv[0:src.shape[0], t, :], st[0:src.shape[0], t, :])
                link(b, ins)
                if n == 1:
                    ts(var[:, 2:3], mv[:, 2, 1:2], EPS, None, ALU.add)
                ts(var[:, 0:2], mv[:, 0:2, 1], scale, add, ALU.mult, ALU.add).then_inc(var_ready.sem, 1)

            def normalise(b, n, dst, src):
                dve.wait_ge(rstd_ready.sem, rstd_ready.at(b, n))
                for t in range(TT):
                    ins = ts(dst[:, t, :], src[:, t, :], mv[:, t, 0:1], rstd[:, t:t + 1], ALU.subtract, ALU.mult)
                return ins

            def tiles(a):
                return [a[:, t, :] for t in range(TT)]

            def maxes(b, s):
                dve.wait_ge(score_done.sem, score_done.at(b, s + 1))
                k = 2 * (s % 2)
                red(nmax[:, s % 2, :], ps[:, k:k + 2, 0:KEYS], AX.X, ALU.max, negate=True).then_inc(max_ready.sem, 1)

            def k_out(b, p):
                dve.wait_ge(k_done.sem, k_done.at(b, p + 1))
                cp(kT[:, p % 2, :], ps[:, 7, 0:KEYS]).then_inc(k_ready.sem, 1)

            def norm(b, s):
                p, t = divmod(s, TT)
                dve.wait_ge(pv_done.sem, pv_done.at(b, s + 1))
                o = ps[:, 6, 0:2 * (DH0 + 1)].rearrange("p (h d) -> p h d", h=2)
                link(b, dve.reciprocal(rinv[:, :], o[:, :, DH0]))
                tt(aN[:, t, p * P:(p + 1) * P].rearrange("p (h d) -> p h d", h=2), o[:, :, 0:DH0],
                   rinv[:, :].unsqueeze(2).to_broadcast([P, 2, DH0]), ALU.mult).then_inc(norm_ready.sem, 1)

            with dve.Fori(0, B) as b:
                links[0] = 0
                dve.wait_ge(x_in.sem, x_in.at(b, 16))
                dve.wait_ge(c_in.sem, c_in.at(b, 16))
                stats(b, 1, tiles(xin) + [cin[:, :]], 1.0 + EPS, EPS * EPS)
                normalise(b, 1, xn, xin)
                ts(cn[:, :], cin[:, :], mv[0:C, 2, 0:1], rstd[0:C, 2:3], ALU.subtract, ALU.mult).then_inc(xn_ready.sem, 1)
                dve.wait_ge(cT_done.sem, cT_done.at(b, 1))
                for c in range(DC):
                    ts(kvT[:, c, S:KEYS], ps[:, 7, c * C:(c + 1) * C], g1[:, c:c + 1], bb1[:, c:c + 1], ALU.mult, ALU.add)
                cp(cT[:, :, :].rearrange("p c q -> p (c q)"), ps[:, 7, 2 * C:4 * C]).then_inc(cT_ready.sem, 1)
                for k in range(KT):
                    dve.wait_ge(v_done.sem, v_done.at(b, 2 * k + 2))
                    cp(V[:, k, 8:16, 0:DH0], ps[0:KP, 2 * k + 1, :].rearrange("p (h d) -> p h d", d=DH0)).then_inc(v_dve.sem, 1)
                k_out(b, 0)
                maxes(b, 0)
                for s in range(STEPS):
                    if s + 1 < STEPS:
                        maxes(b, s + 1)
                    if s >= 1:
                        norm(b, s - 1)
                    dve.wait_ge(pt_done.sem, pt_done.at(b, s + 1))
                    cp(PT[:, s % 2, 1, :, :].rearrange("p k q -> p (k q)"), ps[0:KP, 5, 0:KT * P]).then_inc(pt_dve.sem, 1)
                    if s % TT == 0 and s // TT + 1 < PAIRS:
                        k_out(b, s // TT + 1)
                norm(b, STEPS - 1)
                for g in (1, 3):
                    dve.wait_ge(aT_done.sem, aT_done.at(b, g + 1))
                    cp(aT[:, 2 * g:2 * g + 2, :].rearrange("p a q -> p (a q)"), ps[:, g, :]).then_inc(aT_dve.sem, 1)
                for t in range(TT):
                    dve.wait_ge(wo_done.sem, wo_done.at(b, t + 1))
                    ins = tt(x1[:, t, :], ps[:, 4 + t, 0:D], xin[:, t, :], ALU.add)
                ins.then_inc(x1_ready.sem, 1)
                dve.wait_ge(x1_ready.sem, x1_ready.at(b, 1))
                stats(b, 2, tiles(x1), 1.0, EPS)
                normalise(b, 2, xn, x1).then_inc(xn_ready.sem, 1)
                dve.wait_ge(logit_done.sem, logit_done.at(b, 1))
                link(b, stt(lg[:, :], ps[0:1, 7, 0:E], 1.0 / S, brow[:, :], ALU.mult, ALU.add))
                red(nlg[:, :], lg[:, :], AX.X, ALU.max, negate=True).then_inc(logit_ready.sem, 1)
                dve.wait_ge(rexp_ready.sem, rexp_ready.at(b, 1))
                link(b, dve.reciprocal(rex[:, :], exs[:, :]))
                link(b, ts(rw[:, :], ex[:, :], rex[:, 0:1], None, ALU.mult))
                dve.nop(nofuse=True)
                link(b, dve.max(top[:, :], rw[:, :]))
                dve.nop(nofuse=True)
                dve.max_index(idx[:, :], top[:, :], rw[:, :]).then_inc(idx_ready.sem, 1)
                tt(gap[:, :], top[:, 1:2], top[:, 0:1], ALU.subtract).then_inc(gap_ready.sem, 1)
                dve.wait_ge(egap_ready.sem, egap_ready.at(b, 1))
                link(b, ts(wden[:, :], egap[:, :], 1.0, None, ALU.add))
                link(b, dve.reciprocal(wtop[:, 0:1], wden[:, :]))
                tt(wtop[:, 1:2], egap[:, :], wtop[:, 0:1], ALU.mult).then_inc(wtop_ready.sem, 1)
                dve.wait_ge(wtop_ready.sem, wtop_ready.at(b, 1))
                for k in range(TOPK):
                    ins = ts(wrow[:, k, :], ones[0:1, :], wtop[:, k:k + 1], None, ALU.mult)
                ins.then_inc(wrow_ready.sem, 1)
                dve.wait_ge(wB_done.sem, wB_done.at(b, 1))
                link(b, cp(wB[:, :], ps[:, 7, 0:2]))
                dve.wait_ge(b2_done.sem, b2_done.at(b, 1))
                for t in range(TT):
                    ins = tt(y2[:, t, :], ps[:, 6, S:S + D], xn[:, t, :], ALU.add)
                link(b, ins)
                for k in range(TOPK):
                    for t in range(TT):
                        dve.wait_ge(moe_done.sem, moe_done.at(b, t + 1))
                        ins = stt(y2[:, t, :], ps[:, 4 + t, k * D:(k + 1) * D], wB[:, k:k + 1], y2[:, t, :], ALU.mult, ALU.add)
                    link(b, ins)
                stats(b, 3, tiles(y2), 1.0, EPS)
                link(b, normalise(b, 3, y2, y2))
                for t in range(TT):
                    ins = tt(y2[:, t, :], y2[:, t, :], gammaB[:, :], ALU.mult)
                link(b, ins)
                dve.wait_ge(x1b_ready.sem, x1b_ready.at(b, 1))
                for t in range(TT):
                    ins = tt(x2[:, t, :], y2[:, t, :], x1b[:, t, :], ALU.add)
                ins.then_inc(x2_ready.sem, 1)
                dve.wait_ge(x2_ready.sem, x2_ready.at(b, 1))
                stats(b, 4, tiles(x2), 1.0, EPS)
                normalise(b, 4, xn, x2).then_inc(xn_ready.sem, 1)
                dve.wait_ge(k1_done.sem, k1_done.at(b, 1))
                for g in range(HG):
                    ins = ts(k1T[:, g, :], ps[:, 2, g * C:(g + 1) * C], bkp[:, g:g + 1], None, ALU.add)
                ins.then_inc(k1_ready.sem, 1)
                dve.wait_ge(v1_done.sem, v1_done.at(b, 1))
                tt(v1[:, :, 0:DH1], ps[0:C, 3, 0:D].rearrange("p (h d) -> p h d", h=H1),
                   bvB[0:C, :].rearrange("p (h d) -> p h d", h=H1), ALU.add).then_inc(v1_ready.sem, 1)
                for t in range(TT):
                    dve.wait_ge(s1_done.sem, s1_done.at(b, t + 1))
                    s1 = ps[:, 4 * t:4 * t + 4, 0:HG * C].rearrange("p i (g c) -> p i g c", g=HG)
                    link(b, red(nmax1[:, t, :, :], s1, AX.X, ALU.max, negate=True))
                    tt(P1[:, t, :, :, :], s1, nmax1[:, t, :, :].unsqueeze(3).to_broadcast([P, HI, HG, C]), ALU.add)\
                        .then_inc(s1_shift.sem, 1)
                for t in range(TT):
                    for i in (1, 3):
                        dve.wait_ge(t1_done.sem, t1_done.at(b, 4 * t + i + 1))
                        if t:
                            dve.wait_ge(pv1_done.sem, pv1_done.at(b, t))
                        cp(PT1[:, i, :, :].rearrange("p g q -> p (g q)"), ps[0:C, 4 * t + i, :]).then_inc(t1_dve.sem, 1)
                    dve.wait_ge(pv1_done.sem, pv1_done.at(b, t + 1))
                    o = ps[:, 4 * t, 0:H1 * (DH1 + 1)].rearrange("p (h d) -> p h d", h=H1)
                    link(b, dve.reciprocal(rinv1[:, :], o[:, :, DH1]))
                    tt(a1[:, t, :].rearrange("p (h d) -> p h d", h=H1), o[:, :, 0:DH1],
                       rinv1[:, :].unsqueeze(2).to_broadcast([P, H1, DH1]), ALU.mult).then_inc(a1_ready.sem, 1)
                dve.wait_ge(wo1_done.sem, wo1_done.at(b, 1))
                dve.wait_ge(x2b_ready.sem, x2b_ready.at(b, 1))
                link(b, tt(x3[:, :, :], ps[:, 2, :].rearrange("p (t d) -> p t d", t=TT), x2b[:, :, :], ALU.add))
                stats(b, 5, tiles(x3), 1.0, EPS)
                link(b, normalise(b, 5, xn, x3))
                link(b, red(am[:, :], xn[:, :, :], AX.X, ALU.max, apply_absolute_value=True))
                link(b, ts(am[:, :], am[:, :], 1e-5, 1.0 / 127.0, ALU.max, ALU.mult))
                link(b, dve.reciprocal(sc[:, :], am[:, :]))
                for t in range(TT):
                    ins = ts(qf[:, t, :], xn[:, t, :], sc[:, t:t + 1], MAGIC, ALU.mult, ALU.add)
                link(b, ins)
                ts(qx[:, :, :], qf[:, :, :], MAGIC, 127.0, ALU.subtract, ALU.min).then_inc(xn_ready.sem, 1)
                for t in range(TT):
                    ins = ts(dg[:, t, :], ident[:, :], am[:, t:t + 1], mw[:, 0:1], ALU.mult, ALU.mult)
                ins.then_inc(dg_ready.sem, 1)
                dve.wait_ge(sB_ready.sem, sB_ready.at(b, 1))
                for g in range(4):
                    dve.wait_ge(f1_done.sem, f1_done.at(b, g + 1))
                    tt(hb[:, 2 * g:2 * g + 2, 1:S + 1], ps[:, g, :].rearrange("p (a q) -> p a q", a=2),
                       sB[:, :].unsqueeze(1).to_broadcast([P, 2, S]), ALU.mult).then_inc(hb_ready.sem, 1)
                for g in range(4):
                    dve.wait_ge(tap_ready.sem, tap_ready.at(b, g + 1))
                    for j in (2 * g, 2 * g + 1):
                        ins = stt(cv[:, j, :], hb[:, j, 0:S], cw[:, j, 0:1], cv[:, j, :], ALU.mult, ALU.add)
                    link(b, ins)
                    for j in (2 * g, 2 * g + 1):
                        ins = stt(cv[:, j, :], hb[:, j, 2:S + 2], cw[:, j, 2:3], cv[:, j, :], ALU.mult, ALU.add)
                    ins.then_inc(conv_ready.sem, 1)
                dve.wait_ge(silu_ready.sem, silu_ready.at(b, 4))
                red(mj[:, :], cv[:, :, :].rearrange("p j q -> p q j"), AX.X, ALU.max, apply_absolute_value=True)\
                    .then_inc(mj_ready.sem, 1)
                dve.wait_ge(mjT_done.sem, mjT_done.at(b, 1))
                link(b, red(am2[:, :], ps[:, 6, 0:S].rearrange("p (t q) -> p t q", t=TT), AX.X, ALU.max))
                link(b, ts(am2[:, :], am2[:, :], 1e-5, 1.0 / 127.0, ALU.max, ALU.mult))
                link(b, dve.reciprocal(sc2[:, :], am2[:, :]))
                for t in range(TT):
                    ins = ts(dg2[:, t, :], ident[:, :], sc2[:, t:t + 1], None, ALU.mult)
                ins.then_inc(dg2_ready.sem, 1)
                ts(inv2[:, :], am2[:, :], mw[:, 1:2], None, ALU.mult)
                dve.wait_ge(sB2_ready.sem, sB2_ready.at(b, 1))
                for g in range(4):
                    v = cv[:, 2 * g:2 * g + 2, :]
                    link(b, tt(v, v, sB2[:, :].unsqueeze(1).to_broadcast([P, 2, S]), ALU.mult))
                    ts(q2[:, 2 * g:2 * g + 2, :], v, MAGIC, MAGIC, ALU.add, ALU.subtract).then_inc(q2_ready.sem, 1)
                for t in range(TT):
                    dve.wait_ge(f2_done.sem, f2_done.at(b, t + 1))
                    ins = stt(x4[:, t, :], ps[:, 4 + t, 0:D], inv2[:, t:t + 1], x3[:, t, :], ALU.mult, ALU.add)
                ins.then_inc(x4_ready.sem, 1)
            assert links[0] == VEC_LINKS, links[0]


SETUP_DVE_Q = 10
SETUP_DVE_END = SETUP_DVE_Q + 8 + 4 + 1 + 4

_INS = ['x', 'ctx_1024', 'L0_xattn_ln1_g', 'L0_xattn_ln1_b', 'L0_xattn_ln2_g', 'L0_xattn_ln2_b', 'L0_xattn_Wq',
        'L0_xattn_Wkv', 'L0_xattn_Wo', 'L0_ffn_W1', 'L0_ffn_b1', 'L0_ffn_W2', 'L0_ffn_b2', 'L0_ffn_Wr', 'L0_ffn_br',
        'L0_ffn_gamma', 'L0_ffn_beta', 'L1_xattn_wq', 'L1_xattn_bq', 'L1_xattn_wk', 'L1_xattn_bk', 'L1_xattn_wv',
        'L1_xattn_bv', 'L1_xattn_wo', 'L1_xattn_bo', 'L1_ffn_w1', 'L1_ffn_conv_w', 'L1_ffn_conv_b', 'L1_ffn_w2']
_OUTS = [((B, S, D), 'float32')]


def kernel(**inputs):
    import numpy as _np
    import concourse.bacc as _bacc
    from concourse import mybir as _mybir
    from concourse.bass_utils import run_bass_kernel_spmd as _run

    nc = _bacc.Bacc("TRN2", target_bir_lowering=False, num_devices=1)
    arrays, args = {}, []
    for name in _INS:
        a = _np.ascontiguousarray(inputs[name])
        arrays[f"in_{name}_dram"] = a
        args.append(nc.dram_tensor(f"in_{name}_dram", a.shape, _mybir.dt.from_np(a.dtype), kind="ExternalInput").ap())
    for i, (shape, dtype) in enumerate(_OUTS):
        dt = _mybir.dt.from_np(_np.dtype(dtype))
        args.append(nc.dram_tensor(f"out_{i}_dram", shape, dt, kind="ExternalOutput").ap())
    build(nc, *args)
    r = _run(nc, [arrays], core_ids=[0])
    return r.results[0]["out_0_dram"]
```

```python
from contextlib import ExitStack

import concourse.bass as bass
from concourse import mybir

F32 = mybir.dt.float32
BF16 = mybir.dt.bfloat16
U32 = mybir.dt.uint32
ALU = mybir.AluOpType
ACT = mybir.ActivationFunctionType
AX = mybir.AxisListType

P = 128
B, S, D = 16, 256, 256
C = 77
DC = D // P
TT = S // P
H0, DH0 = 16, 64
INNER = H0 * DH0
PAIRS = H0 // 2
UNITS = H0 * TT
KEYS = S + C
KT = 3
KP = KEYS // KT
E, F, TOPK = 8, 1024, 2
FT = F // P
H1, DH1 = 16, 16
HT = D // P
HH = H1 // HT
EPS = 1e-5
MAGIC = 1.5 * 2.0 ** 23

SLOTS = 45
CHAIN_AT = 8
UNIT_AT = 5
AFTER = UNIT_AT + UNITS
BANK_S, BANK_PT, BANK_PV, BANK_PJ = (0, 1), 2, 3, 4

FRONT_LINKS = 43
CHAIN_LINKS = 35
TURN_LINKS = 28


class Signal:

    def __init__(self, sem, per):
        self.sem, self.per = sem, per

    def at(self, b, n):
        return b * self.per + n


def first(b):
    return isinstance(b, int) and b == 0


def turns(eng, turn):
    turn(0, front=True, chain=False, tail=False)
    turn(1, front=True, chain=True, tail=False)
    with eng.Fori(2, B) as b:
        turn(b, front=True, chain=True, tail=True)
    turn(B, front=False, chain=True, tail=True)
    turn(B + 1, front=False, chain=False, tail=True)


def build(nc, x, ctx_in, ln1_g, ln1_b, ln2_g, ln2_b, Wq, Wkv, Wo, W1, b1, W2, b2, Wr, br, gamma, beta,
          wq, bq, wk, bk, wv, bv, wo, bo, fw1, conv_w, conv_b, fw2, out):
    assert KT * KP == KEYS and KP <= P
    with ExitStack() as stack:
        def sb(name, shape, dt=F32):
            return stack.enter_context(nc.sbuf_tensor(name, shape, dt))

        def sem(name):
            return stack.enter_context(nc.semaphore(name))

        def signal(name, per):
            return Signal(sem(name), per)

        wq0 = sb("wq0", [P, DC, INNER])
        wkv0 = sb("wkv0", [P, DC, 2 * INNER])
        wo0 = sb("wo0", [P, PAIRS, D])
        wr = sb("wr", [P, DC, E])
        brow = sb("brow", [1, E])
        g1 = sb("g1", [P, DC]); bb1 = sb("bb1", [P, DC])
        g2 = sb("g2", [P, DC]); bb2 = sb("bb2", [P, DC])
        gammaB = sb("gammaB", [P, D]); betaB = sb("betaB", [P, D])
        boB = sb("boB", [P, D]); bvB = sb("bvB", [P, D])
        bqp = sb("bqp", [P, HT]); bkp = sb("bkp", [P, HT])
        wqT = sb("wqT", [P, DC, D]); wkT = sb("wkT", [P, DC, D])
        wvT = sb("wvT", [P, DC, D]); woT = sb("woT", [P, DC, D])
        f1T = sb("f1T", [P, DC, F], BF16)
        f2T = sb("f2T", [P, FT, D], BF16)
        cw = sb("cw", [P, FT, 3]); cb = sb("cb", [P, FT])
        mw = sb("mw", [P, 2]); ws = sb("ws", [P, 2]); absum = sb("absum", [P, 2])
        ident = sb("ident", [P, P]); identb = sb("identb", [P, P], BF16)
        ones = sb("ones", [P, P])
        own = sb("own", [P, HH])
        mhalf = sb("mhalf", [P, 3])
        xin = sb("xin", [P, TT, D]); cin = sb("cin", [C, D])
        xf = sb("xf", [P, TT, D]); cn = sb("cn", [C, D])
        st = sb("st", [P, 3, 6]); mv = sb("mv", [P, 3, 2]); var = sb("var", [P, 3]); rstd = sb("rstd", [P, 3])
        kvT = sb("kvT", [P, DC, KEYS]); cT = sb("cT", [P, DC, C])
        qT = sb("qT", [P, 2, S]); kT = sb("kT", [P, 2, KEYS])
        V = sb("V", [KP, KT, H0, DH0 + 1])
        nmax = sb("nmax", [P, 2])
        Pr = sb("Pr", [P, 2, KEYS])
        PT = sb("PT", [KP, 2, KT * P])
        rinv = sb("rinv", [P, 2])
        aN = sb("aN", [P, TT, INNER])
        aT = sb("aT", [P, PAIRS, S])
        lg = sb("lg", [1, E]); nlg = sb("nlg", [1, 1]); ex = sb("ex", [1, E]); exs = sb("exs", [1, 1])
        rex = sb("rex", [1, 1]); rw = sb("rw", [1, E]); top = sb("top", [1, 8]); idx = sb("idx", [1, 8], U32)
        gap = sb("gap", [1, 1]); egap = sb("egap", [1, 1]); wden = sb("wden", [1, 1]); wtop = sb("wtop", [1, 2])
        ysum = sb("ysum", [P, DC])
        x1 = sb("x1", [P, TT, D]); y1 = sb("y1", [P, TT, D]); yT = sb("yT", [P, DC, S])
        wrow = sb("wrow", [1, 2, P]); wB = sb("wB", [P, 2])
        W1s = sb("W1s", [P, TOPK, DC, F]); W2s = sb("W2s", [P, TOPK, FT, D])
        b1r = sb("b1r", [FT, TOPK, P]); b2r = sb("b2r", [1, TOPK, D])
        k1 = sb("k1", [P, HT, C])
        k1d = sb("k1d", [P, HT, HH, C])
        v1 = sb("v1", [C, H1, DH1 + 1])
        b1T = sb("b1T", [P, TOPK * FT])
        hT = sb("hT", [P, TOPK, FT, S])
        y2 = sb("y2", [P, TT, D]); x2 = sb("x2", [P, TT, D]); x3 = sb("x3", [P, TT, D]); xn = sb("xn", [P, TT, D])
        st2 = sb("st2", [P, TT, 6]); mv2 = sb("mv2", [P, TT, 2]); var2 = sb("var2", [P, TT]); rstd2 = sb("rstd2", [P, TT])
        q1T = sb("q1T", [P, HT, S])
        nmax1 = sb("nmax1", [P, HH]); P1 = sb("P1", [P, H1, C])
        rinv1 = sb("rinv1", [P, H1]); a1 = sb("a1", [P, TT, D])
        am = sb("am", [P, TT]); sc = sb("sc", [P, TT])
        qx = sb("qx", [P, TT, D], BF16); qxT = sb("qxT", [P, DC, S], BF16)
        dg = sb("dg", [P, TT, P]); sB = sb("sB", [P, S])
        hb = sb("hb", [P, FT, S + 2])
        mj = sb("mj", [P, S])
        q2 = sb("q2", [P, FT, S], BF16)
        am2 = sb("am2", [P, TT]); inv2 = sb("inv2", [P, TT])
        PT1 = hT[0:C, 1, :, :].rearrange("p a q -> p (a q)").rearrange("p (h q) -> p h q", h=H1)
        cv = hT[:, 0, :, :]
        a1T = yT
        x4 = y2
        stg1 = W1s[:, 0, :, :].rearrange("p a n -> p (a n)")
        stg2 = W1s[:, 1, :, :].rearrange("p a n -> p (a n)")
        stgq = hT[:, 0, :, :].rearrange("p a n -> p (a n)")
        stb1 = q2[:, :, :].rearrange("p a n -> p (a n)")
        stb2 = hT[:, 1, :, :].rearrange("p a n -> p (a n)").bitcast(BF16)[:, 0:FT * D]

        ps = stack.enter_context(nc.psum_tensor("ps", [P, 8, 512], F32))
        psb = ps[:, :, :].rearrange("p a n -> p (a n)").bitcast(BF16).rearrange("p (a n) -> p a n", a=8)

        ld = {n: sem(f"ld_{n}") for n in ("vec", "w0", "l1", "ffn", "bias")}
        ident_made = sem("ident_made"); consts_made = sem("consts_made")
        setup_pe = sem("setup_pe"); setup_dve = sem("setup_dve")
        x_in = signal("x_in", 16); c_in = signal("c_in", 16); out_done = signal("out_done", 16)
        var_ready = signal("var_ready", 2); rstd_ready = signal("rstd_ready", 2)
        xf_ready = signal("xf_ready", 1); xT_done = signal("xT_done", 1); cT_done = signal("cT_done", 1)
        kvx_ready = signal("kvx_ready", 1); kvc_ready = signal("kvc_ready", 1)
        v_done = signal("v_done", 2 * KT); v_act = signal("v_act", KT); v_dve = signal("v_dve", KT)
        q_done = signal("q_done", PAIRS); q_ready = signal("q_ready", PAIRS)
        k_done = signal("k_done", PAIRS); k_ready = signal("k_ready", PAIRS)
        score_done = signal("score_done", UNITS); max_ready = signal("max_ready", UNITS)
        exp_ready = signal("exp_ready", UNITS); pt_done = signal("pt_done", UNITS); pt_ready = signal("pt_ready", UNITS)
        pv_done = signal("pv_done", UNITS); norm_ready = signal("norm_ready", UNITS)
        aT_done = signal("aT_done", 4); aT_act = signal("aT_act", 2); aT_dve = signal("aT_dve", 2)
        wo_done = signal("wo_done", TT); x1_ready = signal("x1_ready", TT)
        k1_done = signal("k1_done", 1); v1_done = signal("v1_done", 1); k1v1_ready = signal("k1v1_ready", 1)
        y1_ready = signal("y1_ready", 1); y1T_done = signal("y1T_done", 1); y1T_ready = signal("y1T_ready", 1)
        logit_done = signal("logit_done", 1); logit_ready = signal("logit_ready", 1)
        rexp_ready = signal("rexp_ready", 1); idx_ready = signal("idx_ready", 1)
        gap_ready = signal("gap_ready", 1); egap_ready = signal("egap_ready", 1)
        wtop_ready = signal("wtop_ready", 1); wB_done = signal("wB_done", 1); wB_ready = signal("wB_ready", 1)
        w1_in = [signal(f"w1_in{e}", 16) for e in range(TOPK)]
        w2_in = [signal(f"w2_in{e}", 16) for e in range(TOPK)]
        b_in = signal("b_in", 16 * 2 * TOPK)
        x1b_ready = signal("x1b_ready", 1)
        b1T_done = signal("b1T_done", 1); b1T_ready = signal("b1T_ready", 1)
        h_done = signal("h_done", TOPK * FT // 2); gelu_ready = signal("gelu_ready", TOPK * FT // 2)
        moe_done = signal("moe_done", TOPK); b2_done = signal("b2_done", 1)
        var2_ready = signal("var2_ready", 3); rstd2_ready = signal("rstd2_ready", 3)
        xn_ready = signal("xn_ready", 1); x2b_ready = signal("x2b_ready", 1)
        ynT_done = signal("ynT_done", 1); ynT_ready = signal("ynT_ready", 1)
        q1_done = signal("q1_done", 1); q1_ready = signal("q1_ready", 1)
        s1_done = signal("s1_done", TT * HT); s1_shift = signal("s1_shift", TT * HT); e1_ready = signal("e1_ready", TT)
        t1_done = signal("t1_done", TT * 4); t1_act = signal("t1_act", TT * 2); t1_dve = signal("t1_dve", TT * 2)
        pv1_done = signal("pv1_done", TT); a1_ready = signal("a1_ready", TT)
        a1T_done = signal("a1T_done", 1); a1T_ready = signal("a1T_ready", 1); wo1_done = signal("wo1_done", 1)
        qx_ready = signal("qx_ready", 1); dg_ready = signal("dg_ready", 2)
        qxT_done = signal("qxT_done", 1); qxT_ready = signal("qxT_ready", 1)
        sB_done = signal("sB_done", 2); sB_ready = signal("sB_ready", 2)
        f1_done = signal("f1_done", 4); hb_ready = signal("hb_ready", 4); tap_ready = signal("tap_ready", 4)
        conv_ready = signal("conv_ready", 4); silu_ready = signal("silu_ready", 4)
        mj_ready = signal("mj_ready", 1); mjT_done = signal("mjT_done", 1)
        q2_ready = signal("q2_ready", 4); f2_done = signal("f2_done", TT); x4_ready = signal("x4_ready", 1)
        front_link = signal("front_link", FRONT_LINKS); chain_link = signal("chain_link", CHAIN_LINKS)

        block = stack.enter_context(nc.Block())

        def row(v):
            return v.rearrange("(a n) -> a n", a=1)

        def flat(v):
            return v.rearrange("p a n -> p (a n)")

        def walk(b, front, chain, tail, front_slot, chain_part):
            for s in range(SLOTS):
                if not front and s >= CHAIN_AT and not chain:
                    break

                def part(b=b, s=s):
                    if s < CHAIN_AT:
                        if tail:
                            chain_part(b - 2, s + SLOTS - CHAIN_AT)
                    elif chain:
                        chain_part(b - 1, s - CHAIN_AT)

                if front:
                    front_slot(b, s, part)
                else:
                    part()

        @block.sync
        def _(sp):
            def load_x(b):
                sp.dma_start(xin[:, :, :], x[b].rearrange("(t p) d -> p t d", p=P)).then_inc(x_in.sem, 16)
                sp.dma_start(cin[:, :], ctx_in[b]).then_inc(c_in.sem, 16)

            load_x(0)
            with nc.allow_non_contiguous_dma(reason="small vectors laid out one feature per partition"):
                for dst, src in ((g1, ln1_g), (bb1, ln1_b), (g2, ln2_g), (bb2, ln2_b)):
                    sp.dma_start(dst[:, :], src.rearrange("(c p) -> p c", p=P)).then_inc(ld["vec"], 16)
                sp.dma_start(stg1, fw1.rearrange("(a p) n -> p a n", p=P)).then_inc(ld["ffn"], 16)
                sp.dma_start(stg2, fw2.rearrange("(a p) n -> p a n", p=P)).then_inc(ld["ffn"], 16)
                for k, w in enumerate((wq, wk, wv, wo)):
                    sp.dma_start(stgq[:, k * 512:(k + 1) * 512], w.rearrange("(a p) n -> p a n", p=P))\
                      .then_inc(ld["l1"], 16)
                sp.dma_start(wq0[:, :, :], Wq.rearrange("(c p) n -> p c n", p=P)).then_inc(ld["w0"], 16)
                sp.dma_start(wkv0[:, :, :], Wkv.rearrange("(c p) n -> p c n", p=P)).then_inc(ld["w0"], 16)
                sp.dma_start(wo0[:, :, :], Wo.rearrange("(j p) n -> p j n", p=P)).then_inc(ld["w0"], 16)
                sp.dma_start(wr[:, :, :], Wr.rearrange("(c p) n -> p c n", p=P)).then_inc(ld["w0"], 16)
                sp.dma_start(brow[:, :], row(br)).then_inc(ld["bias"], 16)
                sp.dma_start(cw[:, :, :], conv_w.rearrange("(j p) a k -> p j (a k)", p=P)).then_inc(ld["bias"], 16)
                sp.dma_start(cb[:, :], conv_b.rearrange("(j p) -> p j", p=P)).then_inc(ld["bias"], 16)
                for dst, src in ((gammaB, gamma), (betaB, beta), (boB, bo), (bvB, bv)):
                    sp.dma_start(dst[:, :], row(src).to_broadcast([P, D])).then_inc(ld["bias"], 16)
                for dst, src in ((bqp, bq), (bkp, bk)):
                    sp.dma_start(dst[:, :], src.rearrange("(t p) -> p t", p=P)).then_inc(ld["bias"], 16)
            sp.wait_ge(setup_dve, SETUP_DVE_END)

            def turn(b, front, chain, tail):
                if tail:
                    sp.wait_ge(x4_ready.sem, x4_ready.at(b - 2, 1))
                    sp.nop(nofuse=True)
                    sp.dma_start(out[b - 2].rearrange("(t p) d -> p t d", p=P), x4[:, :, :]).then_inc(out_done.sem, 16)
                if front:
                    sp.wait_ge(x1_ready.sem, x1_ready.at(b, TT))
                    sp.nop(nofuse=True)
                    sp.wait_ge(cT_done.sem, cT_done.at(b, 1))
                    sp.nop(nofuse=True)
                    load_x((b + 1) % B)
                    sp.wait_ge(idx_ready.sem, idx_ready.at(b, 1))
                    sp.nop(nofuse=True)
                    for k in range(TOPK):
                        e = sp.value_load(idx[0:1, k:k + 1], min_val=0, max_val=E - 1)
                        sp.dma_start(b1r[:, k, :], b1[e].rearrange("(j p) -> j p", p=P)).then_inc(b_in.sem, 16)
                        sp.dma_start(b2r[:, k, :], row(b2[e])).then_inc(b_in.sem, 16)
                        sp.dma_start(W1s[:, k, :, :], W1[e].rearrange("(c p) n -> p c n", p=P)).then_inc(w1_in[k].sem, 16)
                        sp.dma_start(W2s[:, k, :, :], W2[e].rearrange("(j p) n -> p j n", p=P)).then_inc(w2_in[k].sem, 16)

            turns(sp, turn)
            sp.wait_ge(out_done.sem, 16 * B)
            sp.wait_ge(x_in.sem, 16 * (B + 1))
            sp.wait_ge(c_in.sem, 16 * (B + 1))

        @block.gpsimd
        def _(pool):
            pool.memset(ident[:, :], 0.0).then_inc(ident_made, 1)
            pool.memset(identb[:, :], 0.0).then_inc(ident_made, 1)
            pool.memset(ones[:, :], 1.0).then_inc(consts_made, 1)
            pool.memset(mhalf[:, :], -0.5).then_inc(consts_made, 1)
            pool.memset(own[:, :], 1.0).then_inc(consts_made, 1)
            pool.wait_ge(ident_made, 2)
            for m in (ident, identb):
                pool.affine_select(out=m[:, :], in_=m[:, :], compare_op=ALU.not_equal, fill=1.0,
                                   base=0, pattern=[[-1, P]], channel_multiplier=1).then_inc(ident_made, 1)
            pool.wait_ge(consts_made, 3)
            pool.affine_select(out=own[:, :], in_=own[:, :], compare_op=ALU.is_ge, fill=0.0,
                               base=0, pattern=[[-DH1, HH]], channel_multiplier=1).then_inc(consts_made, 1)
            pool.wait_ge(consts_made, 4)
            pool.affine_select(out=own[:, :], in_=own[:, :], compare_op=ALU.is_ge, fill=0.0,
                               base=DH1 - 1, pattern=[[DH1, HH]], channel_multiplier=-1).then_inc(consts_made, 1)
            pool.memset(V[:, :, :, DH0:DH0 + 1], 1.0).then_inc(consts_made, 1)
            pool.memset(v1[:, :, DH1:DH1 + 1], 1.0).then_inc(consts_made, 1)
            pool.memset(hb[:, :, 0:1], 0.0).then_inc(consts_made, 1)
            pool.memset(hb[:, :, S + 1:S + 2], 0.0).then_inc(consts_made, 1)
            pool.memset(mv[:, :, :], 1.0).then_inc(consts_made, 1)
            pool.wait_ge(consts_made, CONSTS)
            pool.wait_ge(ld["bias"], 16 * 9)

            def front_slot(b, s, chain):
                for n, at in ((1, 0), (2, AFTER + 4)):
                    if s == at:
                        pool.wait_ge(var_ready.sem, var_ready.at(b, n))
                        pool.tensor_tensor(rstd[:, :], var[:, :], mhalf[:, :], ALU.pow).then_inc(rstd_ready.sem, 1)
                chain()

            def chain_part(b, c):
                if c == 0:
                    pool.wait_ge(y1_ready.sem, y1_ready.at(b, 1))
                    for t in range(TT):
                        ins = pool.tensor_tensor(x1[:, t, :], x1[:, t, :], betaB[:, :], ALU.add)
                    ins.then_inc(x1b_ready.sem, 1)
                if c == 17:
                    pool.wait_ge(xn_ready.sem, xn_ready.at(b, 1))
                    for t in range(TT):
                        ins = pool.tensor_tensor(x2[:, t, :], x2[:, t, :], boB[:, :], ALU.add)
                    ins.then_inc(x2b_ready.sem, 1)
                for n, at in ((1, 13), (2, 15), (3, 30)):
                    if c == at:
                        pool.wait_ge(var2_ready.sem, var2_ready.at(b, n))
                        pool.tensor_tensor(rstd2[:, :], var2[:, :], mhalf[:, 0:TT], ALU.pow).then_inc(rstd2_ready.sem, 1)

            turns(pool, lambda b, front, chain, tail: walk(b, front, chain, tail, front_slot, chain_part))

        @block.tensor
        def _(pe):
            mm, tr = pe.matmul, pe.transpose
            pe.wait_ge(ident_made, 4)
            pe.wait_ge(consts_made, CONSTS)
            pe.wait_ge(ld["l1"], 64)
            for k in range(4):
                for a in range(2):
                    for c in range(DC):
                        ins = tr(ps[:, k, (2 * a + c) * P:(2 * a + c + 1) * P],
                                 stgq[:, k * 512 + a * 256 + c * P:k * 512 + a * 256 + (c + 1) * P], ident[:, :])
                ins.then_inc(setup_pe, 1)
            pe.wait_ge(setup_dve, 2)
            mm(ps[:, 7, 0:2], ones[:, :], absum[:, :], start=True, stop=True).then_inc(setup_pe, 1)
            pe.wait_ge(setup_dve, SETUP_DVE_Q)
            for c in range(DC):
                for j in range(FT):
                    ins = tr(psb[:, 4 + c, j * P:(j + 1) * P], stb1[:, j * D + c * P:j * D + (c + 1) * P], identb[:, :])
            for j in range(FT):
                for c in range(DC):
                    ins = tr(psb[:, 6 + j // 4, (j % 4) * 256 + c * P:(j % 4) * 256 + (c + 1) * P],
                             stb2[:, c * F + j * P:c * F + (j + 1) * P], identb[:, :])
            ins.then_inc(setup_pe, 1)
            pe.wait_ge(ld["w0"], 64)
            pe.wait_ge(setup_dve, SETUP_DVE_END)

            def transpose_tokens(dst, bank, src, idn):
                for c in range(DC):
                    for t in range(TT):
                        ins = tr(dst[:, bank, c * S + t * P:c * S + (t + 1) * P], src[:, t, c * P:(c + 1) * P], idn[:, :])
                return ins

            def project_q(b, p):
                if p:
                    pe.wait_ge(k_ready.sem, k_ready.at(b, p))
                for c in range(DC):
                    ins = mm(ps[:, BANK_PJ, 0:S], wq0[:, c, p * P:(p + 1) * P], kvT[:, c, 0:S], start=c == 0, stop=c == DC - 1)
                ins.then_inc(q_done.sem, 1)

            def project_k(b, p):
                pe.wait_ge(q_ready.sem, q_ready.at(b, p + 1))
                for c in range(DC):
                    ins = mm(ps[:, BANK_PJ, 0:KEYS], wkv0[:, c, p * P:(p + 1) * P], kvT[:, c, :], start=c == 0, stop=c == DC - 1)
                ins.then_inc(k_done.sem, 1)

            def project_v(b, i, bank):
                k, n = divmod(i, 2)
                for c in range(DC):
                    ins = mm(ps[0:KP, bank, :], kvT[:, c, k * KP:(k + 1) * KP],
                             wkv0[:, c, INNER + n * 512:INNER + (n + 1) * 512], start=c == 0, stop=c == DC - 1)
                ins.then_inc(v_done.sem, 1)

            def scores(b, u):
                p, t, h = u // 4, u // 2 % 2, u % 2
                pe.wait_ge(k_ready.sem, k_ready.at(b, p + 1))
                if u >= 2:
                    pe.wait_ge(exp_ready.sem, exp_ready.at(b, u - 1))
                r = slice(DH0 * h, DH0 * h + DH0)
                mm(ps[:, BANK_S[u % 2], 0:KEYS], qT[r, p % 2, t * P:(t + 1) * P], kT[r, p % 2, :],
                   start=True, stop=True).then_inc(score_done.sem, 1)

            def transpose_p(b, u):
                pe.wait_ge(exp_ready.sem, exp_ready.at(b, u + 1))
                if u:
                    pe.wait_ge(pt_ready.sem, pt_ready.at(b, u))
                for k in range(KT):
                    ins = tr(ps[0:KP, BANK_PT, k * P:(k + 1) * P], Pr[:, u % 2, k * KP:(k + 1) * KP], ident[:, :])
                ins.then_inc(pt_done.sem, 1)

            def attend(b, u):
                pe.wait_ge(pt_ready.sem, pt_ready.at(b, u + 1))
                if u:
                    pe.wait_ge(norm_ready.sem, norm_ready.at(b, u))
                for k in range(KT):
                    ins = mm(ps[:, BANK_PV, 0:DH0 + 1], PT[:, u % 2, k * P:(k + 1) * P], V[:, k, 2 * (u // 4) + u % 2, :],
                             start=k == 0, stop=k == KT - 1)
                ins.then_inc(pv_done.sem, 1)

            def front_slot(b, s, chain):
                u = s - UNIT_AT
                if 0 <= u < UNITS:
                    if u + 1 < UNITS:
                        scores(b, u + 1)
                    chain()
                    if u:
                        attend(b, u - 1)
                    transpose_p(b, u)
                    ahead = u // 4 + 1 < PAIRS
                    if ahead and u % 4 == 0:
                        project_q(b, u // 4 + 1)
                    if ahead and u % 4 == 1:
                        project_k(b, u // 4 + 1)
                    return
                chain()
                if s == 1:
                    pe.wait_ge(xf_ready.sem, xf_ready.at(b, 1))
                    transpose_tokens(ps, 0, xf, ident).then_inc(xT_done.sem, 1)
                    for n, src in enumerate((cn, cin)):
                        for c in range(DC):
                            ins = tr(ps[:, 1, (2 * n + c) * C:(2 * n + c + 1) * C], src[:, c * P:(c + 1) * P], ident[0:C, 0:C])
                    ins.then_inc(cT_done.sem, 1)
                if s == 2:
                    pe.wait_ge(kvx_ready.sem, kvx_ready.at(b, 1))
                    pe.wait_ge(kvc_ready.sem, kvc_ready.at(b, 1))
                    project_q(b, 0)
                    project_v(b, 0, 2)
                    project_v(b, 1, 3)
                if s == 3:
                    project_v(b, 2, 0)
                    project_v(b, 3, 1)
                    project_k(b, 0)
                if s == 4:
                    pe.wait_ge(v_act.sem, v_act.at(b, 1))
                    pe.wait_ge(v_dve.sem, v_dve.at(b, 1))
                    project_v(b, 4, 2)
                    project_v(b, 5, 3)
                    pe.wait_ge(v_act.sem, v_act.at(b, 3))
                    pe.wait_ge(v_dve.sem, v_dve.at(b, 3))
                    scores(b, 0)
                if s == AFTER:
                    attend(b, UNITS - 1)
                    pe.wait_ge(norm_ready.sem, norm_ready.at(b, UNITS))
                if s in (AFTER, AFTER + 1):
                    for g in (2 * (s - AFTER), 2 * (s - AFTER) + 1):
                        for p in (2 * g, 2 * g + 1):
                            for t in range(TT):
                                ins = tr(ps[:, (0, 1, 2, 4)[g], (p % 2) * S + t * P:(p % 2) * S + (t + 1) * P],
                                         aN[:, t, p * P:(p + 1) * P], ident[:, :])
                        ins.then_inc(aT_done.sem, 1)
                if s in (AFTER + 2, AFTER + 3):
                    t = s - AFTER - 2
                    pe.wait_ge(aT_act.sem, aT_act.at(b, 2))
                    pe.wait_ge(aT_dve.sem, aT_dve.at(b, 2))
                    for p in range(PAIRS):
                        ins = mm(ps[:, (3, 0)[t], 0:D], aT[:, p, t * P:(t + 1) * P], wo0[:, p, :], start=p == 0, stop=p == PAIRS - 1)
                    ins.then_inc(wo_done.sem, 1)
                if s == AFTER + 2:
                    for g in range(HT):
                        for c in range(DC):
                            ins = mm(ps[:, 1, g * C:(g + 1) * C], wkT[:, c, g * P:(g + 1) * P], cT[:, c, :],
                                     start=c == 0, stop=c == DC - 1)
                    ins.then_inc(k1_done.sem, 1)
                    for c in range(DC):
                        ins = mm(ps[0:C, 2, 0:D], cT[:, c, :], wvT[:, c, :], start=c == 0, stop=c == DC - 1)
                    ins.then_inc(v1_done.sem, 1)
                if s == AFTER + 5:
                    pe.wait_ge(y1_ready.sem, y1_ready.at(b, 1))
                    transpose_tokens(ps, 4, y1, ident).then_inc(y1T_done.sem, 1)
                if s == AFTER + 6:
                    pe.wait_ge(y1T_ready.sem, y1T_ready.at(b, 1))
                    for c in range(DC):
                        ins = mm(ps[0:1, 0, 0:E], ysum[:, c:c + 1], wr[:, c, :], start=c == 0, stop=c == DC - 1)
                    ins.then_inc(logit_done.sem, 1)
                if s == AFTER + 7:
                    pe.wait_ge(wtop_ready.sem, wtop_ready.at(b, 1))
                    pe.nop(nofuse=True)
                    mm(ps[:, 1, 0:2], ones[0:1, :], wtop[:, :], start=True, stop=True).then_inc(wB_done.sem, 1)

            def layer1_scores(b, n):
                t, g = divmod(n, HT)
                if n == 0:
                    pe.wait_ge(q1_ready.sem, q1_ready.at(b, 1))
                    pe.wait_ge(k1v1_ready.sem, k1v1_ready.at(b, 1))
                elif g:
                    pe.wait_ge(s1_shift.sem, s1_shift.at(b, n))
                else:
                    pe.wait_ge(a1_ready.sem, a1_ready.at(b, t))
                for m in range(2):
                    ins = mm(ps[:, ((5, 6), (7, 5))[g][m], 0:4 * C], q1T[:, g, t * P:(t + 1) * P],
                             k1d[:, g, 4 * m:4 * m + 4, :].rearrange("p h c -> p (h c)"), start=True, stop=True)
                ins.then_inc(s1_done.sem, 1)

            def layer1_transpose(b, t, ms):
                if ms[0] == 0:
                    pe.wait_ge(e1_ready.sem, e1_ready.at(b, t + 1))
                for m in ms:
                    if m == 3:
                        pe.wait_ge(t1_act.sem, t1_act.at(b, 2 * t + 1))
                    for h in range(4 * m, 4 * m + 4):
                        ins = tr(ps[0:C, (6, 7, 5, 6)[m], (h % 4) * P:(h % 4 + 1) * P], P1[:, h, :], ident[:, :])
                    ins.then_inc(t1_done.sem, 1)

            def layer1_attend(b, t):
                pe.wait_ge(t1_act.sem, t1_act.at(b, 2 * t + 2))
                pe.wait_ge(t1_dve.sem, t1_dve.at(b, 2 * t + 2))
                for h in range(H1):
                    ins = mm(ps[:, 7, h * (DH1 + 1):(h + 1) * (DH1 + 1)], PT1[:, h, :], v1[:, h, :], start=True, stop=True)
                ins.then_inc(pv1_done.sem, 1)

            def chain_part(b, c):
                if c == 0:
                    pe.wait_ge(b_in.sem, b_in.at(b, 16 * 2 * TOPK))
                    pe.nop(nofuse=True)
                    for k in range(TOPK):
                        ins = tr(ps[:, 7, k * FT:(k + 1) * FT], b1r[:, k, :], ident[0:FT, 0:FT])
                    ins.then_inc(b1T_done.sem, 1)
                if c == 1:
                    if not first(b):
                        pe.wait_ge(x4_ready.sem, x4_ready.at(b, 0))
                if 1 <= c <= 8:
                    i = c - 1
                    k = i // 4
                    if i % 4 == 0:
                        pe.wait_ge(w1_in[k].sem, w1_in[k].at(b, 16))
                    if i == 2:
                        pe.wait_ge(b1T_ready.sem, b1T_ready.at(b, 1))
                    if i >= 3:
                        pe.wait_ge(gelu_ready.sem, gelu_ready.at(b, i - 2))
                    for j in (2 * (i % 4), 2 * (i % 4) + 1):
                        for d in range(DC):
                            ins = mm(ps[:, 5 + i % 3, (j % 2) * S:(j % 2 + 1) * S], W1s[:, k, d, j * P:(j + 1) * P], yT[:, d, :],
                                     start=d == 0, stop=d == DC - 1)
                    ins.then_inc(h_done.sem, 1)
                if c == 11:
                    pe.wait_ge(gelu_ready.sem, gelu_ready.at(b, 8))
                    pe.wait_ge(wB_ready.sem, wB_ready.at(b, 1))
                    pe.nop(nofuse=True)
                    for k in range(TOPK):
                        ins = mm(ps[:, 6, 0:D], wrow[:, k, :], b2r[:, k, :], start=k == 0, stop=k == TOPK - 1)
                    ins.then_inc(b2_done.sem, 1)
                if 9 <= c <= 12:
                    k, t = divmod(c - 9, TT)
                    if t == 0:
                        pe.wait_ge(w2_in[k].sem, w2_in[k].at(b, 16))
                        pe.wait_ge(gelu_ready.sem, gelu_ready.at(b, 6 + 2 * k))
                    for j in range(FT):
                        ins = mm(ps[:, (7, 5)[k], t * D:(t + 1) * D], hT[:, k, j, t * P:(t + 1) * P], W2s[:, k, j, :],
                                 start=j == 0, stop=j == FT - 1)
                    if t == TT - 1:
                        ins.then_inc(moe_done.sem, 1)
                if c == 17:
                    pe.wait_ge(xn_ready.sem, xn_ready.at(b, 1))
                    transpose_tokens(ps, 6, xn, ident).then_inc(ynT_done.sem, 1)
                if c == 18:
                    pe.wait_ge(ynT_ready.sem, ynT_ready.at(b, 1))
                    for g in range(HT):
                        for d in range(DC):
                            ins = mm(ps[:, 7, g * S:(g + 1) * S], wqT[:, d, g * P:(g + 1) * P], yT[:, d, :],
                                     start=d == 0, stop=d == DC - 1)
                    ins.then_inc(q1_done.sem, 1)
                for t in range(TT):
                    if c in (19 + 5 * t, 20 + 5 * t):
                        layer1_scores(b, HT * t + c - 19 - 5 * t)
                    if c in (21 + 5 * t, 22 + 5 * t):
                        layer1_transpose(b, t, ((0, 1), (2, 3))[c - 21 - 5 * t])
                    if c == 23 + 5 * t:
                        layer1_attend(b, t)
                if c == 29:
                    pe.wait_ge(a1_ready.sem, a1_ready.at(b, TT))
                    transpose_tokens(ps, 5, a1, ident).then_inc(a1T_done.sem, 1)
                if c == 30:
                    pe.wait_ge(a1T_ready.sem, a1T_ready.at(b, 1))
                    for t in range(TT):
                        for d in range(DC):
                            ins = mm(ps[:, 6, t * D:(t + 1) * D], a1T[:, d, t * P:(t + 1) * P], woT[:, d, :],
                                     start=d == 0, stop=d == DC - 1)
                    ins.then_inc(wo1_done.sem, 1)
                if c == 33:
                    pe.wait_ge(qx_ready.sem, qx_ready.at(b, 1))
                    transpose_tokens(psb, 5, qx, identb).then_inc(qxT_done.sem, 1)
                if c in (33, 40):
                    pe.wait_ge(dg_ready.sem, dg_ready.at(b, 1 if c == 33 else 2))
                    for t in range(TT):
                        ins = mm(ps[:, 7, t * P:(t + 1) * P], ones[:, :], dg[:, t, :], start=True, stop=True)
                    ins.then_inc(sB_done.sem, 1)
                if c in (34, 35):
                    if c == 34:
                        pe.wait_ge(qxT_ready.sem, qxT_ready.at(b, 1))
                    for n in (2 * (c - 34), 2 * (c - 34) + 1):
                        if n >= 2:
                            pe.wait_ge(hb_ready.sem, hb_ready.at(b, n - 1))
                        for j in (2 * n, 2 * n + 1):
                            for d in range(DC):
                                ins = mm(ps[:, (6, 5, 7, 6)[n], (j % 2) * S:(j % 2 + 1) * S], f1T[:, d, j * P:(j + 1) * P],
                                         qxT[:, d, :], start=d == 0, stop=d == DC - 1)
                        ins.then_inc(f1_done.sem, 1)
                if c == 39:
                    pe.wait_ge(mj_ready.sem, mj_ready.at(b, 1))
                    for t in range(TT):
                        ins = tr(ps[:, 5, t * P:(t + 1) * P], mj[:, t * P:(t + 1) * P], ident[:, :])
                    ins.then_inc(mjT_done.sem, 1)
                if c == 43:
                    pe.wait_ge(q2_ready.sem, q2_ready.at(b, 4))
                    for t in range(TT):
                        for j in range(FT):
                            ins = mm(ps[:, 5 + t, 0:D], q2[:, j, t * P:(t + 1) * P], f2T[:, j, :], start=j == 0, stop=j == FT - 1)
                        ins.then_inc(f2_done.sem, 1)

            turns(pe, lambda b, front, chain, tail: walk(b, front, chain, tail, front_slot, chain_part))

        @block.scalar
        def _(act):
            fn = act.activation
            act.wait_ge(setup_dve, SETUP_DVE_END)
            act.wait_ge(ld["vec"], 64)

            def q_out(b, p):
                act.wait_ge(q_done.sem, q_done.at(b, p + 1))
                fn(qT[:, p % 2, :], ps[:, BANK_PJ, 0:S], ACT.Copy, scale=DH0 ** -0.5).then_inc(q_ready.sem, 1)

            def v_out(b, k, bank):
                act.wait_ge(v_done.sem, v_done.at(b, 2 * k + 1))
                fn(V[:, k, 0:8, 0:DH0], ps[0:KP, bank, :].rearrange("p (h d) -> p h d", d=DH0), ACT.Copy)\
                    .then_inc(v_act.sem, 1)

            def exps(b, u):
                act.wait_ge(max_ready.sem, max_ready.at(b, u + 1))
                fn(Pr[:, u % 2, :], ps[:, BANK_S[u % 2], 0:KEYS], ACT.Exp, bias=nmax[:, u % 2:u % 2 + 1])\
                    .then_inc(exp_ready.sem, 1)

            def front_slot(b, s, chain):
                u = s - UNIT_AT
                if 0 <= u < UNITS:
                    if u + 1 < UNITS:
                        exps(b, u + 1)
                    chain()
                    act.wait_ge(pt_done.sem, pt_done.at(b, u + 1))
                    fn(PT[:, u % 2, :], ps[0:KP, BANK_PT, 0:KT * P], ACT.Copy).then_inc(pt_ready.sem, 1)
                    if u % 4 == 0 and u // 4 + 1 < PAIRS:
                        q_out(b, u // 4 + 1)
                    return
                chain()
                if s == 1:
                    act.wait_ge(xT_done.sem, xT_done.at(b, 1))
                    for c in range(DC):
                        ins = fn(kvT[:, c, 0:S], ps[:, 0, c * S:(c + 1) * S], ACT.Identity, scale=g2[:, c:c + 1], bias=bb2[:, c:c + 1])
                    ins.then_inc(kvx_ready.sem, 1)
                if s == 2:
                    q_out(b, 0)
                    v_out(b, 0, 2)
                if s == 3:
                    v_out(b, 1, 0)
                if s == 4:
                    v_out(b, 2, 2)
                    exps(b, 0)
                if s in (AFTER, AFTER + 1):
                    g = 2 * (s - AFTER)
                    act.wait_ge(aT_done.sem, aT_done.at(b, g + 1))
                    fn(flat(aT[:, 2 * g:2 * g + 2, :]), ps[:, (0, 1, 2, 4)[g], :], ACT.Copy).then_inc(aT_act.sem, 1)
                if s == AFTER + 5:
                    act.wait_ge(y1T_done.sem, y1T_done.at(b, 1))
                    for c in range(DC):
                        ins = fn(yT[:, c, :], ps[:, 4, c * S:(c + 1) * S], ACT.Copy, accum_out=ysum[:, c:c + 1])
                    ins.then_inc(y1T_ready.sem, 1)
                if s == AFTER + 6:
                    act.wait_ge(logit_ready.sem, logit_ready.at(b, 1))
                    fn(ex[:, :], lg[:, :], ACT.Exp, bias=nlg[:, :], accum_out=exs[:, :]).then_inc(rexp_ready.sem, 1)
                    act.wait_ge(gap_ready.sem, gap_ready.at(b, 1))
                    fn(egap[:, :], gap[:, :], ACT.Exp).then_inc(egap_ready.sem, 1)

            def chain_part(b, c):
                if c == 0:
                    act.wait_ge(b1T_done.sem, b1T_done.at(b, 1))
                    fn(b1T[:, :], ps[:, 7, 0:TOPK * FT], ACT.Copy).then_inc(b1T_ready.sem, 1)
                if c in (2, 4, 6, 8):
                    for i in (c - 2, c - 1):
                        act.wait_ge(h_done.sem, h_done.at(b, i + 1))
                        if i == 0:
                            act.wait_ge(b1T_ready.sem, b1T_ready.at(b, 1))
                        for j in (2 * i, 2 * i + 1):
                            ins = fn(hT[:, j // FT, j % FT, :], ps[:, 5 + i % 3, (j % 2) * S:(j % 2 + 1) * S], ACT.Gelu,
                                     bias=b1T[:, j:j + 1])
                        ins.then_inc(gelu_ready.sem, 1)
                if c == 17:
                    act.wait_ge(ynT_done.sem, ynT_done.at(b, 1))
                    fn(flat(yT[:, :, :]), ps[:, 6, :], ACT.Copy).then_inc(ynT_ready.sem, 1)
                if c == 18:
                    act.wait_ge(q1_done.sem, q1_done.at(b, 1))
                    for g in range(HT):
                        ins = fn(q1T[:, g, :], ps[:, 7, g * S:(g + 1) * S], ACT.Identity, scale=DH1 ** -0.5, bias=bqp[:, g:g + 1])
                    ins.then_inc(q1_ready.sem, 1)
                for t in range(TT):
                    if c == 20 + 5 * t:
                        act.wait_ge(s1_shift.sem, s1_shift.at(b, HT * t + HT))
                        v = P1[:, :, :].rearrange("p h c -> p (h c)")
                        fn(v, v, ACT.Exp).then_inc(e1_ready.sem, 1)
                    if c in (21 + 5 * t, 22 + 5 * t):
                        m = 2 * (c - 21 - 5 * t)
                        act.wait_ge(t1_done.sem, t1_done.at(b, 4 * t + m + 1))
                        fn(PT1[:, 4 * m:4 * m + 4, :].rearrange("p h q -> p (h q)"), ps[0:C, (6, 7, 5, 6)[m], :], ACT.Copy)\
                            .then_inc(t1_act.sem, 1)
                if c == 29:
                    act.wait_ge(a1T_done.sem, a1T_done.at(b, 1))
                    fn(flat(a1T[:, :, :]), ps[:, 5, :], ACT.Copy).then_inc(a1T_ready.sem, 1)
                if c == 33:
                    act.wait_ge(qxT_done.sem, qxT_done.at(b, 1))
                    fn(flat(qxT[:, :, :]), psb[:, 5, 0:DC * S], ACT.Copy).then_inc(qxT_ready.sem, 1)
                if c in (33, 40):
                    act.wait_ge(sB_done.sem, sB_done.at(b, 1 if c == 33 else 2))
                    fn(sB[:, :], ps[:, 7, 0:S], ACT.Copy).then_inc(sB_ready.sem, 1)
                if c in (34, 35):
                    for n in (2 * (c - 34), 2 * (c - 34) + 1):
                        act.wait_ge(hb_ready.sem, hb_ready.at(b, n + 1))
                        for j in (2 * n, 2 * n + 1):
                            ins = fn(cv[:, j, :], hb[:, j, 1:S + 1], ACT.Identity, scale=cw[:, j, 1:2], bias=cb[:, j:j + 1])
                        ins.then_inc(tap_ready.sem, 1)
                if c == 37:
                    for n in range(4):
                        act.wait_ge(conv_ready.sem, conv_ready.at(b, n + 1))
                        v = flat(cv[:, 2 * n:2 * n + 2, :])
                        fn(v, v, ACT.Silu).then_inc(silu_ready.sem, 1)

            turns(act, lambda b, front, chain, tail: walk(b, front, chain, tail, front_slot, chain_part))

        @block.vector
        def _(dve):
            tt, ts, stt, cp, red = (dve.tensor_tensor, dve.tensor_scalar, dve.scalar_tensor_tensor,
                                    dve.tensor_copy, dve.tensor_reduce)
            n_setup = [0]

            def did(ins):
                n_setup[0] += 1
                ins.then_inc(setup_dve, 1)
                dve.wait_ge(setup_dve, n_setup[0])

            dve.wait_ge(ld["ffn"], 32)
            for k, w in enumerate((stg1, stg2)):
                did(red(absum[:, k:k + 1], w, AX.X, ALU.add, apply_absolute_value=True))
            dve.wait_ge(setup_pe, 5)
            did(ts(mw[:, :], ps[:, 7, 0:2], 1.0 / (F * D), 1e-5, ALU.mult, ALU.max))
            did(dve.reciprocal(ws[:, :], mw[:, :]))
            for k, (w, dst) in enumerate(((stg1, stb1), (stg2, stb2))):
                did(ts(w, w, ws[:, k:k + 1], MAGIC, ALU.mult, ALU.add))
                did(ts(w, w, MAGIC, 1.0, ALU.subtract, ALU.min))
                did(ts(dst, w, -1.0, None, ALU.max))
            assert n_setup[0] == SETUP_DVE_Q
            dve.wait_ge(setup_pe, 4)
            dve.wait_ge(consts_made, CONSTS)
            for k, dst in enumerate((wqT, wkT, wvT, woT)):
                for c in range(DC):
                    did(cp(dst[:, c, :].rearrange("p (a n) -> p a n", a=2),
                           ps[:, k, :].rearrange("p (a c n) -> p a c n", a=2, c=DC)[:, :, c, :]))
            dve.wait_ge(ld["bias"], 16 * 9)
            did(ts(bqp[:, :], bqp[:, :], DH1 ** -0.5, None, ALU.mult))
            dve.wait_ge(setup_pe, 6)
            for c in range(DC):
                did(cp(f1T[:, c, :], psb[:, 4 + c, :]))
            for n in range(2):
                did(cp(f2T[:, 4 * n:4 * n + 4, :].rearrange("p a n -> p (a n)"), psb[:, 6 + n, :]))
            assert n_setup[0] == SETUP_DVE_END, n_setup[0]

            links = {}

            def link(chain_of, b, ins):
                links[chain_of] = links.get(chain_of, 0) + 1
                ins.then_inc(chain_of.sem, 1)
                dve.wait_ge(chain_of.sem, chain_of.at(b, links[chain_of]))

            def flink(b, ins):
                link(front_link, b, ins)

            def clink(b, ins):
                link(chain_link, b, ins)

            def stats(order, b, srcs, st, mv):
                for t, src in enumerate(srcs):
                    ins = dve.bn_stats(st[0:src.shape[0], t, :], src)
                order(b, ins)
                dve.nop(nofuse=True)
                for t, src in enumerate(srcs):
                    ins = dve.bn_aggr(mv[0:src.shape[0], t, :], st[0:src.shape[0], t, :])
                order(b, ins)

            def normalise(dst, src, mv, rstd):
                for t in range(TT):
                    ins = ts(dst[:, t, :], src[:, t, :], mv[:, t, 0:1], rstd[:, t:t + 1], ALU.subtract, ALU.mult)
                return ins

            def tiles(a):
                return [a[:, t, :] for t in range(TT)]

            def maxes(b, u):
                dve.wait_ge(score_done.sem, score_done.at(b, u + 1))
                red(nmax[:, u % 2:u % 2 + 1], ps[:, BANK_S[u % 2], 0:KEYS], AX.X, ALU.max, negate=True)\
                    .then_inc(max_ready.sem, 1)

            def k_out(b, p):
                dve.wait_ge(k_done.sem, k_done.at(b, p + 1))
                cp(kT[:, p % 2, :], ps[:, BANK_PJ, 0:KEYS]).then_inc(k_ready.sem, 1)

            def v_out(b, k, bank):
                dve.wait_ge(v_done.sem, v_done.at(b, 2 * k + 2))
                cp(V[:, k, 8:16, 0:DH0], ps[0:KP, bank, :].rearrange("p (h d) -> p h d", d=DH0)).then_inc(v_dve.sem, 1)

            def norm(b, u):
                p, t, h = u // 4, u // 2 % 2, u % 2
                dve.wait_ge(pv_done.sem, pv_done.at(b, u + 1))
                r = rinv[:, u % 2:u % 2 + 1]
                flink(b, dve.reciprocal(r, ps[:, BANK_PV, DH0:DH0 + 1]))
                ts(aN[:, t, (2 * p + h) * DH0:(2 * p + h + 1) * DH0], ps[:, BANK_PV, 0:DH0], r, None, ALU.mult)\
                    .then_inc(norm_ready.sem, 1)

            def front_slot(b, s, chain):
                if s == 0:
                    links[front_link] = 0
                u = s - UNIT_AT
                if 0 <= u < UNITS:
                    if u + 1 < UNITS:
                        maxes(b, u + 1)
                    chain()
                    if u:
                        norm(b, u - 1)
                    if u % 4 == 1 and u // 4 + 1 < PAIRS:
                        k_out(b, u // 4 + 1)
                    return
                if s == 0:
                    dve.wait_ge(x_in.sem, x_in.at(b, 16))
                    dve.wait_ge(c_in.sem, c_in.at(b, 16))
                    stats(flink, b, tiles(xin) + [cin[:, :]], st, mv)
                    ts(var[:, 2:3], mv[:, 2, 1:2], EPS, None, ALU.add)
                    ts(var[:, 0:2], mv[:, 0:2, 1], 1.0 + EPS, EPS * EPS, ALU.mult, ALU.add).then_inc(var_ready.sem, 1)
                if s == 1:
                    dve.wait_ge(rstd_ready.sem, rstd_ready.at(b, 1))
                    normalise(xf, xin, mv, rstd)
                    ts(cn[:, :], cin[:, :], mv[0:C, 2, 0:1], rstd[0:C, 2:3], ALU.subtract, ALU.mult).then_inc(xf_ready.sem, 1)
                chain()
                if s == 1:
                    dve.wait_ge(cT_done.sem, cT_done.at(b, 1))
                    for c in range(DC):
                        ts(kvT[:, c, S:KEYS], ps[:, 1, c * C:(c + 1) * C], g1[:, c:c + 1], bb1[:, c:c + 1], ALU.mult, ALU.add)
                    cp(flat(cT[:, :, :]), ps[:, 1, 2 * C:4 * C]).then_inc(kvc_ready.sem, 1)
                if s == 2:
                    v_out(b, 0, 3)
                if s == 3:
                    v_out(b, 1, 1)
                    k_out(b, 0)
                if s == 4:
                    v_out(b, 2, 3)
                    maxes(b, 0)
                if s == AFTER:
                    norm(b, UNITS - 1)
                if s in (AFTER, AFTER + 1):
                    g = 2 * (s - AFTER) + 1
                    dve.wait_ge(aT_done.sem, aT_done.at(b, g + 1))
                    cp(flat(aT[:, 2 * g:2 * g + 2, :]), ps[:, (0, 1, 2, 4)[g], :]).then_inc(aT_dve.sem, 1)
                if s == AFTER + 2:
                    dve.wait_ge(wo_done.sem, wo_done.at(b, 1))
                    tt(x1[:, 0, :], ps[:, 3, 0:D], xin[:, 0, :], ALU.add).then_inc(x1_ready.sem, 1)
                    dve.wait_ge(k1_done.sem, k1_done.at(b, 1))
                    for g in range(HT):
                        ins = ts(k1[:, g, :], ps[:, 1, g * C:(g + 1) * C], bkp[:, g:g + 1], None, ALU.add)
                    flink(b, ins)
                    for g in range(HT):
                        tt(k1d[:, g, :, :], k1[:, g, :].unsqueeze(1).to_broadcast([P, HH, C]),
                           own[:, :].unsqueeze(2).to_broadcast([P, HH, C]), ALU.mult)
                    dve.wait_ge(v1_done.sem, v1_done.at(b, 1))
                    tt(v1[:, :, 0:DH1], ps[0:C, 2, 0:D].rearrange("p (h d) -> p h d", h=H1),
                       bvB[0:C, :].rearrange("p (h d) -> p h d", h=H1), ALU.add).then_inc(k1v1_ready.sem, 1)
                if s == AFTER + 3:
                    dve.wait_ge(wo_done.sem, wo_done.at(b, 2))
                    tt(x1[:, 1, :], ps[:, 0, 0:D], xin[:, 1, :], ALU.add).then_inc(x1_ready.sem, 1)
                if s == AFTER + 4:
                    dve.wait_ge(x1_ready.sem, x1_ready.at(b, TT))
                    stats(flink, b, tiles(x1), st, mv)
                    ts(var[:, 0:2], mv[:, 0:2, 1], EPS, None, ALU.add).then_inc(var_ready.sem, 1)
                if s == AFTER + 5:
                    dve.wait_ge(rstd_ready.sem, rstd_ready.at(b, 2))
                    normalise(y1, x1, mv, rstd).then_inc(y1_ready.sem, 1)
                if s == AFTER + 6:
                    dve.wait_ge(logit_done.sem, logit_done.at(b, 1))
                    flink(b, stt(lg[:, :], ps[0:1, 0, 0:E], 1.0 / S, brow[:, :], ALU.mult, ALU.add))
                    red(nlg[:, :], lg[:, :], AX.X, ALU.max, negate=True).then_inc(logit_ready.sem, 1)
                    dve.wait_ge(rexp_ready.sem, rexp_ready.at(b, 1))
                    flink(b, dve.reciprocal(rex[:, :], exs[:, :]))
                    flink(b, ts(rw[:, :], ex[:, :], rex[:, 0:1], None, ALU.mult))
                    dve.nop(nofuse=True)
                    flink(b, dve.max(top[:, :], rw[:, :]))
                    dve.nop(nofuse=True)
                    dve.max_index(idx[:, :], top[:, :], rw[:, :]).then_inc(idx_ready.sem, 1)
                    tt(gap[:, :], top[:, 1:2], top[:, 0:1], ALU.subtract).then_inc(gap_ready.sem, 1)
                    dve.wait_ge(egap_ready.sem, egap_ready.at(b, 1))
                    flink(b, ts(wden[:, :], egap[:, :], 1.0, None, ALU.add))
                    flink(b, dve.reciprocal(wtop[:, 0:1], wden[:, :]))
                    tt(wtop[:, 1:2], egap[:, :], wtop[:, 0:1], ALU.mult).then_inc(wtop_ready.sem, 1)
                if s == AFTER + 7:
                    dve.wait_ge(wtop_ready.sem, wtop_ready.at(b, 1))
                    for k in range(TOPK):
                        ts(wrow[:, k, :], ones[0:1, :], wtop[:, k:k + 1], None, ALU.mult)
                    dve.wait_ge(wB_done.sem, wB_done.at(b, 1))
                    cp(wB[:, :], ps[:, 1, 0:2]).then_inc(wB_ready.sem, 1)

            def chain_part(b, c):
                if c == 0:
                    links[chain_link] = 0
                if c == SLOTS - CHAIN_AT:
                    links[chain_link] = TURN_LINKS
                if c == 11:
                    if not first(b):
                        dve.wait_ge(out_done.sem, out_done.at(b, 0))
                    dve.wait_ge(b2_done.sem, b2_done.at(b, 1))
                    for t in range(TT):
                        ins = tt(y2[:, t, :], ps[:, 6, 0:D], y1[:, t, :], ALU.add)
                    clink(b, ins)
                if c in (12, 13):
                    k = c - 12
                    dve.wait_ge(moe_done.sem, moe_done.at(b, k + 1))
                    dve.wait_ge(wB_ready.sem, wB_ready.at(b, 1))
                    for t in range(TT):
                        ins = stt(y2[:, t, :], ps[:, (7, 5)[k], t * D:(t + 1) * D], wB[:, k:k + 1], y2[:, t, :], ALU.mult, ALU.add)
                    clink(b, ins)
                if c == 13:
                    stats(clink, b, tiles(y2), st2, mv2)
                    ts(var2[:, :], mv2[:, :, 1], EPS, None, ALU.add).then_inc(var2_ready.sem, 1)
                if c == 14:
                    dve.wait_ge(rstd2_ready.sem, rstd2_ready.at(b, 1))
                    clink(b, normalise(y2, y2, mv2, rstd2))
                    for t in range(TT):
                        ins = tt(y2[:, t, :], y2[:, t, :], gammaB[:, :], ALU.mult)
                    clink(b, ins)
                    dve.wait_ge(x1b_ready.sem, x1b_ready.at(b, 1))
                    for t in range(TT):
                        ins = tt(x2[:, t, :], y2[:, t, :], x1[:, t, :], ALU.add)
                    clink(b, ins)
                if c == 15:
                    stats(clink, b, tiles(x2), st2, mv2)
                    ts(var2[:, :], mv2[:, :, 1], EPS, None, ALU.add).then_inc(var2_ready.sem, 1)
                if c == 16:
                    dve.wait_ge(rstd2_ready.sem, rstd2_ready.at(b, 2))
                    normalise(xn, x2, mv2, rstd2).then_inc(xn_ready.sem, 1)
                for t in range(TT):
                    if c in (19 + 5 * t, 20 + 5 * t):
                        g = c - 19 - 5 * t
                        dve.wait_ge(s1_done.sem, s1_done.at(b, HT * t + g + 1))
                        for m in range(2):
                            v = ps[:, ((5, 6), (7, 5))[g][m], 0:4 * C].rearrange("p (h c) -> p h c", h=4)
                            ins = red(nmax1[:, 4 * m:4 * m + 4], v, AX.X, ALU.max, negate=True)
                        clink(b, ins)
                        for m in range(2):
                            v = ps[:, ((5, 6), (7, 5))[g][m], 0:4 * C].rearrange("p (h c) -> p h c", h=4)
                            h = HH * g + 4 * m
                            ins = tt(P1[:, h:h + 4, :], v, nmax1[:, 4 * m:4 * m + 4].unsqueeze(2).to_broadcast([P, 4, C]), ALU.add)
                        ins.then_inc(s1_shift.sem, 1)
                    if c in (21 + 5 * t, 22 + 5 * t):
                        m = 2 * (c - 21 - 5 * t) + 1
                        dve.wait_ge(t1_done.sem, t1_done.at(b, 4 * t + m + 1))
                        cp(PT1[:, 4 * m:4 * m + 4, :].rearrange("p h q -> p (h q)"), ps[0:C, (6, 7, 5, 6)[m], :])\
                            .then_inc(t1_dve.sem, 1)
                    if c == 23 + 5 * t:
                        dve.wait_ge(pv1_done.sem, pv1_done.at(b, t + 1))
                        o = ps[:, 7, 0:H1 * (DH1 + 1)].rearrange("p (h d) -> p h d", h=H1)
                        clink(b, dve.reciprocal(rinv1[:, :], o[:, :, DH1]))
                        tt(a1[:, t, :].rearrange("p (h d) -> p h d", h=H1), o[:, :, 0:DH1],
                           rinv1[:, :].unsqueeze(2).to_broadcast([P, H1, DH1]), ALU.mult).then_inc(a1_ready.sem, 1)
                if c == 30:
                    dve.wait_ge(wo1_done.sem, wo1_done.at(b, 1))
                    dve.wait_ge(x2b_ready.sem, x2b_ready.at(b, 1))
                    clink(b, tt(x3[:, :, :], ps[:, 6, :].rearrange("p (t d) -> p t d", t=TT), x2[:, :, :], ALU.add))
                    stats(clink, b, tiles(x3), st2, mv2)
                    ts(var2[:, :], mv2[:, :, 1], EPS, None, ALU.add).then_inc(var2_ready.sem, 1)
                if c == 31:
                    dve.wait_ge(rstd2_ready.sem, rstd2_ready.at(b, 3))
                    clink(b, normalise(xn, x3, mv2, rstd2))
                    clink(b, red(am[:, :], xn[:, :, :], AX.X, ALU.max, apply_absolute_value=True))
                    clink(b, ts(am[:, :], am[:, :], 1e-5, 1.0 / 127.0, ALU.max, ALU.mult))
                    clink(b, dve.reciprocal(sc[:, :], am[:, :]))
                    for t in range(TT):
                        ins = ts(y2[:, t, :], xn[:, t, :], sc[:, t:t + 1], MAGIC, ALU.mult, ALU.add)
                    clink(b, ins)
                    ts(qx[:, :, :], y2[:, :, :], MAGIC, 127.0, ALU.subtract, ALU.min).then_inc(qx_ready.sem, 1)
                if c == 32:
                    for t in range(TT):
                        ins = ts(dg[:, t, :], ident[:, :], am[:, t:t + 1], mw[:, 0:1], ALU.mult, ALU.mult)
                    ins.then_inc(dg_ready.sem, 1)
                if c in (34, 35):
                    dve.wait_ge(sB_ready.sem, sB_ready.at(b, 1))
                    for n in (2 * (c - 34), 2 * (c - 34) + 1):
                        dve.wait_ge(f1_done.sem, f1_done.at(b, n + 1))
                        tt(hb[:, 2 * n:2 * n + 2, 1:S + 1], ps[:, (6, 5, 7, 6)[n], :].rearrange("p (a q) -> p a q", a=2),
                           sB[:, :].unsqueeze(1).to_broadcast([P, 2, S]), ALU.mult).then_inc(hb_ready.sem, 1)
                if c in (35, 36):
                    for n in (2 * (c - 35), 2 * (c - 35) + 1):
                        dve.wait_ge(tap_ready.sem, tap_ready.at(b, n + 1))
                        for j in (2 * n, 2 * n + 1):
                            ins = stt(cv[:, j, :], hb[:, j, 0:S], cw[:, j, 0:1], cv[:, j, :], ALU.mult, ALU.add)
                        clink(b, ins)
                        for j in (2 * n, 2 * n + 1):
                            ins = stt(cv[:, j, :], hb[:, j, 2:S + 2], cw[:, j, 2:3], cv[:, j, :], ALU.mult, ALU.add)
                        ins.then_inc(conv_ready.sem, 1)
                if c == 38:
                    dve.wait_ge(silu_ready.sem, silu_ready.at(b, 4))
                    red(mj[:, :], cv[:, :, :].rearrange("p j q -> p q j"), AX.X, ALU.max, apply_absolute_value=True)\
                        .then_inc(mj_ready.sem, 1)
                if c == 39:
                    dve.wait_ge(mjT_done.sem, mjT_done.at(b, 1))
                    clink(b, red(am2[:, :], ps[:, 5, 0:S].rearrange("p (t q) -> p t q", t=TT), AX.X, ALU.max))
                    clink(b, ts(am2[:, :], am2[:, :], 1e-5, 1.0 / 127.0, ALU.max, ALU.mult))
                    clink(b, dve.reciprocal(sc[:, :], am2[:, :]))
                    for t in range(TT):
                        ins = ts(dg[:, t, :], ident[:, :], sc[:, t:t + 1], None, ALU.mult)
                    ins.then_inc(dg_ready.sem, 1)
                    ts(inv2[:, :], am2[:, :], mw[:, 1:2], None, ALU.mult)
                if c in (41, 42):
                    dve.wait_ge(sB_ready.sem, sB_ready.at(b, 2))
                    for n in (2 * (c - 41), 2 * (c - 41) + 1):
                        v = cv[:, 2 * n:2 * n + 2, :]
                        clink(b, tt(v, v, sB[:, :].unsqueeze(1).to_broadcast([P, 2, S]), ALU.mult))
                        ts(q2[:, 2 * n:2 * n + 2, :], v, MAGIC, MAGIC, ALU.add, ALU.subtract).then_inc(q2_ready.sem, 1)
                if c == 43:
                    for t in range(TT):
                        dve.wait_ge(f2_done.sem, f2_done.at(b, t + 1))
                        ins = stt(x4[:, t, :], ps[:, 5 + t, 0:D], inv2[:, t:t + 1], x3[:, t, :], ALU.mult, ALU.add)
                    ins.then_inc(x4_ready.sem, 1)

            def turn(b, front, chain, tail):
                walk(b, front, chain, tail, front_slot, chain_part)
                assert not front or links[front_link] == FRONT_LINKS, links
                assert not chain or links[chain_link] == TURN_LINKS, links
                assert chain or not tail or links[chain_link] == CHAIN_LINKS, links

            turns(dve, turn)


CONSTS = 10
SETUP_DVE_Q = 10
SETUP_DVE_END = SETUP_DVE_Q + 8 + 1 + 4

_INS = ['x', 'ctx_1024', 'L0_xattn_ln1_g', 'L0_xattn_ln1_b', 'L0_xattn_ln2_g', 'L0_xattn_ln2_b', 'L0_xattn_Wq',
        'L0_xattn_Wkv', 'L0_xattn_Wo', 'L0_ffn_W1', 'L0_ffn_b1', 'L0_ffn_W2', 'L0_ffn_b2', 'L0_ffn_Wr', 'L0_ffn_br',
        'L0_ffn_gamma', 'L0_ffn_beta', 'L1_xattn_wq', 'L1_xattn_bq', 'L1_xattn_wk', 'L1_xattn_bk', 'L1_xattn_wv',
        'L1_xattn_bv', 'L1_xattn_wo', 'L1_xattn_bo', 'L1_ffn_w1', 'L1_ffn_conv_w', 'L1_ffn_conv_b', 'L1_ffn_w2']
_OUTS = [((B, S, D), 'float32')]


def kernel(**inputs):
    import numpy as _np
    import concourse.bacc as _bacc
    from concourse import mybir as _mybir
    from concourse.bass_utils import run_bass_kernel_spmd as _run

    nc = _bacc.Bacc("TRN2", target_bir_lowering=False, num_devices=1)
    arrays, args = {}, []
    for name in _INS:
        a = _np.ascontiguousarray(inputs[name])
        arrays[f"in_{name}_dram"] = a
        args.append(nc.dram_tensor(f"in_{name}_dram", a.shape, _mybir.dt.from_np(a.dtype), kind="ExternalInput").ap())
    for i, (shape, dtype) in enumerate(_OUTS):
        dt = _mybir.dt.from_np(_np.dtype(dtype))
        args.append(nc.dram_tensor(f"out_{i}_dram", shape, dt, kind="ExternalOutput").ap())
    build(nc, *args)
    r = _run(nc, [arrays], core_ids=[0])
    return r.results[0]["out_0_dram"]
```

```python
from contextlib import ExitStack

import concourse.bass as bass
from concourse import mybir

F32 = mybir.dt.float32
BF16 = mybir.dt.bfloat16
U32 = mybir.dt.uint32
ALU = mybir.AluOpType
ACT = mybir.ActivationFunctionType
AX = mybir.AxisListType

P = 128
B, S, D = 16, 256, 256
C = 77
DC = D // P
TT = S // P
H0, DH0 = 16, 64
INNER = H0 * DH0
PAIRS = H0 // 2
UNITS = H0 * TT
KEYS = S + C
KT = 3
KP = KEYS // KT
E, F, TOPK = 8, 1024, 2
FT = F // P
H1, DH1 = 16, 16
HT = D // P
HH = H1 // HT
EPS = 1e-5
MAGIC = 1.5 * 2.0 ** 23

SLOTS = UNITS + 4
CHAIN_AT = 10
PARTS = 46
PAIRED = (1, 2, 4, 6, 8, 10, 11, 12, 13, 17, 33)
SILU_PART = 39
START = [CHAIN_AT + c - sum(c >= q for q in PAIRED) + (c > SILU_PART) for c in range(PARTS)]
assert START[-1] < SLOTS + CHAIN_AT
TAIL = min(c for c in range(PARTS) if START[c] >= SLOTS)
BANK_S, BANK_PT, BANK_PV, BANK_PJ = (0, 1), 2, 3, 4
HIGH_VALUES_AT = (3, 6, 10)
Y1T_AT = 4
NEXT_XT_AT, NEXT_CT_AT = 14, 18
NEXT_VALUES_AT = (22, 26, 30)
NEXT_Q_AT, NEXT_K_AT = 28, 29
NEXT_STATS_AT, NEXT_NORM_AT = 9, 11
LOGITS_AT = 5
LONG_PARTS_AT = (31,)

NORM_LINKS = 2
ROUTER_LINKS = 8
CHAIN_LINKS = 33
TURN_LINKS = 24


class Signal:

    def __init__(self, sem, per):
        self.sem, self.per = sem, per

    def at(self, b, n):
        return b * self.per + n


def first(b):
    return isinstance(b, int) and b == 0


def turns(eng, turn):
    turn(0, front=True, chain=False, tail=False, ahead=True)
    turn(1, front=True, chain=True, tail=False, ahead=True)
    with eng.Fori(2, B - 1) as b:
        turn(b, front=True, chain=True, tail=True, ahead=True)
    turn(B - 1, front=True, chain=True, tail=True, ahead=False)
    turn(B, front=False, chain=True, tail=True, ahead=False)
    turn(B + 1, front=False, chain=False, tail=True, ahead=False)


def build(nc, x, ctx_in, ln1_g, ln1_b, ln2_g, ln2_b, Wq, Wkv, Wo, W1, b1, W2, b2, Wr, br, gamma, beta,
          wq, bq, wk, bk, wv, bv, wo, bo, fw1, conv_w, conv_b, fw2, out):
    assert KT * KP == KEYS and KP <= P
    with ExitStack() as stack:
        def sb(name, shape, dt=F32):
            return stack.enter_context(nc.sbuf_tensor(name, shape, dt))

        def sem(name):
            return stack.enter_context(nc.semaphore(name))

        def signal(name, per):
            return Signal(sem(name), per)

        wq0 = sb("wq0", [P, DC, INNER])
        wkv0 = sb("wkv0", [P, DC, 2 * INNER])
        wo0 = sb("wo0", [P, PAIRS, D])
        wr = sb("wr", [P, DC, E])
        brow = sb("brow", [1, E])
        g1 = sb("g1", [P, DC]); bb1 = sb("bb1", [P, DC])
        g2 = sb("g2", [P, DC]); bb2 = sb("bb2", [P, DC])
        gammaB = sb("gammaB", [P, D]); betaB = sb("betaB", [P, D])
        boB = sb("boB", [P, D]); bvB = sb("bvB", [P, D])
        bqp = sb("bqp", [P, HT]); bkp = sb("bkp", [P, HT])
        wqT = sb("wqT", [P, DC, D]); wkT = sb("wkT", [P, DC, D])
        wvT = sb("wvT", [P, DC, D]); woT = sb("woT", [P, DC, D])
        f1T = sb("f1T", [P, DC, F], BF16)
        f2T = sb("f2T", [P, FT, D], BF16)
        cw = sb("cw", [P, FT, 3]); cb = sb("cb", [P, FT])
        mw = sb("mw", [P, 2]); ws = sb("ws", [P, 2]); absum = sb("absum", [P, 2])
        ident = sb("ident", [P, P]); identb = sb("identb", [P, P], BF16)
        ones = sb("ones", [P, P])
        own = sb("own", [P, HH])
        mhalf = sb("mhalf", [P, 3])
        xin = sb("xin", [P, TT, D]); xres = sb("xres", [P, TT, D]); cin = sb("cin", [C, D])
        xf = sb("xf", [P, TT, D]); cn = sb("cn", [C, D])
        st = sb("st", [P, 3, 6]); mv = sb("mv", [P, 3, 2]); var = sb("var", [P, 3]); rstd = sb("rstd", [P, 3])
        kvT = sb("kvT", [P, DC, KEYS]); cT = sb("cT", [P, DC, C])
        kvTn = sb("kvTn", [P, DC, KEYS]); cTn = sb("cTn", [P, DC, C])
        lgr = sb("lgr", [1, E])
        qT = sb("qT", [P, 2, S]); kT = sb("kT", [P, 2, KEYS])
        V = sb("V", [KP, KT, H0, DH0 + 1])
        nmax = sb("nmax", [P, 2])
        Pr = sb("Pr", [P, 2, KEYS])
        PT = sb("PT", [KP, 2, KT * P])
        aU = sb("aU", [P, 2, TT, 2, DH0 + 1]); rinv = sb("rinv", [P, 2, TT, 2]); aN = sb("aN", [P, 2, TT, P])
        aT = sb("aT", [P, PAIRS, S])
        lg = sb("lg", [1, E]); nlg = sb("nlg", [1, 1]); ex = sb("ex", [1, E]); exs = sb("exs", [1, 1])
        rex = sb("rex", [1, 1]); rw = sb("rw", [1, E]); top = sb("top", [1, 8]); idx = sb("idx", [1, 8], U32)
        gap = sb("gap", [1, 1]); egap = sb("egap", [1, 1]); wden = sb("wden", [1, 1]); wtop = sb("wtop", [1, 2])
        ysum = sb("ysum", [P, DC])
        sty = sb("sty", [P, TT, 6]); mvy = sb("mvy", [P, TT, 2]); vary = sb("vary", [P, TT]); rstdy = sb("rstdy", [P, TT])
        x1 = sb("x1", [P, TT, D]); y1 = sb("y1", [P, TT, D]); yT = sb("yT", [P, DC, S])
        wrow = sb("wrow", [1, 2, P]); wB = sb("wB", [P, 2])
        W1s = sb("W1s", [P, TOPK, DC, F]); W2s = sb("W2s", [P, TOPK, FT, D])
        b1r = sb("b1r", [FT, TOPK, P]); b2r = sb("b2r", [1, TOPK, D])
        k1 = sb("k1", [P, HT, C])
        k1d = sb("k1d", [P, HT, HH, C])
        v1 = sb("v1", [C, H1, DH1 + 1])
        b1T = sb("b1T", [P, TOPK * FT])
        hT = sb("hT", [P, TOPK, FT, S])
        y2 = sb("y2", [P, TT, D]); x2 = sb("x2", [P, TT, D]); x3 = sb("x3", [P, TT, D]); xn = sb("xn", [P, TT, D])
        st2 = sb("st2", [P, TT, 6]); mv2 = sb("mv2", [P, TT, 2]); var2 = sb("var2", [P, TT]); rstd2 = sb("rstd2", [P, TT])
        q1T = sb("q1T", [P, HT, S])
        nmax1 = sb("nmax1", [P, HH]); P1 = sb("P1", [P, H1, C])
        rinv1 = sb("rinv1", [P, H1]); a1 = sb("a1", [P, TT, D])
        am = sb("am", [P, TT]); sc = sb("sc", [P, TT])
        qx = sb("qx", [P, TT, D], BF16); qxT = sb("qxT", [P, DC, S], BF16)
        dg = sb("dg", [P, TT, P]); sB = sb("sB", [P, S])
        hb = sb("hb", [P, FT, S + 2])
        mj = sb("mj", [P, S])
        q2 = sb("q2", [P, FT, S], BF16)
        am2 = sb("am2", [P, TT]); inv2 = sb("inv2", [P, TT])
        PT1 = hT[0:C, 1, :, :].rearrange("p a q -> p (a q)").rearrange("p (h q) -> p h q", h=H1)
        cv = hT[:, 0, :, :]
        a1T = yT
        x4 = y2
        tap = (a1, q1T)
        stg1 = W1s[:, 0, :, :].rearrange("p a n -> p (a n)")
        stg2 = W1s[:, 1, :, :].rearrange("p a n -> p (a n)")
        stgq = hT[:, 0, :, :].rearrange("p a n -> p (a n)")
        stb1 = q2[:, :, :].rearrange("p a n -> p (a n)")
        stb2 = hT[:, 1, :, :].rearrange("p a n -> p (a n)").bitcast(BF16)[:, 0:FT * D]

        ps = stack.enter_context(nc.psum_tensor("ps", [P, 8, 512], F32))
        psb = ps[:, :, :].rearrange("p a n -> p (a n)").bitcast(BF16).rearrange("p (a n) -> p a n", a=8)

        ld = {n: sem(f"ld_{n}") for n in ("vec", "w0", "out", "l1", "ffn", "bias")}
        ident_made = sem("ident_made"); consts_made = sem("consts_made")
        setup_pe = sem("setup_pe"); setup_dve = sem("setup_dve")
        x_in = signal("x_in", 16); c_in = signal("c_in", 16); out_done = signal("out_done", 16)
        xvar_ready = signal("xvar_ready", 1); xrstd_ready = signal("xrstd_ready", 1); xres_ready = signal("xres_ready", 1)
        yvar_ready = signal("yvar_ready", 1); yrstd_ready = signal("yrstd_ready", 1)
        xf_ready = signal("xf_ready", 1); xT_done = signal("xT_done", 1); cT_done = signal("cT_done", 1)
        kvx_ready = signal("kvx_ready", 1); kvc_ready = signal("kvc_ready", 1)
        kvT_ready = signal("kvT_ready", 1); cT_ready = signal("cT_ready", 1); k1d_ready = signal("k1d_ready", 1)
        v_done = signal("v_done", 2 * KT); v_ready = signal("v_ready", 2 * KT)
        q_done = signal("q_done", PAIRS); q_ready = signal("q_ready", PAIRS)
        k_done = signal("k_done", PAIRS); k_ready = signal("k_ready", PAIRS)
        score_done = signal("score_done", UNITS); max_ready = signal("max_ready", UNITS)
        exp_ready = signal("exp_ready", UNITS); pt_done = signal("pt_done", UNITS); pt_ready = signal("pt_ready", UNITS)
        pv_done = signal("pv_done", UNITS); norm_ready = signal("norm_ready", UNITS)
        rinv_ready = signal("rinv_ready", PAIRS); aN_ready = signal("aN_ready", PAIRS)
        aT_done = signal("aT_done", PAIRS); aT_ready = signal("aT_ready", PAIRS)
        wo_done = signal("wo_done", TT); x1_ready = signal("x1_ready", TT)
        kv1_done = signal("kv1_done", 1); k1v1_ready = signal("k1v1_ready", 1)
        y1_ready = signal("y1_ready", 1); y1T_done = signal("y1T_done", 1); y1T_ready = signal("y1T_ready", 1)
        logit_done = signal("logit_done", 1); lgr_ready = signal("lgr_ready", 1); logit_ready = signal("logit_ready", 1)
        rexp_ready = signal("rexp_ready", 1); idx_ready = signal("idx_ready", 1)
        gap_ready = signal("gap_ready", 1); egap_ready = signal("egap_ready", 1)
        wtop_ready = signal("wtop_ready", 1); wB_done = signal("wB_done", 1); wB_ready = signal("wB_ready", 1)
        w1_in = [signal(f"w1_in{e}", 16) for e in range(TOPK)]
        w2_in = [signal(f"w2_in{e}", 16) for e in range(TOPK)]
        b_in = signal("b_in", 16 * 2 * TOPK)
        x1b_ready = signal("x1b_ready", 1)
        b1T_done = signal("b1T_done", 1); b1T_ready = signal("b1T_ready", 1)
        h_done = signal("h_done", TOPK * FT // 2); gelu_ready = signal("gelu_ready", TOPK * FT // 2)
        moe_done = signal("moe_done", TOPK); b2_done = signal("b2_done", 1)
        var2_ready = signal("var2_ready", 3); rstd2_ready = signal("rstd2_ready", 3)
        xn_ready = signal("xn_ready", 1); x2b_ready = signal("x2b_ready", 1)
        ynT_done = signal("ynT_done", 1); ynT_ready = signal("ynT_ready", 1)
        q1_done = signal("q1_done", 1); q1_ready = signal("q1_ready", 1)
        s1_done = signal("s1_done", TT * HT); s1_shift = signal("s1_shift", TT * HT); e1_ready = signal("e1_ready", TT * HT)
        t1_done = signal("t1_done", TT * 4); t1_act = signal("t1_act", TT * 2); t1_dve = signal("t1_dve", TT * 2)
        pv1_done = signal("pv1_done", TT); a1_ready = signal("a1_ready", TT)
        a1T_done = signal("a1T_done", 1); a1T_ready = signal("a1T_ready", 1); wo1_done = signal("wo1_done", 1)
        qx_ready = signal("qx_ready", 1); dg_ready = signal("dg_ready", 2)
        qxT_done = signal("qxT_done", 1); qxT_ready = signal("qxT_ready", 1)
        sB_done = signal("sB_done", 2); sB_ready = signal("sB_ready", 2)
        f1_done = signal("f1_done", 4); hb_ready = signal("hb_ready", 4); tap_ready = signal("tap_ready", 4)
        conv_dve = signal("conv_dve", 3); conv_pool = signal("conv_pool", 1); silu_ready = signal("silu_ready", 4)
        mj_ready = signal("mj_ready", 1); mjT_done = signal("mjT_done", 1)
        q2_ready = signal("q2_ready", 4); f2_done = signal("f2_done", TT); x4_ready = signal("x4_ready", 1)
        pool_link = signal("pool_link", 2); norm_link = signal("norm_link", NORM_LINKS);
        router_link = signal("router_link", ROUTER_LINKS); chain_link = signal("chain_link", CHAIN_LINKS)

        block = stack.enter_context(nc.Block())

        def row(v):
            return v.rearrange("(a n) -> a n", a=1)

        def flat(v):
            return v.rearrange("p a n -> p (a n)")

        def walk(b, front, chain, tail, ahead, slot, chain_part, setup=None):
            for s in range(SLOTS):
                def part(s=s):
                    if setup and not chain and not tail:
                        setup(s)
                    for c in range(PARTS):
                        if chain and START[c] == s:
                            chain_part(b - 1, c)
                        if tail and START[c] == s + SLOTS:
                            chain_part(b - 2, c)

                slot(b, s, front, chain, tail, ahead, part)

        @block.sync
        def _(sp):
            def load_x(b):
                sp.dma_start(xin[:, :, :], x[b].rearrange("(t p) d -> p t d", p=P)).then_inc(x_in.sem, 16)
                sp.dma_start(cin[:, :], ctx_in[b]).then_inc(c_in.sem, 16)

            load_x(0)
            with nc.allow_non_contiguous_dma(reason="small vectors laid out one feature per partition"):
                for dst, src in ((g1, ln1_g), (bb1, ln1_b), (g2, ln2_g), (bb2, ln2_b)):
                    sp.dma_start(dst[:, :], src.rearrange("(c p) -> p c", p=P)).then_inc(ld["vec"], 16)
                sp.dma_start(wkv0[:, :, :], Wkv.rearrange("(c p) n -> p c n", p=P)).then_inc(ld["w0"], 16)
                sp.dma_start(wq0[:, :, :], Wq.rearrange("(c p) n -> p c n", p=P)).then_inc(ld["w0"], 16)
                for k, w in enumerate((wq, wk, wv, wo)):
                    sp.dma_start(stgq[:, k * 512:(k + 1) * 512], w.rearrange("(a p) n -> p a n", p=P))\
                      .then_inc(ld["l1"], 16)
                sp.dma_start(stg1, fw1.rearrange("(a p) n -> p a n", p=P)).then_inc(ld["ffn"], 16)
                sp.dma_start(stg2, fw2.rearrange("(a p) n -> p a n", p=P)).then_inc(ld["ffn"], 16)
                sp.dma_start(wo0[:, :, :], Wo.rearrange("(j p) n -> p j n", p=P)).then_inc(ld["out"], 16)
                sp.dma_start(wr[:, :, :], Wr.rearrange("(c p) n -> p c n", p=P)).then_inc(ld["out"], 16)
                sp.dma_start(brow[:, :], row(br)).then_inc(ld["bias"], 16)
                sp.dma_start(cw[:, :, :], conv_w.rearrange("(j p) a k -> p j (a k)", p=P)).then_inc(ld["bias"], 16)
                sp.dma_start(cb[:, :], conv_b.rearrange("(j p) -> p j", p=P)).then_inc(ld["bias"], 16)
                for dst, src in ((gammaB, gamma), (betaB, beta), (boB, bo), (bvB, bv)):
                    sp.dma_start(dst[:, :], row(src).to_broadcast([P, D])).then_inc(ld["bias"], 16)
                for dst, src in ((bqp, bq), (bkp, bk)):
                    sp.dma_start(dst[:, :], src.rearrange("(t p) -> p t", p=P)).then_inc(ld["bias"], 16)

            def turn(b, front, chain, tail, ahead):
                if ahead:
                    sp.wait_ge(xres_ready.sem, xres_ready.at(b, 1))
                    sp.nop(nofuse=True)
                    sp.wait_ge(cT_done.sem, cT_done.at(b, 1))
                    sp.nop(nofuse=True)
                    load_x(b + 1)
                if chain and first(b - 1):
                    sp.wait_ge(setup_dve, SETUP_DVE_END)
                if chain:
                    sp.wait_ge(idx_ready.sem, idx_ready.at(b - 1, 1))
                    sp.nop(nofuse=True)
                    for k in range(TOPK):
                        e = sp.value_load(idx[0:1, k:k + 1], min_val=0, max_val=E - 1)
                        sp.dma_start(b1r[:, k, :], b1[e].rearrange("(j p) -> j p", p=P)).then_inc(b_in.sem, 16)
                        sp.dma_start(b2r[:, k, :], row(b2[e])).then_inc(b_in.sem, 16)
                        sp.dma_start(W1s[:, k, :, :], W1[e].rearrange("(c p) n -> p c n", p=P)).then_inc(w1_in[k].sem, 16)
                        sp.dma_start(W2s[:, k, :, :], W2[e].rearrange("(j p) n -> p j n", p=P)).then_inc(w2_in[k].sem, 16)
                if tail:
                    sp.wait_ge(x4_ready.sem, x4_ready.at(b - 2, 1))
                    sp.nop(nofuse=True)
                    sp.dma_start(out[b - 2].rearrange("(t p) d -> p t d", p=P), x4[:, :, :]).then_inc(out_done.sem, 16)

            turns(sp, turn)
            sp.wait_ge(out_done.sem, 16 * B)

        @block.gpsimd
        def _(pool):
            pool.memset(ident[:, :], 0.0).then_inc(ident_made, 1)
            pool.memset(identb[:, :], 0.0).then_inc(ident_made, 1)
            pool.memset(ones[:, :], 1.0).then_inc(consts_made, 1)
            pool.memset(mhalf[:, :], -0.5).then_inc(consts_made, 1)
            pool.memset(own[:, :], 1.0).then_inc(consts_made, 1)
            pool.wait_ge(ident_made, 2)
            for m in (ident, identb):
                pool.affine_select(out=m[:, :], in_=m[:, :], compare_op=ALU.not_equal, fill=1.0,
                                   base=0, pattern=[[-1, P]], channel_multiplier=1).then_inc(ident_made, 1)
            pool.wait_ge(consts_made, 3)
            pool.affine_select(out=own[:, :], in_=own[:, :], compare_op=ALU.is_ge, fill=0.0,
                               base=0, pattern=[[-DH1, HH]], channel_multiplier=1).then_inc(consts_made, 1)
            pool.wait_ge(consts_made, 4)
            pool.affine_select(out=own[:, :], in_=own[:, :], compare_op=ALU.is_ge, fill=0.0,
                               base=DH1 - 1, pattern=[[DH1, HH]], channel_multiplier=-1).then_inc(consts_made, 1)
            pool.memset(V[:, :, :, DH0:DH0 + 1], 1.0).then_inc(consts_made, 1)
            pool.memset(v1[:, :, DH1:DH1 + 1], 1.0).then_inc(consts_made, 1)
            pool.memset(hb[:, :, 0:1], 0.0).then_inc(consts_made, 1)
            pool.memset(hb[:, :, S + 1:S + 2], 0.0).then_inc(consts_made, 1)
            pool.memset(mv[:, :, :], 1.0).then_inc(consts_made, 1)
            pool.wait_ge(consts_made, CONSTS)

            def input_norm(b):
                pool.wait_ge(xvar_ready.sem, xvar_ready.at(b, 1))
                pool.tensor_tensor(rstd[:, :], var[:, :], mhalf[:, :], ALU.pow).then_inc(xrstd_ready.sem, 1)

            def keep_kvT(b):
                pool.wait_ge(kvx_ready.sem, kvx_ready.at(b, 1))
                pool.wait_ge(kvc_ready.sem, kvc_ready.at(b, 1))
                pool.nop(nofuse=True)
                pool.tensor_copy(kvT[:, :, :], kvTn[:, :, :]).then_inc(kvT_ready.sem, 1)

            def normalise_pair(b, p):
                pool.wait_ge(rinv_ready.sem, rinv_ready.at(b, p + 1))
                if p >= 2:
                    pool.wait_ge(aT_done.sem, aT_done.at(b, p - 1))
                elif not first(b):
                    pool.wait_ge(aT_done.sem, aT_done.at(b - 1, PAIRS - 1 + p))
                for t in range(TT):
                    ins = pool.tensor_tensor(aN[:, p % 2, t, :].rearrange("p (h d) -> p h d", h=2), aU[:, p % 2, t, :, 0:DH0],
                                             rinv[:, p % 2, t, :].unsqueeze(2).to_broadcast([P, 2, DH0]), ALU.mult)
                ins.then_inc(aN_ready.sem, 1)

            def slot(b, s, front, chain, tail, ahead, part):
                if front and 4 < s < UNITS and s % 4 == 1:
                    normalise_pair(b, s // 4 - 1)
                if front and s == UNITS:
                    normalise_pair(b, PAIRS - 1)
                if front and s == 3:
                    if chain:
                        pool.wait_ge(x1_ready.sem, x1_ready.at(b - 1, TT))
                        pool.wait_ge(kv1_done.sem, kv1_done.at(b - 1, 1))
                        pool.nop(nofuse=True)
                    pool.wait_ge(xf_ready.sem, xf_ready.at(b, 1))
                    pool.nop(nofuse=True)
                    pool.tensor_copy(xres[:, :, :], xin[:, :, :]).then_inc(xres_ready.sem, 1)
                    pool.wait_ge(kvc_ready.sem, kvc_ready.at(b, 1))
                    pool.nop(nofuse=True)
                    pool.tensor_copy(cT[:, :, :], cTn[:, :, :]).then_inc(cT_ready.sem, 1)
                if ahead and s == NEXT_STATS_AT:
                    input_norm(b + 1)
                if ahead and s == NEXT_K_AT - 2:
                    pool.wait_ge(k_done.sem, k_done.at(b, PAIRS))
                    keep_kvT(b + 1)
                if chain and s == 2:
                    pool.wait_ge(yvar_ready.sem, yvar_ready.at(b - 1, 1))
                    pool.tensor_tensor(rstdy[:, :], vary[:, :], mhalf[:, 0:TT], ALU.pow).then_inc(yrstd_ready.sem, 1)
                if chain and s == 4:
                    pool.wait_ge(k1v1_ready.sem, k1v1_ready.at(b - 1, 1))
                    for g in range(HT):
                        ins = pool.tensor_tensor(k1d[:, g, :, :], k1[:, g, :].unsqueeze(1).to_broadcast([P, HH, C]),
                                                 own[:, :].unsqueeze(2).to_broadcast([P, HH, C]), ALU.mult)
                    ins.then_inc(k1d_ready.sem, 1)
                part()

            def chain_part(b, c):
                if c == 0:
                    pool.wait_ge(y1_ready.sem, y1_ready.at(b, 1))
                    for t in range(TT):
                        ins = pool.tensor_tensor(x1[:, t, :], x1[:, t, :], betaB[:, :], ALU.add)
                    ins.then_inc(x1b_ready.sem, 1)
                if c == 17:
                    pool.wait_ge(xn_ready.sem, xn_ready.at(b, 1))
                    for t in range(TT):
                        ins = pool.tensor_tensor(x2[:, t, :], x2[:, t, :], boB[:, :], ALU.add)
                    ins.then_inc(x2b_ready.sem, 1)
                if c == 35:
                    pool.wait_ge(tap_ready.sem, tap_ready.at(b, 1))
                    pool.nop(nofuse=True)
                    for m in range(2):
                        for j in range(2):
                            ins = pool.tensor_scalar(tap[m][:, j, :], hb[:, j, 2 * m:2 * m + S], cw[:, j, 2 * m:2 * m + 1],
                                                     None, ALU.mult)
                    ins.then_inc(pool_link.sem, 1)
                    pool.wait_ge(pool_link.sem, pool_link.at(b, 1))
                    v = cv[:, 0:2, :]
                    pool.tensor_tensor(v, v, tap[0][:, :, :], ALU.add).then_inc(pool_link.sem, 1)
                    pool.wait_ge(pool_link.sem, pool_link.at(b, 2))
                    pool.tensor_tensor(v, v, tap[1][:, :, :], ALU.add).then_inc(conv_pool.sem, 1)
                for n, at in ((1, 13), (2, 15), (3, 30)):
                    if c == at:
                        pool.wait_ge(var2_ready.sem, var2_ready.at(b, n))
                        pool.tensor_tensor(rstd2[:, :], var2[:, :], mhalf[:, 0:TT], ALU.pow).then_inc(rstd2_ready.sem, 1)

            input_norm(0)
            keep_kvT(0)
            pool.wait_ge(ld["bias"], 16 * 9)
            turns(pool, lambda b, front, chain, tail, ahead: walk(b, front, chain, tail, ahead, slot, chain_part))

        @block.tensor
        def _(pe):
            mm, tr = pe.matmul, pe.transpose
            pe.wait_ge(ident_made, 4)

            def setup(n):
                if n in (1, 2):
                    if n == 1:
                        pe.wait_ge(ld["l1"], 64)
                    else:
                        pe.wait_ge(setup_dve, DC)
                    for k in ((0, 1, 2), (3,))[n - 1]:
                        for a in range(2):
                            for c in range(DC):
                                ins = tr(ps[:, 5 + k % 3, (2 * a + c) * P:(2 * a + c + 1) * P],
                                         stgq[:, k * 512 + a * 256 + c * P:k * 512 + a * 256 + (c + 1) * P], ident[:, :])
                        ins.then_inc(setup_pe, 1)
                if n == 5:
                    pe.wait_ge(setup_dve, SETUP_SUMS)
                    mm(ps[:, 7, 0:2], ones[:, :], absum[:, :], start=True, stop=True).then_inc(setup_pe, 1)
                if n in (12, 13):
                    c = n - 12
                    pe.wait_ge(setup_dve, SETUP_TERNARY)
                    for j in range(FT):
                        ins = tr(psb[:, 5 + c, j * P:(j + 1) * P], stb1[:, j * D + c * P:j * D + (c + 1) * P], identb[:, :])
                    ins.then_inc(setup_pe, 1)
                if n in (14, 15):
                    i = n - 14
                    if i:
                        pe.wait_ge(setup_dve, SETUP_TERNARY + 1)
                    for j in range(4 * i, 4 * i + 4):
                        for c in range(DC):
                            ins = tr(psb[:, (7, 5)[i], (j % 4) * 256 + c * P:(j % 4) * 256 + (c + 1) * P],
                                     stb2[:, c * F + j * P:c * F + (j + 1) * P], identb[:, :])
                    ins.then_inc(setup_pe, 1)
                if n == 16:
                    pe.wait_ge(ld["out"], 32)

            def transpose_tokens(dst, bank, src, idn):
                for c in range(DC):
                    for t in range(TT):
                        ins = tr(dst[:, bank, c * S + t * P:c * S + (t + 1) * P], src[:, t, c * P:(c + 1) * P], idn[:, :])
                return ins

            def project_q(b, p, kv):
                for c in range(DC):
                    ins = mm(ps[:, BANK_PJ, 0:S], wq0[:, c, p * P:(p + 1) * P], kv[:, c, 0:S], start=c == 0, stop=c == DC - 1)
                ins.then_inc(q_done.sem, 1)

            def project_k(b, p, kv):
                pe.wait_ge(q_ready.sem, q_ready.at(b, p + 1))
                for c in range(DC):
                    ins = mm(ps[:, BANK_PJ, 0:KEYS], wkv0[:, c, p * P:(p + 1) * P], kv[:, c, :], start=c == 0, stop=c == DC - 1)
                ins.then_inc(k_done.sem, 1)

            def project_v(b, n, k, kv):
                for c in range(DC):
                    ins = mm(ps[0:KP, BANK_PJ, :], kv[:, c, k * KP:(k + 1) * KP],
                             wkv0[:, c, INNER + n * 512:INNER + (n + 1) * 512], start=c == 0, stop=c == DC - 1)
                ins.then_inc(v_done.sem, 1)

            def transpose_latents(b):
                pe.wait_ge(xf_ready.sem, xf_ready.at(b, 1))
                transpose_tokens(ps, BANK_PJ, xf, ident).then_inc(xT_done.sem, 1)

            def transpose_context(b):
                for n, src in enumerate((cn, cin)):
                    for c in range(DC):
                        ins = tr(ps[:, BANK_PJ, (2 * n + c) * C:(2 * n + c + 1) * C], src[:, c * P:(c + 1) * P], ident[0:C, 0:C])
                ins.then_inc(cT_done.sem, 1)

            def scores(b, u):
                p, t, h = u // 4, u // 2 % 2, u % 2
                pe.wait_ge(k_ready.sem, k_ready.at(b, p + 1))
                if u >= 2:
                    pe.wait_ge(exp_ready.sem, exp_ready.at(b, u - 1))
                r = slice(DH0 * h, DH0 * h + DH0)
                mm(ps[:, BANK_S[u % 2], 0:KEYS], qT[r, p % 2, t * P:(t + 1) * P], kT[r, p % 2, :],
                   start=True, stop=True).then_inc(score_done.sem, 1)

            def transpose_p(b, u):
                pe.wait_ge(exp_ready.sem, exp_ready.at(b, u + 1))
                if u:
                    pe.wait_ge(pt_ready.sem, pt_ready.at(b, u))
                for k in range(KT):
                    ins = tr(ps[0:KP, BANK_PT, k * P:(k + 1) * P], Pr[:, u % 2, k * KP:(k + 1) * KP], ident[:, :])
                ins.then_inc(pt_done.sem, 1)

            def attend(b, u):
                pe.wait_ge(pt_ready.sem, pt_ready.at(b, u + 1))
                if u:
                    pe.wait_ge(norm_ready.sem, norm_ready.at(b, u))
                for k in range(KT):
                    ins = mm(ps[:, BANK_PV, 0:DH0 + 1], PT[:, u % 2, k * P:(k + 1) * P], V[:, k, 2 * (u // 4) + u % 2, :],
                             start=k == 0, stop=k == KT - 1)
                ins.then_inc(pv_done.sem, 1)

            def transpose_a(b, p):
                pe.wait_ge(aN_ready.sem, aN_ready.at(b, p + 1))
                for t in range(TT):
                    ins = tr(ps[:, BANK_PJ, t * P:(t + 1) * P], aN[:, p % 2, t, :], ident[:, :])
                ins.then_inc(aT_done.sem, 1)

            def out_product(b, t, pairs):
                for p in pairs:
                    ins = mm(ps[:, 2 + t, 0:D], aT[:, p, t * P:(t + 1) * P], wo0[:, p, :], start=p == 0, stop=p == PAIRS - 1)
                if pairs[-1] == PAIRS - 1:
                    ins.then_inc(wo_done.sem, 1)

            def scores(b, u):
                p, t, h = u // 4, u // 2 % 2, u % 2
                pe.wait_ge(k_ready.sem, k_ready.at(b, p + 1))
                if u >= 2:
                    pe.wait_ge(exp_ready.sem, exp_ready.at(b, u - 1))
                r = slice(DH0 * h, DH0 * h + DH0)
                mm(ps[:, BANK_S[u % 2], 0:KEYS], qT[r, p % 2, t * P:(t + 1) * P], kT[r, p % 2, :],
                   start=True, stop=True).then_inc(score_done.sem, 1)

            def transpose_p(b, u):
                pe.wait_ge(exp_ready.sem, exp_ready.at(b, u + 1))
                if u:
                    pe.wait_ge(pt_ready.sem, pt_ready.at(b, u))
                for k in range(KT):
                    ins = tr(ps[0:KP, BANK_PT, k * P:(k + 1) * P], Pr[:, u % 2, k * KP:(k + 1) * KP], ident[:, :])
                ins.then_inc(pt_done.sem, 1)

            def attend(b, u):
                pe.wait_ge(pt_ready.sem, pt_ready.at(b, u + 1))
                if u:
                    pe.wait_ge(norm_ready.sem, norm_ready.at(b, u))
                for k in range(KT):
                    ins = mm(ps[:, BANK_PV, 0:DH0 + 1], PT[:, u % 2, k * P:(k + 1) * P], V[:, k, 2 * (u // 4) + u % 2, :],
                             start=k == 0, stop=k == KT - 1)
                ins.then_inc(pv_done.sem, 1)

            def projections(b, u, front, chain, ahead):
                j, m = divmod(u, 4)
                if front and m == 0 and j + 1 < PAIRS:
                    if u == 0:
                        pe.wait_ge(v_ready.sem, v_ready.at(b, KT))
                        pe.wait_ge(kvT_ready.sem, kvT_ready.at(b, 1))
                    elif u == 4 and chain:
                        pe.wait_ge(y1T_ready.sem, y1T_ready.at(b - 1, 1))
                    elif u == 4:
                        pe.wait_ge(v_ready.sem, v_ready.at(b, KT + 1))
                    else:
                        pe.wait_ge(aT_ready.sem, aT_ready.at(b, j - 1))
                    project_q(b, j + 1, kvT)
                if front and m == 1 and j + 1 < PAIRS:
                    project_k(b, j + 1, kvT)
                if front and u in HIGH_VALUES_AT:
                    pe.wait_ge(k_ready.sem, k_ready.at(b, j + 2))
                    project_v(b, 1, j, kvT)
                if front and m == 3 and j:
                    if u < 15:
                        pe.wait_ge(v_ready.sem, v_ready.at(b, KT + j + 1))
                    elif not ahead:
                        pe.wait_ge(k_ready.sem, k_ready.at(b, min(j + 2, PAIRS)))
                        if u == UNITS - 1:
                            pe.wait_ge(aT_ready.sem, aT_ready.at(b, j - 1))
                    elif u == 15:
                        pe.wait_ge(kvx_ready.sem, kvx_ready.at(b + 1, 1))
                    elif u == 19:
                        pe.wait_ge(kvc_ready.sem, kvc_ready.at(b + 1, 1))
                    else:
                        pe.wait_ge(v_ready.sem, v_ready.at(b + 1, j - 4))
                    transpose_a(b, j - 1)
                if not ahead:
                    return
                if u == NEXT_XT_AT:
                    pe.wait_ge(k_ready.sem, k_ready.at(b, j + 2))
                    transpose_latents(b + 1)
                if u == NEXT_CT_AT:
                    pe.wait_ge(k_ready.sem, k_ready.at(b, j + 2))
                    pe.wait_ge(cT_ready.sem, cT_ready.at(b, 1))
                    transpose_context(b + 1)
                if u in NEXT_VALUES_AT:
                    pe.wait_ge(kvc_ready.sem, kvc_ready.at(b + 1, 1))
                    if u < NEXT_K_AT:
                        pe.wait_ge(k_ready.sem, k_ready.at(b, j + 2))
                    else:
                        pe.wait_ge(k_ready.sem, k_ready.at(b + 1, 1))
                    project_v(b + 1, 0, j - 5, kvTn)
                if u == NEXT_Q_AT:
                    pe.wait_ge(aT_ready.sem, aT_ready.at(b, j - 1))
                    project_q(b + 1, 0, kvTn)
                if u == NEXT_K_AT:
                    project_k(b + 1, 0, kvTn)

            def router(b, front_of):
                pe.wait_ge(y1T_ready.sem, y1T_ready.at(b, 1))
                if front_of is not None:
                    pe.wait_ge(pt_ready.sem, pt_ready.at(front_of, LOGITS_AT))
                for c in range(DC):
                    ins = mm(ps[0:1, BANK_PT, KT * P:KT * P + E], ysum[:, c:c + 1], wr[:, c, :], start=c == 0, stop=c == DC - 1)
                ins.then_inc(logit_done.sem, 1)

            def slot(b, s, front, chain, tail, ahead, part):
                u = s
                if chain and s == 0:
                    pe.wait_ge(x1_ready.sem, x1_ready.at(b - 1, TT))
                    pe.wait_ge(k1v1_ready.sem, k1v1_ready.at(b - 1, 1))
                if u < UNITS:
                    if front and 0 < u < UNITS - 1:
                        scores(b, u + 1)
                    if front and u in LONG_PARTS_AT:
                        attend(b, u - 1)
                    part()
                    if chain and s == Y1T_AT:
                        if front:
                            pe.wait_ge(v_ready.sem, v_ready.at(b, KT + 1))
                        pe.wait_ge(y1_ready.sem, y1_ready.at(b - 1, 1))
                        transpose_tokens(ps, BANK_PJ, y1, ident).then_inc(y1T_done.sem, 1)
                    if front and u and u not in LONG_PARTS_AT:
                        attend(b, u - 1)
                    if chain and s == LOGITS_AT:
                        router(b - 1, b if front else None)
                    if front:
                        if chain and s == LOGITS_AT + 1:
                            pe.wait_ge(lgr_ready.sem, lgr_ready.at(b - 1, 1))
                        transpose_p(b, u)
                    projections(b, u, front, chain, ahead)
                    return
                if front and s == UNITS:
                    attend(b, UNITS - 1)
                if ahead and s < UNITS + 2:
                    scores(b + 1, s - UNITS)
                if front and s == UNITS:
                    pe.wait_ge(aT_ready.sem, aT_ready.at(b, PAIRS - 1))
                    out_product(b, 0, range(PAIRS - 1))
                if front and s == UNITS + 1:
                    pe.wait_ge(norm_ready.sem, norm_ready.at(b, UNITS))
                    out_product(b, 1, range(PAIRS // 2))
                    transpose_a(b, PAIRS - 1)
                if front and s == UNITS + 2:
                    pe.wait_ge(aT_ready.sem, aT_ready.at(b, PAIRS))
                    out_product(b, 0, range(PAIRS - 1, PAIRS))
                    out_product(b, 1, range(PAIRS // 2, PAIRS))
                if front and s == UNITS + 3:
                    pe.wait_ge(cT_ready.sem, cT_ready.at(b, 1))
                    for g in range(HT):
                        for c in range(DC):
                            ins = mm(ps[:, BANK_PJ, g * C:(g + 1) * C], wkT[:, c, g * P:(g + 1) * P], cT[:, c, :],
                                     start=c == 0, stop=c == DC - 1)
                    for c in range(DC):
                        ins = mm(ps[0:C, BANK_PJ, S:S + D], cT[:, c, :], wvT[:, c, :], start=c == 0, stop=c == DC - 1)
                    ins.then_inc(kv1_done.sem, 1)
                part()

            def layer1_scores(b, n):
                t, g = divmod(n, HT)
                if n == 0:
                    pe.wait_ge(q1_ready.sem, q1_ready.at(b, 1))
                    pe.wait_ge(k1d_ready.sem, k1d_ready.at(b, 1))
                elif g:
                    pe.wait_ge(s1_shift.sem, s1_shift.at(b, n))
                else:
                    pe.wait_ge(a1_ready.sem, a1_ready.at(b, t))
                for m in range(2):
                    ins = mm(ps[:, ((5, 6), (7, 5))[g][m], 0:4 * C], q1T[:, g, t * P:(t + 1) * P],
                             k1d[:, g, 4 * m:4 * m + 4, :].rearrange("p h c -> p (h c)"), start=True, stop=True)
                ins.then_inc(s1_done.sem, 1)

            def layer1_transpose(b, t, ms):
                pe.wait_ge(e1_ready.sem, e1_ready.at(b, HT * t + ms[0] // 2 + 1))
                for m in ms:
                    if m == 1:
                        pe.wait_ge(s1_shift.sem, s1_shift.at(b, HT * t + HT))
                    if m == 3:
                        pe.wait_ge(t1_act.sem, t1_act.at(b, 2 * t + 1))
                    for h in range(4 * m, 4 * m + 4):
                        ins = tr(ps[0:C, (6, 7, 5, 6)[m], (h % 4) * P:(h % 4 + 1) * P], P1[:, h, :], ident[:, :])
                    ins.then_inc(t1_done.sem, 1)

            def layer1_attend(b, t):
                pe.wait_ge(t1_act.sem, t1_act.at(b, 2 * t + 2))
                pe.wait_ge(t1_dve.sem, t1_dve.at(b, 2 * t + 2))
                for h in range(H1):
                    ins = mm(ps[:, 7, h * (DH1 + 1):(h + 1) * (DH1 + 1)], PT1[:, h, :], v1[:, h, :], start=True, stop=True)
                ins.then_inc(pv1_done.sem, 1)

            def chain_part(b, c):
                if c == 0:
                    if not first(b):
                        pe.wait_ge(x4_ready.sem, x4_ready.at(b, 0))
                    pe.wait_ge(b_in.sem, b_in.at(b, 16 * 2 * TOPK))
                    pe.nop(nofuse=True)
                    for k in range(TOPK):
                        ins = tr(ps[:, 7, k * FT:(k + 1) * FT], b1r[:, k, :], ident[0:FT, 0:FT])
                    ins.then_inc(b1T_done.sem, 1)
                    pe.wait_ge(wtop_ready.sem, wtop_ready.at(b, 1))
                    pe.nop(nofuse=True)
                    mm(ps[:, 6, 0:2], ones[0:1, :], wtop[:, :], start=True, stop=True).then_inc(wB_done.sem, 1)
                if 1 <= c <= 8:
                    i = c - 1
                    k = i // 4
                    if i % 4 == 0:
                        pe.wait_ge(w1_in[k].sem, w1_in[k].at(b, 16))
                    if i == 1:
                        pe.wait_ge(wB_ready.sem, wB_ready.at(b, 1))
                    if i == 2:
                        pe.wait_ge(b1T_ready.sem, b1T_ready.at(b, 1))
                    if i >= 3:
                        pe.wait_ge(gelu_ready.sem, gelu_ready.at(b, i - 2))
                    for j in (2 * (i % 4), 2 * (i % 4) + 1):
                        for d in range(DC):
                            ins = mm(ps[:, 5 + i % 3, (j % 2) * S:(j % 2 + 1) * S], W1s[:, k, d, j * P:(j + 1) * P], yT[:, d, :],
                                     start=d == 0, stop=d == DC - 1)
                    ins.then_inc(h_done.sem, 1)
                if c == 11:
                    pe.wait_ge(gelu_ready.sem, gelu_ready.at(b, 8))
                    pe.wait_ge(wB_ready.sem, wB_ready.at(b, 1))
                    pe.nop(nofuse=True)
                    for k in range(TOPK):
                        ins = mm(ps[:, 6, 0:D], wrow[:, k, :], b2r[:, k, :], start=k == 0, stop=k == TOPK - 1)
                    ins.then_inc(b2_done.sem, 1)
                if 9 <= c <= 12:
                    k, t = divmod(c - 9, TT)
                    if t == 0:
                        pe.wait_ge(w2_in[k].sem, w2_in[k].at(b, 16))
                        pe.wait_ge(gelu_ready.sem, gelu_ready.at(b, 6 + 2 * k))
                    for j in range(FT):
                        ins = mm(ps[:, (7, 5)[k], t * D:(t + 1) * D], hT[:, k, j, t * P:(t + 1) * P], W2s[:, k, j, :],
                                 start=j == 0, stop=j == FT - 1)
                    if t == TT - 1:
                        ins.then_inc(moe_done.sem, 1)
                if c == 17:
                    pe.wait_ge(xn_ready.sem, xn_ready.at(b, 1))
                    transpose_tokens(ps, 6, xn, ident).then_inc(ynT_done.sem, 1)
                if c == 18:
                    pe.wait_ge(ynT_ready.sem, ynT_ready.at(b, 1))
                    for g in range(HT):
                        for d in range(DC):
                            ins = mm(ps[:, 7, g * S:(g + 1) * S], wqT[:, d, g * P:(g + 1) * P], yT[:, d, :],
                                     start=d == 0, stop=d == DC - 1)
                    ins.then_inc(q1_done.sem, 1)
                for t in range(TT):
                    if c in (19 + 5 * t, 20 + 5 * t):
                        layer1_scores(b, HT * t + c - 19 - 5 * t)
                    if c in (21 + 5 * t, 22 + 5 * t):
                        layer1_transpose(b, t, ((0, 1), (2, 3))[c - 21 - 5 * t])
                    if c == 23 + 5 * t:
                        layer1_attend(b, t)
                if c == 29:
                    pe.wait_ge(a1_ready.sem, a1_ready.at(b, TT))
                    transpose_tokens(ps, 5, a1, ident).then_inc(a1T_done.sem, 1)
                if c == 30:
                    pe.wait_ge(a1T_ready.sem, a1T_ready.at(b, 1))
                    for t in range(TT):
                        for d in range(DC):
                            ins = mm(ps[:, 6, t * D:(t + 1) * D], a1T[:, d, t * P:(t + 1) * P], woT[:, d, :],
                                     start=d == 0, stop=d == DC - 1)
                    ins.then_inc(wo1_done.sem, 1)
                if c == 33:
                    pe.wait_ge(qx_ready.sem, qx_ready.at(b, 1))
                    transpose_tokens(psb, 5, qx, identb).then_inc(qxT_done.sem, 1)
                if c in (33, 42):
                    pe.wait_ge(dg_ready.sem, dg_ready.at(b, 1 if c == 33 else 2))
                    for t in range(TT):
                        ins = mm(ps[:, 7, t * P:(t + 1) * P], ones[:, :], dg[:, t, :], start=True, stop=True)
                    ins.then_inc(sB_done.sem, 1)
                if 34 <= c <= 37:
                    n = c - 34
                    if n == 0:
                        pe.wait_ge(qxT_ready.sem, qxT_ready.at(b, 1))
                    if n >= 2:
                        pe.wait_ge(hb_ready.sem, hb_ready.at(b, n - 1))
                    for j in (2 * n, 2 * n + 1):
                        for d in range(DC):
                            ins = mm(ps[:, (6, 5, 7, 6)[n], (j % 2) * S:(j % 2 + 1) * S], f1T[:, d, j * P:(j + 1) * P],
                                     qxT[:, d, :], start=d == 0, stop=d == DC - 1)
                    ins.then_inc(f1_done.sem, 1)
                if c == 41:
                    pe.wait_ge(mj_ready.sem, mj_ready.at(b, 1))
                    for t in range(TT):
                        ins = tr(ps[:, 5, t * P:(t + 1) * P], mj[:, t * P:(t + 1) * P], ident[:, :])
                    ins.then_inc(mjT_done.sem, 1)
                if c == 45:
                    pe.wait_ge(q2_ready.sem, q2_ready.at(b, 4))
                    for t in range(TT):
                        for j in range(FT):
                            ins = mm(ps[:, 5 + t, 0:D], q2[:, j, t * P:(t + 1) * P], f2T[:, j, :], start=j == 0, stop=j == FT - 1)
                        ins.then_inc(f2_done.sem, 1)

            transpose_latents(0)
            pe.wait_ge(ld["w0"], 32)
            pe.wait_ge(kvx_ready.sem, kvx_ready.at(0, 1))
            transpose_context(0)
            pe.wait_ge(kvc_ready.sem, kvc_ready.at(0, 1))
            for k in range(KT):
                if k:
                    pe.wait_ge(v_ready.sem, v_ready.at(0, k))
                project_v(0, 0, k, kvTn)
            pe.wait_ge(v_ready.sem, v_ready.at(0, KT))
            project_q(0, 0, kvTn)
            project_k(0, 0, kvTn)
            scores(0, 0)
            scores(0, 1)
            pe.wait_ge(consts_made, CONSTS)
            turns(pe, lambda b, front, chain, tail, ahead: walk(b, front, chain, tail, ahead, slot, chain_part, setup))

        @block.scalar
        def _(act):
            fn = act.activation
            act.wait_ge(ld["vec"], 64)

            def q_out(b, p):
                act.wait_ge(q_done.sem, q_done.at(b, p + 1))
                fn(qT[:, p % 2, :], ps[:, BANK_PJ, 0:S], ACT.Copy, scale=DH0 ** -0.5).then_inc(q_ready.sem, 1)

            def v_out(b, n, k):
                act.wait_ge(v_done.sem, v_done.at(b, KT * n + k + 1))
                fn(V[:, k, 8 * n:8 * n + 8, 0:DH0], ps[0:KP, BANK_PJ, :].rearrange("p (h d) -> p h d", d=DH0), ACT.Copy)\
                    .then_inc(v_ready.sem, 1)

            def a_out(b, p):
                act.wait_ge(aT_done.sem, aT_done.at(b, p + 1))
                fn(aT[:, p, :], ps[:, BANK_PJ, 0:S], ACT.Copy).then_inc(aT_ready.sem, 1)

            def exps(b, u):
                act.wait_ge(max_ready.sem, max_ready.at(b, u + 1))
                fn(Pr[:, u % 2, :], ps[:, BANK_S[u % 2], 0:KEYS], ACT.Exp, bias=nmax[:, u % 2:u % 2 + 1])\
                    .then_inc(exp_ready.sem, 1)

            def latents_out(b):
                act.wait_ge(xT_done.sem, xT_done.at(b, 1))
                for c in range(DC):
                    ins = fn(kvTn[:, c, 0:S], ps[:, BANK_PJ, c * S:(c + 1) * S], ACT.Identity, scale=g2[:, c:c + 1], bias=bb2[:, c:c + 1])
                ins.then_inc(kvx_ready.sem, 1)

            def late_part(b, c):
                if 34 <= c <= 37:
                    n = c - 34
                    act.wait_ge(hb_ready.sem, hb_ready.at(b, n + 1))
                    for j in (2 * n, 2 * n + 1):
                        ins = fn(cv[:, j, :], hb[:, j, 1:S + 1], ACT.Identity, scale=cw[:, j, 1:2], bias=cb[:, j:j + 1])
                    ins.then_inc(tap_ready.sem, 1)
                if c == SILU_PART:
                    for n in range(4):
                        if n == 0:
                            act.wait_ge(conv_pool.sem, conv_pool.at(b, 1))
                        else:
                            act.wait_ge(conv_dve.sem, conv_dve.at(b, n))
                        v = flat(cv[:, 2 * n:2 * n + 2, :])
                        fn(v, v, ACT.Silu).then_inc(silu_ready.sem, 1)

            def slot(b, s, front, chain, tail, ahead, part):
                u = s
                j, m = divmod(u, 4)
                if front and 0 < u < UNITS - 1:
                    exps(b, u + 1)
                if ahead and UNITS <= s < UNITS + 2:
                    exps(b + 1, s - UNITS)
                if front and s == UNITS + 1:
                    a_out(b, PAIRS - 1)
                part()
                if chain and s == Y1T_AT:
                    act.wait_ge(y1T_done.sem, y1T_done.at(b - 1, 1))
                    for c in range(DC):
                        ins = fn(yT[:, c, :], ps[:, BANK_PJ, c * S:(c + 1) * S], ACT.Copy, accum_out=ysum[:, c:c + 1])
                    ins.then_inc(y1T_ready.sem, 1)
                if front and u < UNITS:
                    act.wait_ge(pt_done.sem, pt_done.at(b, u + 1))
                    fn(PT[:, u % 2, :], ps[0:KP, BANK_PT, 0:KT * P], ACT.Copy).then_inc(pt_ready.sem, 1)
                if chain and s == LOGITS_AT:
                    act.wait_ge(logit_done.sem, logit_done.at(b - 1, 1))
                    fn(lgr[:, :], ps[0:1, BANK_PT, KT * P:KT * P + E], ACT.Copy).then_inc(lgr_ready.sem, 1)
                if chain and s == LOGITS_AT + 1:
                    act.wait_ge(logit_ready.sem, logit_ready.at(b - 1, 1))
                    fn(ex[:, :], lg[:, :], ACT.Exp, bias=nlg[:, :], accum_out=exs[:, :]).then_inc(rexp_ready.sem, 1)
                if chain and s == LOGITS_AT + 2:
                    act.wait_ge(gap_ready.sem, gap_ready.at(b - 1, 1))
                    fn(egap[:, :], gap[:, :], ACT.Exp).then_inc(egap_ready.sem, 1)
                if front and m == 0 and j + 1 < PAIRS:
                    q_out(b, j + 1)
                if front and u in HIGH_VALUES_AT:
                    v_out(b, 1, j)
                if front and m == 3 and j and u < UNITS:
                    a_out(b, j - 1)
                if ahead and u == NEXT_XT_AT:
                    latents_out(b + 1)
                if ahead and u in NEXT_VALUES_AT:
                    v_out(b + 1, 0, j - 5)
                if ahead and u == NEXT_Q_AT:
                    q_out(b + 1, 0)
                for c in range(PARTS):
                    if chain and START[c] == s:
                        late_part(b - 1, c)
                    if tail and START[c] == s + SLOTS:
                        late_part(b - 2, c)

            def chain_part(b, c):
                if c == 0:
                    act.wait_ge(b1T_done.sem, b1T_done.at(b, 1))
                    fn(b1T[:, :], ps[:, 7, 0:TOPK * FT], ACT.Copy).then_inc(b1T_ready.sem, 1)
                if c in (2, 4, 6, 8):
                    for i in (c - 2, c - 1):
                        act.wait_ge(h_done.sem, h_done.at(b, i + 1))
                        if i == 0:
                            act.wait_ge(b1T_ready.sem, b1T_ready.at(b, 1))
                        for j in (2 * i, 2 * i + 1):
                            ins = fn(hT[:, j // FT, j % FT, :], ps[:, 5 + i % 3, (j % 2) * S:(j % 2 + 1) * S], ACT.Gelu,
                                     bias=b1T[:, j:j + 1])
                        ins.then_inc(gelu_ready.sem, 1)
                if c == 17:
                    act.wait_ge(ynT_done.sem, ynT_done.at(b, 1))
                    fn(flat(yT[:, :, :]), ps[:, 6, :], ACT.Copy).then_inc(ynT_ready.sem, 1)
                if c == 18:
                    act.wait_ge(q1_done.sem, q1_done.at(b, 1))
                    for g in range(HT):
                        ins = fn(q1T[:, g, :], ps[:, 7, g * S:(g + 1) * S], ACT.Identity, scale=DH1 ** -0.5, bias=bqp[:, g:g + 1])
                    ins.then_inc(q1_ready.sem, 1)
                for t in range(TT):
                    if c in (20 + 5 * t, 21 + 5 * t):
                        g = c - 20 - 5 * t
                        act.wait_ge(s1_shift.sem, s1_shift.at(b, HT * t + g + 1))
                        v = P1[:, HH * g:HH * (g + 1), :].rearrange("p h c -> p (h c)")
                        fn(v, v, ACT.Exp).then_inc(e1_ready.sem, 1)
                    if c in (21 + 5 * t, 22 + 5 * t):
                        m = 2 * (c - 21 - 5 * t)
                        act.wait_ge(t1_done.sem, t1_done.at(b, 4 * t + m + 1))
                        fn(PT1[:, 4 * m:4 * m + 4, :].rearrange("p h q -> p (h q)"), ps[0:C, (6, 7, 5, 6)[m], :], ACT.Copy)\
                            .then_inc(t1_act.sem, 1)
                if c == 29:
                    act.wait_ge(a1T_done.sem, a1T_done.at(b, 1))
                    fn(flat(a1T[:, :, :]), ps[:, 5, :], ACT.Copy).then_inc(a1T_ready.sem, 1)
                if c == 33:
                    act.wait_ge(qxT_done.sem, qxT_done.at(b, 1))
                    fn(flat(qxT[:, :, :]), psb[:, 5, 0:DC * S], ACT.Copy).then_inc(qxT_ready.sem, 1)
                if c in (33, 42):
                    act.wait_ge(sB_done.sem, sB_done.at(b, 1 if c == 33 else 2))
                    fn(sB[:, :], ps[:, 7, 0:S], ACT.Copy).then_inc(sB_ready.sem, 1)
            latents_out(0)
            for k in range(KT):
                v_out(0, 0, k)
            q_out(0, 0)
            exps(0, 0)
            exps(0, 1)
            turns(act, lambda b, front, chain, tail, ahead: walk(b, front, chain, tail, ahead, slot, chain_part))

        @block.vector
        def _(dve):
            tt, ts, stt, cp, red = (dve.tensor_tensor, dve.tensor_scalar, dve.scalar_tensor_tensor,
                                    dve.tensor_copy, dve.tensor_reduce)
            n_setup = [0]

            def did(ins):
                n_setup[0] += 1
                ins.then_inc(setup_dve, 1)
                dve.wait_ge(setup_dve, n_setup[0])

            def setup(n):
                if n in (1, 2):
                    for k in ((0, 1, 2), (3,))[n - 1]:
                        dve.wait_ge(setup_pe, k + 1)
                        for c in range(DC):
                            did(cp((wqT, wkT, wvT, woT)[k][:, c, :].rearrange("p (a n) -> p a n", a=2),
                                   ps[:, 5 + k % 3, :].rearrange("p (a c n) -> p a c n", a=2, c=DC)[:, :, c, :]))
                if n in (3, 4):
                    if n == 3:
                        dve.wait_ge(ld["ffn"], 32)
                    did(red(absum[:, n - 3:n - 2], (stg1, stg2)[n - 3], AX.X, ALU.add, apply_absolute_value=True))
                    assert n == 3 or n_setup[0] == SETUP_SUMS
                if n == 5:
                    dve.wait_ge(setup_pe, 5)
                    did(ts(mw[:, :], ps[:, 7, 0:2], 1.0 / (F * D), 1e-5, ALU.mult, ALU.max))
                    did(dve.reciprocal(ws[:, :], mw[:, :]))
                if 6 <= n <= 11:
                    k, step = divmod(n - 6, 3)
                    w, dst = ((stg1, stb1), (stg2, stb2))[k]
                    if step == 0:
                        did(ts(w, w, ws[:, k:k + 1], MAGIC, ALU.mult, ALU.add))
                    if step == 1:
                        did(ts(w, w, MAGIC, 1.0, ALU.subtract, ALU.min))
                    if step == 2:
                        did(ts(dst, w, -1.0, None, ALU.max))
                    assert n < 11 or n_setup[0] == SETUP_TERNARY
                if n in (12, 13):
                    dve.wait_ge(setup_pe, n - 6)
                    did(cp(f1T[:, n - 12, :], psb[:, 5 + n - 12, :]))
                if n in (14, 15):
                    i = n - 14
                    dve.wait_ge(setup_pe, n - 6)
                    did(cp(f2T[:, 4 * i:4 * i + 4, :].rearrange("p a n -> p (a n)"), psb[:, (7, 5)[i], :]))
                if n == 16:
                    dve.wait_ge(ld["bias"], 16 * 9)
                    did(ts(bqp[:, :], bqp[:, :], DH1 ** -0.5, None, ALU.mult))
                    assert n_setup[0] == SETUP_DVE_END, n_setup[0]

            links = {}

            def link(chain_of, b, ins):
                links[chain_of] = links.get(chain_of, 0) + 1
                ins.then_inc(chain_of.sem, 1)
                dve.wait_ge(chain_of.sem, chain_of.at(b, links[chain_of]))

            def nlink(b, ins):
                link(norm_link, b, ins)

            def rlink(b, ins):
                link(router_link, b, ins)

            def clink(b, ins):
                link(chain_link, b, ins)

            def stats(order, b, srcs, st, mv):
                for t, src in enumerate(srcs):
                    ins = dve.bn_stats(st[0:src.shape[0], t, :], src)
                order(b, ins)
                dve.nop(nofuse=True)
                for t, src in enumerate(srcs):
                    ins = dve.bn_aggr(mv[0:src.shape[0], t, :], st[0:src.shape[0], t, :])
                order(b, ins)

            def normalise(dst, src, mv, rstd):
                for t in range(TT):
                    ins = ts(dst[:, t, :], src[:, t, :], mv[:, t, 0:1], rstd[:, t:t + 1], ALU.subtract, ALU.mult)
                return ins

            def tiles(a):
                return [a[:, t, :] for t in range(TT)]

            def maxes(b, u):
                dve.wait_ge(score_done.sem, score_done.at(b, u + 1))
                red(nmax[:, u % 2:u % 2 + 1], ps[:, BANK_S[u % 2], 0:KEYS], AX.X, ALU.max, negate=True)\
                    .then_inc(max_ready.sem, 1)

            def k_out(b, p):
                dve.wait_ge(k_done.sem, k_done.at(b, p + 1))
                cp(kT[:, p % 2, :], ps[:, BANK_PJ, 0:KEYS]).then_inc(k_ready.sem, 1)

            def norm(b, u):
                p, t, h = u // 4, u // 2 % 2, u % 2
                dve.wait_ge(pv_done.sem, pv_done.at(b, u + 1))
                if u % 4 == 0 and p >= 2:
                    dve.wait_ge(aN_ready.sem, aN_ready.at(b, p - 1))
                elif u % 4 == 0 and not first(b):
                    dve.wait_ge(aN_ready.sem, aN_ready.at(b - 1, PAIRS - 1 + p))
                cp(aU[:, p % 2, t, h, :], ps[:, BANK_PV, 0:DH0 + 1]).then_inc(norm_ready.sem, 1)

            def inverse_sums(b, p):
                dve.wait_ge(norm_ready.sem, norm_ready.at(b, 4 * p + 4))
                dve.reciprocal(rinv[:, p % 2, :, :], aU[:, p % 2, :, :, DH0]).then_inc(rinv_ready.sem, 1)

            def input_stats(b):
                links[norm_link] = 0
                dve.wait_ge(x_in.sem, x_in.at(b, 16))
                dve.wait_ge(c_in.sem, c_in.at(b, 16))
                stats(nlink, b, tiles(xin) + [cin[:, :]], st, mv)
                ts(var[:, 2:3], mv[:, 2, 1:2], EPS, None, ALU.add)
                ts(var[:, 0:2], mv[:, 0:2, 1], 1.0 + EPS, EPS * EPS, ALU.mult, ALU.add).then_inc(xvar_ready.sem, 1)

            def input_norm(b):
                dve.wait_ge(xrstd_ready.sem, xrstd_ready.at(b, 1))
                normalise(xf, xin, mv, rstd)
                ts(cn[:, :], cin[:, :], mv[0:C, 2, 0:1], rstd[0:C, 2:3], ALU.subtract, ALU.mult).then_inc(xf_ready.sem, 1)

            def context_out(b):
                dve.wait_ge(cT_done.sem, cT_done.at(b, 1))
                for c in range(DC):
                    ts(kvTn[:, c, S:KEYS], ps[:, BANK_PJ, c * C:(c + 1) * C], g1[:, c:c + 1], bb1[:, c:c + 1], ALU.mult, ALU.add)
                cp(flat(cTn[:, :, :]), ps[:, BANK_PJ, 2 * C:4 * C]).then_inc(kvc_ready.sem, 1)

            def router(b, s):
                if s == 2:
                    dve.wait_ge(x1_ready.sem, x1_ready.at(b, TT))
                    stats(rlink, b, tiles(x1), sty, mvy)
                    ts(vary[:, :], mvy[:, :, 1], EPS, None, ALU.add).then_inc(yvar_ready.sem, 1)
                if s == 3:
                    dve.wait_ge(yrstd_ready.sem, yrstd_ready.at(b, 1))
                    normalise(y1, x1, mvy, rstdy).then_inc(y1_ready.sem, 1)
                if s == LOGITS_AT:
                    dve.wait_ge(lgr_ready.sem, lgr_ready.at(b, 1))
                    rlink(b, stt(lg[:, :], lgr[:, :], 1.0 / S, brow[:, :], ALU.mult, ALU.add))
                    red(nlg[:, :], lg[:, :], AX.X, ALU.max, negate=True).then_inc(logit_ready.sem, 1)
                if s == LOGITS_AT + 1:
                    dve.wait_ge(rexp_ready.sem, rexp_ready.at(b, 1))
                    rlink(b, dve.reciprocal(rex[:, :], exs[:, :]))
                    rlink(b, ts(rw[:, :], ex[:, :], rex[:, 0:1], None, ALU.mult))
                    dve.nop(nofuse=True)
                    rlink(b, dve.max(top[:, :], rw[:, :]))
                    dve.nop(nofuse=True)
                    dve.max_index(idx[:, :], top[:, :], rw[:, :]).then_inc(idx_ready.sem, 1)
                    tt(gap[:, :], top[:, 1:2], top[:, 0:1], ALU.subtract).then_inc(gap_ready.sem, 1)
                if s == LOGITS_AT + 2:
                    dve.wait_ge(egap_ready.sem, egap_ready.at(b, 1))
                    rlink(b, ts(wden[:, :], egap[:, :], 1.0, None, ALU.add))
                    rlink(b, dve.reciprocal(wtop[:, 0:1], wden[:, :]))
                    tt(wtop[:, 1:2], egap[:, :], wtop[:, 0:1], ALU.mult).then_inc(wtop_ready.sem, 1)
                if s == LOGITS_AT + 3:
                    dve.wait_ge(wtop_ready.sem, wtop_ready.at(b, 1))
                    for k in range(TOPK):
                        ts(wrow[:, k, :], ones[0:1, :], wtop[:, k:k + 1], None, ALU.mult)

            def slot(b, s, front, chain, tail, ahead, part):
                if s == 0:
                    links[router_link] = 0
                u = s
                if u < UNITS:
                    if front and 0 < u < UNITS - 1:
                        maxes(b, u + 1)
                    if front and u in LONG_PARTS_AT:
                        norm(b, u - 1)
                    part()
                    if front and u and u not in LONG_PARTS_AT:
                        norm(b, u - 1)
                    if front and u > 4 and u % 4 == 1:
                        inverse_sums(b, u // 4 - 1)
                    if front and u % 4 == 1 and u // 4 + 1 < PAIRS:
                        k_out(b, u // 4 + 1)
                    if chain:
                        router(b - 1, s)
                    if ahead and s == NEXT_STATS_AT:
                        input_stats(b + 1)
                    if ahead and s == NEXT_NORM_AT:
                        input_norm(b + 1)
                    if ahead and s == NEXT_CT_AT:
                        context_out(b + 1)
                    if ahead and s == NEXT_K_AT:
                        k_out(b + 1, 0)
                    return
                if front and s == UNITS:
                    norm(b, UNITS - 1)
                    inverse_sums(b, PAIRS - 1)
                if ahead and s < UNITS + 2:
                    maxes(b + 1, s - UNITS)
                if front and s == UNITS + 2:
                    for t in range(TT):
                        dve.wait_ge(wo_done.sem, wo_done.at(b, t + 1))
                        tt(x1[:, t, :], ps[:, 2 + t, 0:D], xres[:, t, :], ALU.add).then_inc(x1_ready.sem, 1)
                if front and s == UNITS + 3:
                    dve.wait_ge(kv1_done.sem, kv1_done.at(b, 1))
                    for g in range(HT):
                        ts(k1[:, g, :], ps[:, BANK_PJ, g * C:(g + 1) * C], bkp[:, g:g + 1], None, ALU.add)
                    tt(v1[:, :, 0:DH1], ps[0:C, BANK_PJ, S:S + D].rearrange("p (h d) -> p h d", h=H1),
                       bvB[0:C, :].rearrange("p (h d) -> p h d", h=H1), ALU.add).then_inc(k1v1_ready.sem, 1)
                part()

            def chain_part(b, c):
                if c == 0:
                    links[chain_link] = 0
                if c == 0:
                    dve.wait_ge(wB_done.sem, wB_done.at(b, 1))
                    cp(wB[:, :], ps[:, 6, 0:2]).then_inc(wB_ready.sem, 1)
                if c == TAIL:
                    links[chain_link] = TURN_LINKS
                if c == 11:
                    if not first(b):
                        dve.wait_ge(out_done.sem, out_done.at(b, 0))
                    dve.wait_ge(b2_done.sem, b2_done.at(b, 1))
                    for t in range(TT):
                        ins = tt(y2[:, t, :], ps[:, 6, 0:D], y1[:, t, :], ALU.add)
                    clink(b, ins)
                if c in (12, 13):
                    k = c - 12
                    dve.wait_ge(moe_done.sem, moe_done.at(b, k + 1))
                    dve.wait_ge(wB_ready.sem, wB_ready.at(b, 1))
                    for t in range(TT):
                        ins = stt(y2[:, t, :], ps[:, (7, 5)[k], t * D:(t + 1) * D], wB[:, k:k + 1], y2[:, t, :], ALU.mult, ALU.add)
                    clink(b, ins)
                if c == 13:
                    stats(clink, b, tiles(y2), st2, mv2)
                    ts(var2[:, :], mv2[:, :, 1], EPS, None, ALU.add).then_inc(var2_ready.sem, 1)
                if c == 14:
                    dve.wait_ge(rstd2_ready.sem, rstd2_ready.at(b, 1))
                    for t in range(TT):
                        ins = stt(y2[:, t, :], y2[:, t, :], mv2[:, t, 0:1], gammaB[:, :], ALU.subtract, ALU.mult)
                    clink(b, ins)
                    dve.wait_ge(x1b_ready.sem, x1b_ready.at(b, 1))
                    for t in range(TT):
                        ins = stt(x2[:, t, :], y2[:, t, :], rstd2[:, t:t + 1], x1[:, t, :], ALU.mult, ALU.add)
                    clink(b, ins)
                if c == 15:
                    stats(clink, b, tiles(x2), st2, mv2)
                    ts(var2[:, :], mv2[:, :, 1], EPS, None, ALU.add).then_inc(var2_ready.sem, 1)
                if c == 16:
                    dve.wait_ge(rstd2_ready.sem, rstd2_ready.at(b, 2))
                    normalise(xn, x2, mv2, rstd2).then_inc(xn_ready.sem, 1)
                for t in range(TT):
                    if c in (19 + 5 * t, 20 + 5 * t):
                        g = c - 19 - 5 * t
                        dve.wait_ge(s1_done.sem, s1_done.at(b, HT * t + g + 1))
                        for m in range(2):
                            v = ps[:, ((5, 6), (7, 5))[g][m], 0:4 * C].rearrange("p (h c) -> p h c", h=4)
                            ins = red(nmax1[:, 4 * m:4 * m + 4], v, AX.X, ALU.max, negate=True)
                        clink(b, ins)
                        for m in range(2):
                            v = ps[:, ((5, 6), (7, 5))[g][m], 0:4 * C].rearrange("p (h c) -> p h c", h=4)
                            h = HH * g + 4 * m
                            ins = tt(P1[:, h:h + 4, :], v, nmax1[:, 4 * m:4 * m + 4].unsqueeze(2).to_broadcast([P, 4, C]), ALU.add)
                        ins.then_inc(s1_shift.sem, 1)
                    if c in (21 + 5 * t, 22 + 5 * t):
                        m = 2 * (c - 21 - 5 * t) + 1
                        dve.wait_ge(t1_done.sem, t1_done.at(b, 4 * t + m + 1))
                        cp(PT1[:, 4 * m:4 * m + 4, :].rearrange("p h q -> p (h q)"), ps[0:C, (6, 7, 5, 6)[m], :])\
                            .then_inc(t1_dve.sem, 1)
                    if c == 23 + 5 * t:
                        dve.wait_ge(pv1_done.sem, pv1_done.at(b, t + 1))
                        o = ps[:, 7, 0:H1 * (DH1 + 1)].rearrange("p (h d) -> p h d", h=H1)
                        clink(b, dve.reciprocal(rinv1[:, :], o[:, :, DH1]))
                        tt(a1[:, t, :].rearrange("p (h d) -> p h d", h=H1), o[:, :, 0:DH1],
                           rinv1[:, :].unsqueeze(2).to_broadcast([P, H1, DH1]), ALU.mult).then_inc(a1_ready.sem, 1)
                if c == 30:
                    dve.wait_ge(wo1_done.sem, wo1_done.at(b, 1))
                    dve.wait_ge(x2b_ready.sem, x2b_ready.at(b, 1))
                    clink(b, tt(x3[:, :, :], ps[:, 6, :].rearrange("p (t d) -> p t d", t=TT), x2[:, :, :], ALU.add))
                    stats(clink, b, tiles(x3), st2, mv2)
                    ts(var2[:, :], mv2[:, :, 1], EPS, None, ALU.add).then_inc(var2_ready.sem, 1)
                if c == 31:
                    dve.wait_ge(rstd2_ready.sem, rstd2_ready.at(b, 3))
                    clink(b, normalise(xn, x3, mv2, rstd2))
                    clink(b, red(am[:, :], xn[:, :, :], AX.X, ALU.max, apply_absolute_value=True))
                    clink(b, ts(am[:, :], am[:, :], 1e-5, 1.0 / 127.0, ALU.max, ALU.mult))
                    clink(b, dve.reciprocal(sc[:, :], am[:, :]))
                    for t in range(TT):
                        ins = ts(y2[:, t, :], xn[:, t, :], sc[:, t:t + 1], MAGIC, ALU.mult, ALU.add)
                    clink(b, ins)
                    ts(qx[:, :, :], y2[:, :, :], MAGIC, 127.0, ALU.subtract, ALU.min).then_inc(qx_ready.sem, 1)
                if c == 32:
                    for t in range(TT):
                        ins = ts(dg[:, t, :], ident[:, :], am[:, t:t + 1], mw[:, 0:1], ALU.mult, ALU.mult)
                    ins.then_inc(dg_ready.sem, 1)
                if 34 <= c <= 37:
                    n = c - 34
                    dve.wait_ge(sB_ready.sem, sB_ready.at(b, 1))
                    dve.wait_ge(f1_done.sem, f1_done.at(b, n + 1))
                    tt(hb[:, 2 * n:2 * n + 2, 1:S + 1], ps[:, (6, 5, 7, 6)[n], :].rearrange("p (a q) -> p a q", a=2),
                       sB[:, :].unsqueeze(1).to_broadcast([P, 2, S]), ALU.mult).then_inc(hb_ready.sem, 1)
                if 36 <= c <= 38:
                    n = c - 35
                    dve.wait_ge(tap_ready.sem, tap_ready.at(b, n + 1))
                    for j in (2 * n, 2 * n + 1):
                        ins = stt(cv[:, j, :], hb[:, j, 0:S], cw[:, j, 0:1], cv[:, j, :], ALU.mult, ALU.add)
                    clink(b, ins)
                    for j in (2 * n, 2 * n + 1):
                        ins = stt(cv[:, j, :], hb[:, j, 2:S + 2], cw[:, j, 2:3], cv[:, j, :], ALU.mult, ALU.add)
                    ins.then_inc(conv_dve.sem, 1)
                if c == 40:
                    dve.wait_ge(silu_ready.sem, silu_ready.at(b, 4))
                    red(mj[:, :], cv[:, :, :].rearrange("p j q -> p q j"), AX.X, ALU.max, apply_absolute_value=True)\
                        .then_inc(mj_ready.sem, 1)
                if c == 41:
                    dve.wait_ge(mjT_done.sem, mjT_done.at(b, 1))
                    clink(b, red(am2[:, :], ps[:, 5, 0:S].rearrange("p (t q) -> p t q", t=TT), AX.X, ALU.max))
                    clink(b, ts(am2[:, :], am2[:, :], 1e-5, 1.0 / 127.0, ALU.max, ALU.mult))
                    clink(b, dve.reciprocal(sc[:, :], am2[:, :]))
                    for t in range(TT):
                        ins = ts(dg[:, t, :], ident[:, :], sc[:, t:t + 1], None, ALU.mult)
                    ins.then_inc(dg_ready.sem, 1)
                    ts(inv2[:, :], am2[:, :], mw[:, 1:2], None, ALU.mult)
                if c in (43, 44):
                    dve.wait_ge(sB_ready.sem, sB_ready.at(b, 2))
                    for n in (2 * (c - 43), 2 * (c - 43) + 1):
                        v = cv[:, 2 * n:2 * n + 2, :]
                        clink(b, tt(v, v, sB[:, :].unsqueeze(1).to_broadcast([P, 2, S]), ALU.mult))
                        ts(q2[:, 2 * n:2 * n + 2, :], v, MAGIC, MAGIC, ALU.add, ALU.subtract).then_inc(q2_ready.sem, 1)
                if c == 45:
                    for t in range(TT):
                        dve.wait_ge(f2_done.sem, f2_done.at(b, t + 1))
                        ins = stt(x4[:, t, :], ps[:, 5 + t, 0:D], inv2[:, t:t + 1], x3[:, t, :], ALU.mult, ALU.add)
                    ins.then_inc(x4_ready.sem, 1)

            def turn(b, front, chain, tail, ahead):
                walk(b, front, chain, tail, ahead, slot, chain_part, setup)
                assert not front or links[norm_link] == NORM_LINKS, links.values()
                assert not chain or (links[router_link], links[chain_link]) == (ROUTER_LINKS, TURN_LINKS), links.values()
                assert chain or not tail or links[chain_link] == CHAIN_LINKS, links.values()

            dve.wait_ge(consts_made, CONSTS)
            input_stats(0)
            input_norm(0)
            dve.wait_ge(ld["vec"], 64)
            context_out(0)
            k_out(0, 0)
            maxes(0, 0)
            maxes(0, 1)
            turns(dve, turn)


CONSTS = 10
SETUP_SUMS = 4 * DC + 2
SETUP_TERNARY = SETUP_SUMS + 8
SETUP_DVE_END = SETUP_TERNARY + 5


_INS = ['x', 'ctx_1024', 'L0_xattn_ln1_g', 'L0_xattn_ln1_b', 'L0_xattn_ln2_g', 'L0_xattn_ln2_b', 'L0_xattn_Wq',
        'L0_xattn_Wkv', 'L0_xattn_Wo', 'L0_ffn_W1', 'L0_ffn_b1', 'L0_ffn_W2', 'L0_ffn_b2', 'L0_ffn_Wr', 'L0_ffn_br',
        'L0_ffn_gamma', 'L0_ffn_beta', 'L1_xattn_wq', 'L1_xattn_bq', 'L1_xattn_wk', 'L1_xattn_bk', 'L1_xattn_wv',
        'L1_xattn_bv', 'L1_xattn_wo', 'L1_xattn_bo', 'L1_ffn_w1', 'L1_ffn_conv_w', 'L1_ffn_conv_b', 'L1_ffn_w2']
_OUTS = [((B, S, D), 'float32')]


def kernel(**inputs):
    import numpy as _np
    import concourse.bacc as _bacc
    from concourse import mybir as _mybir
    from concourse.bass_utils import run_bass_kernel_spmd as _run

    nc = _bacc.Bacc("TRN2", target_bir_lowering=False, num_devices=1)
    arrays, args = {}, []
    for name in _INS:
        a = _np.ascontiguousarray(inputs[name])
        arrays[f"in_{name}_dram"] = a
        args.append(nc.dram_tensor(f"in_{name}_dram", a.shape, _mybir.dt.from_np(a.dtype), kind="ExternalInput").ap())
    for i, (shape, dtype) in enumerate(_OUTS):
        dt = _mybir.dt.from_np(_np.dtype(dtype))
        args.append(nc.dram_tensor(f"out_{i}_dram", shape, dt, kind="ExternalOutput").ap())
    build(nc, *args)
    r = _run(nc, [arrays], core_ids=[0])
    return r.results[0]["out_0_dram"]
```
